# Optimizing a Trainium2 kernel written in Bass

```python
import numpy as np
import jax
import jax.numpy as jnp

def _softmax(x, axis=-1):
    return jax.nn.softmax(x, axis=axis)

def _gelu(x):
    return jax.nn.gelu(x, approximate=True)

def _silu(x):
    return jax.nn.silu(x)

def _sigmoid(x):
    return jax.nn.sigmoid(x)

def _layernorm(x, axis=-1, eps=1e-05):
    m = jnp.mean(x, axis=axis, keepdims=True)
    v = jnp.var(x, axis=axis, keepdims=True)
    return (x - m) / jnp.sqrt(v + eps)

def _scatter_add(tgt, idx, src, axis=0):
    return tgt.at[idx].add(src)

def _segment_sum(src, seg, n):
    return jax.ops.segment_sum(src, seg, n)
kernel_name = 'mk_gnn_preln_d2_gnn_r64_388e84'

def setup_inputs(seed: int=0):
    np.random.seed(seed)
    _w = jnp.asarray

    def _rec_inputs():
        import jax
        import jax.numpy as jnp
        _gk = jax.random.key(seed)
        x = -8.776e-05 + 1 * jax.random.normal(jax.random.fold_in(_gk, 1), (50000, 256), jnp.float32)
        src = jax.random.randint(jax.random.fold_in(_gk, 2), (12500,), 0, 50000, jnp.int32)
        dst = jnp.minimum((50000 * jax.random.uniform(jax.random.fold_in(_gk, 3), (12500,)) ** 2.0).astype(jnp.int32), 49999)
        _o = jnp.argsort(dst, stable=True)
        src = src[_o]
        dst = dst[_o]
        edge_attr_64 = 0.000151818 + 1.00006 * jax.random.normal(jax.random.fold_in(_gk, 11), (12500, 64), jnp.float32)
        edge_weight = jax.random.uniform(jax.random.fold_in(_gk, 13), (12500,), jnp.float32, 0.0, 4.99999)
        return (x, src, dst, edge_attr_64, edge_weight)
    x, src, dst, edge_attr_64, edge_weight = _rec_inputs()

    def _L0_gnn_setup():
        import jax, jax.numpy as jnp
        import numpy as np
        H = 256
        R = 64
        N = 20000
        E = 5000
        CUTOFF_LO = 0.0
        CUTOFF_UP = 5.0
        LN_EPS = 1e-05

        def _layernorm(x, g, b):
            mu = jnp.mean(x, axis=-1, keepdims=True)
            var = jnp.var(x, axis=-1, keepdims=True)
            return (x - mu) * jax.lax.rsqrt(var + LN_EPS) * g + b

        def _cosine_cutoff(r):
            c = 0.5 * (jnp.cos(r * (jnp.pi / CUTOFF_UP)) + 1.0)
            return c * (r < CUTOFF_UP).astype(r.dtype)
        key = jax.random.key(seed)
        ks = jax.random.split(key, 16)

        def xavier(k, shape):
            fan_in, fan_out = (shape[1], shape[0])
            lim = np.sqrt(6.0 / (fan_in + fan_out))
            return jax.random.uniform(k, shape, jnp.float32, -lim, lim)
        x = jax.random.normal(ks[0], (N, H), jnp.float32)
        edge_index = jax.random.randint(ks[1], (2, E), 0, N, jnp.int64)
        edge_weight = jax.random.uniform(ks[2], (E,), jnp.float32, 0.0, CUTOFF_UP)
        edge_attr = jax.random.normal(ks[3], (E, R), jnp.float32)
        return {'x': x, 'edge_index': edge_index, 'edge_weight': edge_weight, 'edge_attr': edge_attr, 'ln_g': jnp.ones((H,), jnp.float32), 'ln_b': jnp.zeros((H,), jnp.float32), 'Wq': xavier(ks[4], (H, H)), 'bq': jnp.zeros((H,), jnp.float32), 'Wk': xavier(ks[5], (H, H)), 'bk': jnp.zeros((H,), jnp.float32), 'Wv': xavier(ks[6], (H, H)), 'bv': jnp.zeros((H,), jnp.float32), 'Wo': xavier(ks[7], (H, H)), 'bo': jnp.zeros((H,), jnp.float32), 'Wdk': xavier(ks[8], (H, R)), 'bdk': jnp.zeros((H,), jnp.float32), 'Wdv': xavier(ks[9], (H, R)), 'bdv': jnp.zeros((H,), jnp.float32)}
    _L0_gnn_all = _L0_gnn_setup()
    _L0_gnn_in = {k: v for k, v in _L0_gnn_all.items() if k in ('ln_g', 'ln_b', 'Wq', 'bq', 'Wk', 'bk', 'Wv', 'bv', 'Wo', 'bo', 'Wdk', 'bdk', 'Wdv', 'bdv')}
    del _L0_gnn_all

    def _L1_gnn_setup():
        import jax, jax.numpy as jnp
        import numpy as np
        N_NODES = 100000
        N_EDGES = 25000
        D = 256
        key = jax.random.key(seed)
        ks = jax.random.split(key, 8)
        h6_all = jax.random.normal(ks[0], (N_NODES, D), dtype=jnp.float32)
        edge_index = jax.random.randint(ks[1], (2, N_EDGES), 0, N_NODES, dtype=jnp.int64)
        edge_weight = jax.random.uniform(ks[2], (N_EDGES,), dtype=jnp.float32)
        s = 1.0 / np.sqrt(D)
        W = jax.random.normal(ks[3], (D, D), dtype=jnp.float32) * s
        b = jnp.zeros((D,), dtype=jnp.float32)
        W1 = jax.random.normal(ks[4], (D, D), dtype=jnp.float32) * s
        b1 = jnp.zeros((D,), dtype=jnp.float32)
        W2 = jax.random.normal(ks[5], (D, D), dtype=jnp.float32) * s
        b2 = jnp.zeros((D,), dtype=jnp.float32)
        return {'h6_all': h6_all, 'edge_index': edge_index, 'edge_weight': edge_weight, 'W': W, 'b': b, 'W1': W1, 'b1': b1, 'W2': W2, 'b2': b2}
    _L1_gnn_all = _L1_gnn_setup()
    _L1_gnn_in = {k: v for k, v in _L1_gnn_all.items() if k in ('W', 'b', 'W1', 'b1', 'W2', 'b2')}
    del _L1_gnn_all
    return {'x': x, 'src': src, 'dst': dst, 'edge_attr_64': edge_attr_64, 'edge_weight': edge_weight, 'L0_gnn_ln_g': _L0_gnn_in['ln_g'], 'L0_gnn_ln_b': _L0_gnn_in['ln_b'], 'L0_gnn_Wq': _L0_gnn_in['Wq'], 'L0_gnn_bq': _L0_gnn_in['bq'], 'L0_gnn_Wk': _L0_gnn_in['Wk'], 'L0_gnn_bk': _L0_gnn_in['bk'], 'L0_gnn_Wv': _L0_gnn_in['Wv'], 'L0_gnn_bv': _L0_gnn_in['bv'], 'L0_gnn_Wo': _L0_gnn_in['Wo'], 'L0_gnn_bo': _L0_gnn_in['bo'], 'L0_gnn_Wdk': _L0_gnn_in['Wdk'], 'L0_gnn_bdk': _L0_gnn_in['bdk'], 'L0_gnn_Wdv': _L0_gnn_in['Wdv'], 'L0_gnn_bdv': _L0_gnn_in['bdv'], 'L1_gnn_W': _L1_gnn_in['W'], 'L1_gnn_b': _L1_gnn_in['b'], 'L1_gnn_W1': _L1_gnn_in['W1'], 'L1_gnn_b1': _L1_gnn_in['b1'], 'L1_gnn_W2': _L1_gnn_in['W2'], 'L1_gnn_b2': _L1_gnn_in['b2']}

def reference(x, src, dst, edge_attr_64, edge_weight, L0_gnn_ln_g, L0_gnn_ln_b, L0_gnn_Wq, L0_gnn_bq, L0_gnn_Wk, L0_gnn_bk, L0_gnn_Wv, L0_gnn_bv, L0_gnn_Wo, L0_gnn_bo, L0_gnn_Wdk, L0_gnn_bdk, L0_gnn_Wdv, L0_gnn_bdv, L1_gnn_W, L1_gnn_b, L1_gnn_W1, L1_gnn_b1, L1_gnn_W2, L1_gnn_b2):
    import jax
    import jax.numpy as jnp

    def _L0_gnn_ref(x, edge_index, edge_weight, edge_attr, ln_g, ln_b, Wq, bq, Wk, bk, Wv, bv, Wo, bo, Wdk, bdk, Wdv, bdv):
        import jax, jax.numpy as jnp
        import numpy as np
        H = 256
        R = 64
        N = 20000
        E = 5000
        CUTOFF_LO = 0.0
        CUTOFF_UP = 5.0
        LN_EPS = 1e-05

        def _layernorm(x, g, b):
            mu = jnp.mean(x, axis=-1, keepdims=True)
            var = jnp.var(x, axis=-1, keepdims=True)
            return (x - mu) * jax.lax.rsqrt(var + LN_EPS) * g + b

        def _cosine_cutoff(r):
            c = 0.5 * (jnp.cos(r * (jnp.pi / CUTOFF_UP)) + 1.0)
            return c * (r < CUTOFF_UP).astype(r.dtype)
        src = edge_index[0]
        dst = edge_index[1]
        x_norm = _layernorm(x, ln_g, ln_b)
        q = x_norm @ Wq.T + bq
        k = x_norm @ Wk.T + bk
        v = x_norm @ Wv.T + bv
        dk = jax.nn.silu(edge_attr @ Wdk.T + bdk)
        dv = jax.nn.silu(edge_attr @ Wdv.T + bdv)
        q_i = q[dst]
        k_j = k[src]
        v_j = v[src]
        attn = jnp.sum(q_i * k_j * dk, axis=1)
        attn = jax.nn.silu(attn) * _cosine_cutoff(edge_weight)
        msg = v_j * dv * attn[:, None]
        agg = jax.ops.segment_sum(msg, dst, num_segments=x.shape[0])
        out = agg @ Wo.T + bo
        return x + out

    def _L1_gnn_ref(h6_all, edge_index, edge_weight, W, b, W1, b1, W2, b2):
        import jax, jax.numpy as jnp
        import numpy as np
        N_NODES = 100000
        N_EDGES = 25000
        D = 256
        'GCNConv(256->256, weighted, self-loops, symmetric norm) + 2-layer MLP head.'
        N = h6_all.shape[0]
        row, col = (edge_index[0], edge_index[1])
        sl = jnp.arange(N, dtype=edge_index.dtype)
        row_sl = jnp.concatenate([row, sl])
        col_sl = jnp.concatenate([col, sl])
        ew_sl = jnp.concatenate([edge_weight, jnp.ones((N,), dtype=edge_weight.dtype)])
        deg = jax.ops.segment_sum(ew_sl, row_sl, num_segments=N)
        dinv = jnp.where(deg > 0, jax.lax.rsqrt(deg), 0.0)
        norm = dinv[row_sl] * ew_sl * dinv[col_sl]
        xw = h6_all @ W
        msgs = xw[col_sl] * norm[:, None]
        h7 = jax.ops.segment_sum(msgs, row_sl, num_segments=N) + b
        h = jax.nn.relu(h7 @ W1 + b1)
        out = h @ W2 + b2
        return out
    edge_index = jnp.stack([src, dst])
    h = jnp.maximum(_layernorm(x, axis=-1), 0.0)
    x = x + _L0_gnn_ref(h, edge_index, edge_weight, edge_attr_64, L0_gnn_ln_g, L0_gnn_ln_b, L0_gnn_Wq, L0_gnn_bq, L0_gnn_Wk, L0_gnn_bk, L0_gnn_Wv, L0_gnn_bv, L0_gnn_Wo, L0_gnn_bo, L0_gnn_Wdk, L0_gnn_bdk, L0_gnn_Wdv, L0_gnn_bdv)
    h = jnp.maximum(_layernorm(x, axis=-1), 0.0)
    x = x + _L1_gnn_ref(h, edge_index, edge_weight, L1_gnn_W, L1_gnn_b, L1_gnn_W1, L1_gnn_b1, L1_gnn_W2, L1_gnn_b2)
    return x

_drawn_inputs = setup_inputs


def setup_inputs(seed=0):
    import zlib

    import numpy as np

    out = dict(_drawn_inputs(seed))
    spreads = {'L0_gnn_ln_g': (1.0, 0.2),
     'L0_gnn_ln_b': (0.0, 0.1),
     'L0_gnn_bq': (0.0, 0.291),
     'L0_gnn_bk': (0.0, 0.284),
     'L0_gnn_bv': (0.0, 0.282),
     'L0_gnn_bo': (0.0, 0.1),
     'L0_gnn_bdk': (0.0, 0.1),
     'L0_gnn_bdv': (0.0, 0.1),
     'L1_gnn_b': (0.0, 0.1),
     'L1_gnn_b1': (0.0, 0.1),
     'L1_gnn_b2': (0.0, 0.1)}
    factors = {}
    for name, (base, spread) in spreads.items():
        noise = np.random.default_rng([zlib.crc32(name.encode()), seed]).standard_normal(out[name].shape)
        drawn = base * np.exp(spread * noise) if base else spread * noise
        out[name] = jnp.asarray(drawn.astype(out[name].dtype))
    for name, factor in factors.items():
        out[name] = (out[name] * factor).astype(out[name].dtype)
    return out
```

```python
from contextlib import ExitStack

import concourse.bass as bass
from concourse import mybir

P = 128
D = 256
R = 64
N = 50000
E = 12500
KC = D // P
EC = -(-E // P)
ET = E - (EC - 1) * P
G = 4
GN = G * P
NG = -(-N // GN)
GT = (N - (NG - 1) * GN) // G
COLS = NG * G
SLOTS = -(-2 * E // P) * P
SPARE = 8
IDLE0 = SLOTS
DUMP0 = IDLE0 + SPARE * P
FILL = 4
ROWS = -(-(DUMP0 + P) // (FILL * P)) * FILL * P
CUTOFF = 5.0
EPS = 1e-5
PI = 3.14159265358979

F32 = mybir.dt.float32
BF16 = mybir.dt.bfloat16
F16 = mybir.dt.float16
I32 = mybir.dt.int32
ALU = mybir.AluOpType
ACT = mybir.ActivationFunctionType


class Step:

    def __init__(self, off, reg=None, unroll=1):
        self.off, self.reg, self.unroll = off, reg, unroll

    def back(self, n):
        return Step(self.off - n, self.reg, self.unroll)

    def within(self, count):
        return self.reg is not None or 0 <= self.off < count

    def past(self, n):
        return self.reg is not None or self.off >= n

    def value(self, add=0, times=1):
        if self.reg is None:
            return (self.off + add) * times
        return self.reg * (self.unroll * times) + (self.off + add) * times

    def slot(self, ring):
        return self.off % ring

    def turns(self, ring, times=16, add=1):
        if self.reg is None:
            return times * (self.off // ring + add)
        return self.reg * (times * (self.unroll // ring)) + times * (self.off // ring + add)


def run_steps(eng, count, depth, unroll, warm, body):
    first = -(-(depth + warm) // unroll)
    last = (count - 1) // unroll
    for s in range(first * unroll):
        body(Step(s))
    with eng.Fori(first, last) as reg:
        for u in range(unroll):
            body(Step(u, reg, unroll))
    for s in range(last * unroll, count + depth):
        body(Step(s))


def build(nc, x, src, dst, edge_attr, edge_weight, ln_g, ln_b, Wq, bq, Wk, bk, Wv, bv, Wo, bo,
          Wdk, bdk, Wdv, bdv, W, b, W1, b1, W2, b2, out):
    ctx = ExitStack()
    with ctx:
        def sb(name, shape, dt=F32):
            return ctx.enter_context(nc.sbuf_tensor(name, shape, dt))

        def ring(name, n, shape, dt=F32):
            return [sb(f"{name}{i}", shape, dt) for i in range(n)]

        def sem(name):
            return ctx.enter_context(nc.semaphore(name))

        def sems(name, n):
            return [sem(f"{name}_{i}") for i in range(n)]

        sums = nc.dram_tensor("sums_dram", (ROWS, 2 * D), F32).ap()
        halves = sums.rearrange("r (h d) -> (r h) d", h=2)
        table = nc.dram_tensor("table_dram", (P * COLS, 2), F32).ap()

        bank = ctx.enter_context(nc.psum_tensor("bank", [P, 8, 512], F32))

        identity = sb("identity", [P, P])
        lower = sb("lower", [P, P])
        upper = sb("upper", [P, P])
        ones = sb("ones", [P, P])
        ones3 = sb("ones3", [3, P], BF16)
        pick3 = sb("pick3", [3, 3])
        minus_half = sb("minus_half", [P, G])
        eps_tile = sb("eps_tile", [P, G])
        half_pi = sb("half_pi", [P, 1])

        kept = sb("kept", [P, EC, D])
        room = kept[:, :, :].rearrange("p c d -> p (c d)")
        early, late = [0], [0]

        def place(taken, shape, dt=F32):
            width = 1
            for n in shape[1:]:
                width *= n
            words = width // 2 if dt in (BF16, F16) else width
            at0 = taken[0]
            taken[0] += words
            assert taken[0] <= EC * D
            view = room[0:shape[0], at0:at0 + words]
            if dt != F32:
                view = view.bitcast(dt)
            names = "abc"[:len(shape) - 1]
            if len(names) > 1:
                view = view.rearrange(f"p ({' '.join(names)}) -> p {' '.join(names)}",
                                      **dict(zip(names, shape[1:])))
            return view

        def temp(shape, dt=F32):
            return place(early, shape, dt)

        w_raw = temp([P, 5, KC, D])
        wd_raw = temp([P, 2, KC, R])
        wq_t = temp([P, 3, KC, D])
        qkv_w = sb("qkv_w", [P, KC, 3 * D])
        wo_t = sb("wo_t", [P, KC, D])
        w_t = temp([P, KC, D])
        wd_t = sb("wd_t", [R + 1, 2 * D])
        w1_raw = temp([P, KC, D])
        w01 = sb("w01", [P, KC, D])
        w2_sb = sb("w2_sb", [P, KC, D])
        g_col = sb("g_col", [P, KC])
        b_col = sb("b_col", [P, KC])
        b0_col = sb("b0_col", [P, KC])
        b1_col = sb("b1_col", [P, KC])
        b01_col = sb("b01_col", [P, KC])
        rows3 = temp([3, 4 * D])
        part3 = temp([3, 4 * D])
        piece = [temp([3, 4 * D], BF16) for _ in range(3)]
        rest3 = temp([3, 4 * D])
        bias3 = sb("bias3", [3, 4 * D], BF16)

        e_rows = temp([EC, 3, P])
        e_rowf = temp([EC, 2, P])
        src_f = sb("src_f", [P, EC])
        dst_f = sb("dst_f", [P, EC])
        ew_f = sb("ew_f", [P, EC])
        node_i = sb("node_i", [P, EC, 2], I32)
        key_i = temp([P, EC, 2], I32)
        key_j = temp([P, EC, 2], I32)
        pkey = temp([P, EC, 2])
        ckey = temp([P, EC, 2])
        at_i = sb("at_i", [P, EC, 2], I32)
        valid = sb("valid", [P, EC])
        edge_no = temp([P, EC], I32)
        away = temp([P, EC])
        cut = sb("cut", [P, EC])
        ew_part = [temp([P, EC]) for _ in range(3)]
        ew_low = [temp([P, EC], BF16) for _ in range(3)]
        ends_d = sb("ends_d", [P, EC, 2])
        dump_f = sb("dump_f", [P, 1])
        dump2_f = sb("dump2_f", [P, 1])
        dump_i = sb("dump_i", [P, 1], I32)

        iota_c = temp([P, COLS], F16)
        iota_p = temp([P, P], F16)
        iota_i = temp([P, COLS], I32)
        touched = temp([P, COLS])
        running = temp([P, COLS])
        idle_f = temp([P, COLS])
        idle_i = temp([P, COLS], I32)
        slot_i = sb("slot_i", [P, COLS], I32)
        pair_f = temp([P, COLS, 2])
        deg1 = temp([P, COLS])
        dinv2 = sb("dinv2", [P, COLS])
        base = sb("base", [P, 1])
        hot_p = [temp([P, 5, P], BF16) for _ in range(2)]
        hot_c = [temp([P, 2, COLS], BF16) for _ in range(2)]


        s_ld, s_ldw, s_rows = sem("s_ld"), sem("s_ldw"), sem("s_rows")
        s_const, s_dve, s_pre_pe = sem("s_const"), sem("s_dve"), sem("s_pre_pe")
        s_fill, s_table = sem("s_fill"), sem("s_table")
        s_hot, s_hotmm, s_pass = sem("s_hot"), sem("s_hotmm"), sem("s_pass")
        s_fillrow, s_tab_sb, s_cos, s_zero = sem("s_fillrow"), sem("s_tab_sb"), sem("s_cos"), sem("s_zero")
        s_deg, s_rsq = sem("s_deg"), sem("s_rsq")
        s_endsf, s_scan, s_turned, s_ready = sem("s_endsf"), sem("s_scan"), sem("s_turned"), sem("s_ready")

        CG = ring("cg_", 3, [P, G, 2 * D])
        fill_row = CG[0]

        X2 = [CG[1][:, i, :].rearrange("p (a d) -> p a d", a=2) for i in range(4)]
        H2 = [CG[2][:, i, :].rearrange("p (a d) -> p a d", a=2) for i in range(2)]
        Z2 = [CG[2][:, 2 + i, :].rearrange("p (a d) -> p a d", a=2) for i in range(2)]
        ib = ring("ib_", 2, [P, 4], I32)
        attr = ring("attr_", 4, [P, R])
        row_d = ring("row_d_", 4, [P, P], I32)
        st = ring("st_", 2, [P, 2, 6])
        sth = ring("sth_", 2, [P, 2, 6])
        mv = ring("mv_", 2, [P, 2, 2])
        mvh = ring("mvh_", 2, [P, 2, 2])
        rs = ring("rs_", 2, [P, 2, 1])
        rsh = ring("rsh_", 2, [P, 2, 1])
        ve = ring("ve_", 2, [P, 2, 1])
        veh = ring("veh_", 2, [P, 2, 1])
        nb = ring("nb_", 2, [P, 2, 1])
        nbh = ring("nbh_", 2, [P, 2, 1])
        zT = ring("zT_", 2, [P, 2 * KC, P])
        aT = ring("aT_", 2, [R + 1, P])
        DS = ring("ds_", 2, [P, 2 * D])
        KD = ring("kd_", 2, [P, D])
        junk = sb("junk", [P, D])
        junk_e = sb("junk_e", [P, P])
        at = ring("at_", 2, [P, 1])
        sa = ring("sa_", 2, [P, 1])
        aa = ring("aa_", 2, [P, 1])
        EQ = ring("eq_", 2, [P, P])
        MSG = ring("msg_", 2, [P, D])
        ST = ring("stt_", 2, [P, KC, P])
        UB = ring("ub_", 4, [P, D])
        tab_d = ring("tab_d_", 2, [P, 2])
        cnt = ring("cnt_", 2, [P, 1])
        fst = ring("fst_", 2, [P, 1])
        dif = ring("dif_", 2, [P, 1])
        sidx = ring("sidx_", 4, [P, 1], I32)
        m_ib, m_row, m_attr = sem("m_ib"), sems("m_row", 4), sems("m_attr", 4)
        m_x, m_tab = sems("m_x", 4), sems("m_tab", 2)
        (m_st, m_mv, m_ve, m_rs, m_nb, m_h, m_sth, m_mvh, m_veh, m_rsh, m_nbh, m_z, m_xh, m_T, m_zT, m_aT, m_D,
         m_qkv, m_ds, m_kd, m_at, m_sa, m_aa, m_eq, m_cnt, m_fst, m_dif, m_idx, m_msg, m_S, m_ST, m_U, m_UB, m_keep) = [
            sem("m_" + n) for n in ("st mv ve rs nb h sth mvh veh rsh nbh z xh T zT aT D qkv ds kd at sa aa eq cnt fst "
                                    "dif idx msg S ST U UB keep").split()]
        m_sc = sem("m_sc")

        C0 = ring("c0_", 2, [P, D])
        X1e = ring("x1e_", 2, [P, D])
        H1e = ring("h1e_", 2, [P, D])
        ic = ring("ic_", 2, [P, 2], I32)
        row_s = ring("row_s_", 4, [P, P], I32)
        tab_s = ring("tab_s_", 2, [P, 2])
        EN = ring("en_", 2, [P, P])
        nr = ring("nr_", 2, [P, 1])
        nr2 = ring("nr2_", 2, [P, 1])
        n_ic, n_row, n_c0, n_tab, n_sc = sem("n_ic"), sems("n_row", 4), sems("n_c0", 2), sems("n_tab", 2), sem("n_sc")
        (n_x1, n_st, n_mv, n_ve, n_rs, n_nb, n_h, n_eq, n_cnt, n_nr, n_nr2, n_en, n_fst, n_dif, n_idx, n_U, n_UB) = [
            sem("n_" + n) for n in "x1 st mv ve rs nb h eq cnt nr nr2 en fst dif idx U UB".split()]

        def part(width):
            return place(late, [P, width])

        X = [part(G * D) for _ in range(3)]
        X1 = [part(G * D) for _ in range(6)]
        H = [part(G * D) for _ in range(2)]
        H1 = [part(G * D) for _ in range(2)]
        AG = [part(G * D) for _ in range(2)]
        OUT = [part(G * D) for _ in range(2)]
        hT = [part(KC * GN) for _ in range(2)]
        rT = [part(KC * GN) for _ in range(2)]
        bi = ring("bi_", 2, [P, G], I32)
        b_st = ring("b_st_", 2, [P, G, 6])
        b_sth = ring("b_sth_", 2, [P, G, 6])
        b_mv = ring("b_mv_", 2, [P, G, 2])
        b_mvh = ring("b_mvh_", 2, [P, G, 2])
        b_ve, b_rs, b_nb = (ring(f"b_{n}_", 2, [P, G, 1]) for n in ("ve", "rs", "nb"))
        b_veh, b_rsh, b_rsd, b_nbh = (ring(f"b_{n}_", 2, [P, G, 1]) for n in ("veh", "rsh", "rsd", "nbh"))
        g_x, g_cg, g_out = sems("g_x", 3), sems("g_cg", 3), sems("g_out", 2)
        (g_bi, g_st, g_mv, g_ve, g_rs, g_nb, g_h, g_xh, g_x1, g_sth, g_mvh, g_veh, g_rsh, g_rsd, g_nbh, g_h1, g_ag, g_T,
         g_hT, g_m1, g_rT, g_m2, g_fin) = [
            sem("g_" + n) for n in "bi st mv ve rs nb h xh x1 sth mvh veh rsh rsd nbh h1 ag T hT m1 rT m2 fin".split()]
        s_end2 = sem("s_end2")

        def pass_on(eng, *waits):
            for s, v in waits:
                eng.wait_ge(s, v)
            if not all(isinstance(v, int) for _, v in waits):
                eng.sem_inc(s_pass)

        block = ctx.enter_context(nc.Block())

        @block.sync
        def _(sp):
            sp.wait_ge(s_zero, 1)
            full = (EC - 1) * P
            for i, t in enumerate((src, dst, edge_weight)):
                to = e_rows[:, i, :] if t.dtype == F32 else e_rows[:, i, :].bitcast(I32)
                sp.dma_start(to[0:EC - 1, :], t[0:full].rearrange("(c p) -> c p", p=P)).then_inc(s_rows, 16)
                sp.dma_start(to[EC - 1:EC, 0:ET], t[full:E].rearrange("(c p) -> c p", c=1)).then_inc(s_rows, 16)
            for i, w in enumerate((Wq, Wk, Wv, Wo, W)):
                sp.dma_start(w_raw[:, i, :, :], w.rearrange("(c p) k -> p c k", p=P)).then_inc(s_ldw, 16)
            for i, w in enumerate((Wdk, Wdv)):
                sp.dma_start(wd_raw[:, i, :, :], w.rearrange("(c p) k -> p c k", p=P)).then_inc(s_ldw, 16)
            sp.dma_start(w1_raw[:, :, :], W1.rearrange("(c p) k -> p c k", p=P)).then_inc(s_ldw, 16)
            sp.dma_start(w2_sb[:, :, :], W2.rearrange("(c p) k -> p c k", p=P)).then_inc(s_ldw, 16)
            with nc.allow_non_contiguous_dma(reason="256 numbers, one a partition"):
                for t, v in ((g_col, ln_g), (b_col, ln_b), (b0_col, b), (b1_col, b1)):
                    sp.dma_start(t[:, :], v.rearrange("(c p) -> p c", p=P)).then_inc(s_ldw, 16)
            for i, v in enumerate((bq, bk, bv, b2)):
                sp.dma_start(rows3[:, i * D:(i + 1) * D],
                             v.rearrange("(a d) -> a d", a=1).broadcast_to([3, D])).then_inc(s_ldw, 16)
            for i, v in enumerate((bdk, bdv)):
                sp.dma_start(wd_t[R:R + 1, i * D:(i + 1) * D], v.rearrange("(a d) -> a d", a=1)).then_inc(s_ldw, 16)
            sp.wait_ge(s_zero, 2)
            for r in range(FILL):
                sp.dma_start(fill_row[:, r, 0:D],
                             bo.rearrange("(a d) -> a d", a=1).broadcast_to([P, D])).then_inc(s_fillrow, 16)
            sp.wait_ge(s_fillrow, 16 * FILL)
            to = sums.rearrange("(p k r) d -> p k (r d)", p=P, r=FILL)
            for k in range(ROWS // (FILL * P)):
                sp.dma_start(to[:, k, :], fill_row[:, :, :].rearrange("p r d -> p (r d)")).then_inc(s_fill, 16)

            sp.wait_ge(s_tab_sb, 1)
            sp.dma_start(table.rearrange("(p c) k -> p (c k)", p=P),
                         pair_f[:, :, :].rearrange("p c k -> p (c k)")).then_inc(s_table, 16)

            def load_edges(s):
                k = s
                if k.within(EC):
                    n = k.off if k.reg is None else None
                    rows = ET if n == EC - 1 else P
                    if k.past(4):
                        pass_on(sp, (m_T, k.value(-3)))
                    sp.dma_start(attr[k.slot(4)][0:rows, :],
                                 edge_attr[bass.ds(k.value(0, P), rows), :]).then_inc(m_attr[k.slot(4)], 16)
                    if k.past(4):
                        pass_on(sp, (m_eq, k.value(-3)))
                    sp.dma_start(row_d[k.slot(4)][:, 0:rows],
                                 dst[bass.ds(k.value(0, P), rows)].rearrange("(a e) -> a e", a=1)
                                 .broadcast_to([P, rows])).then_inc(m_row[k.slot(4)], 16)

            run_steps(sp, EC, 0, 4, 4, load_edges)

            def load_src(s):
                k = s
                if k.within(EC):
                    n = k.off if k.reg is None else None
                    rows = ET if n == EC - 1 else P
                    if k.past(4):
                        pass_on(sp, (n_eq, k.value(-3)))
                    sp.dma_start(row_s[k.slot(4)][:, 0:rows],
                                 src[bass.ds(k.value(0, P), rows)].rearrange("(a e) -> a e", a=1)
                                 .broadcast_to([P, rows])).then_inc(n_row[k.slot(4)], 16)

            run_steps(sp, EC, 0, 4, 4, load_src)

            sp.wait_ge(s_end2, 1)
            STORE = 8

            def nodes(s):
                k = s
                if k.within(NG):
                    parts = GT if k.reg is None and k.off == NG - 1 else P
                    if k.past(3):
                        pass_on(sp, (g_xh, k.value(-2)))
                    sp.dma_start(X[k.slot(3)][0:parts, :],
                                 x[bass.ds(k.value(0, GN), parts * G), :].rearrange("(p j) d -> p (j d)", j=G)
                                 ).then_inc(g_x[k.slot(3)], 16)
                k = s.back(STORE)
                if k.within(NG):
                    parts = GT if k.reg is None and k.off == NG - 1 else P
                    pass_on(sp, (g_fin, k.value(1)))
                    sp.dma_start(out[bass.ds(k.value(0, GN), parts * G), :].rearrange("(p j) d -> p (j d)", j=G),
                                 OUT[k.slot(2)][0:parts, :]).then_inc(g_out[k.slot(2)], 16)

            run_steps(sp, NG, STORE, 6, 3, nodes)
            for q in range(2):
                sp.wait_ge(g_out[q], 16 * ((NG - q + 1) // 2))

        @block.gpsimd
        def _(pool):
            c = [0]

            def link(ins):
                c[0] += 1
                ins.then_inc(s_const, 1)
                pool.wait_ge(s_const, c[0])

            link(pool.memset(ones[:, :], 1.0))
            link(pool.affine_select(out=identity[:, :], in_=ones[:, :], compare_op=ALU.is_equal, fill=0.0,
                                    base=0, pattern=[[-1, P]], channel_multiplier=1))
            link(pool.affine_select(out=lower[:, :], in_=ones[:, :], compare_op=ALU.is_gt, fill=0.0,
                                    base=0, pattern=[[-1, P]], channel_multiplier=1))
            link(pool.affine_select(out=upper[:, :], in_=ones[:, :], compare_op=ALU.is_gt, fill=0.0,
                                    base=0, pattern=[[1, P]], channel_multiplier=-1))
            link(pool.iota(edge_no[:, :], [[P, EC]], base=0, channel_multiplier=1))
            link(pool.iota(iota_i[:, :], [[1, COLS]], base=0, channel_multiplier=0))
            link(pool.iota(idle_i[:, :], [[0, COLS // SPARE], [1, SPARE]], base=IDLE0, channel_multiplier=SPARE))
            link(pool.iota(dump_i[:, :], [[0, 1]], base=2 * DUMP0, channel_multiplier=2))
            link(pool.memset(minus_half[:, :], -0.5))
            link(pool.memset(eps_tile[:, :], EPS))
            last_node = pool.to_reg(N - 1)
            last_half = pool.to_reg(2 * ROWS - 1)
            last_row = pool.to_reg(ROWS - 1)
            last_entry = pool.to_reg(P * COLS - 1)

            pool.wait_ge(s_deg, 1)
            pool.tensor_tensor(deg1[:, :], deg1[:, :],
                               minus_half[:, 0:1].broadcast_to([P, COLS]), ALU.pow).then_inc(s_rsq, 1)

            def inv_sqrt(var, tmp, to, width, ready, mid, done, k):
                pool.wait_ge(ready, k.value(1))
                pool.tensor_tensor(tmp, var, eps_tile[:, 0:width].rearrange("p (a b) -> p a b", b=1),
                                   ALU.add).then_inc(mid, 1)
                pool.wait_ge(mid, k.value(1))
                pool.tensor_tensor(to, tmp, minus_half[:, 0:width].rearrange("p (a b) -> p a b", b=1),
                                   ALU.pow).then_inc(done, 1)

            SC = 7

            def messages(s):
                k = s.back(SC)
                if k.within(EC):
                    w = [(m_UB, k.value(1)), (m_idx, k.value(1))]
                    if k.past(1):
                        w.append((m_sc, k.value(0, 16)))
                    else:
                        w.append((s_fill, 16 * (ROWS // (FILL * P))))
                    pass_on(pool, *w)
                    pool.indirect_dma_start(halves, bass.IndirectOffsetOnAxis(sidx[k.slot(4)][:, :], 0),
                                            UB[k.slot(4)][:, :], None, bounds_check=last_half,
                                            compute_op=ALU.add).then_inc(m_sc, 16)
                k = s.back(1)
                if k.within(EC):
                    inv_sqrt(mv[k.slot(2)][:, :, 1:2], ve[k.slot(2)][:, :, :], rs[k.slot(2)][:, :, :], 2,
                             m_mv, m_ve, m_rs, k)
                k = s
                if k.within(EC):
                    w = [(m_ib, k.value(1))]
                    if k.past(4):
                        w.append((m_xh, k.value(-3)))
                        w.append((m_h, k.value(-3)))
                    pass_on(pool, *w)
                    for i in range(2):
                        pool.indirect_dma_start(X2[k.slot(4)][:, i, :], None, x,
                                                bass.IndirectOffsetOnAxis(ib[k.slot(2)][:, i:i + 1], 0),
                                                bounds_check=last_node, oob_is_err=True
                                                ).then_inc(m_x[k.slot(4)], 16)
                    if not k.past(1):
                        pool.wait_ge(s_table, 16)
                    if k.past(2):
                        pass_on(pool, (m_keep, k.value(-1)))
                    pool.indirect_dma_start(tab_d[k.slot(2)][:, :], None, table,
                                            bass.IndirectOffsetOnAxis(ib[k.slot(2)][:, 2:3], 0),
                                            bounds_check=last_entry, oob_is_err=True
                                            ).then_inc(m_tab[k.slot(2)], 16)
                k = s.back(2)
                if k.within(EC):
                    inv_sqrt(mvh[k.slot(2)][:, :, 1:2], veh[k.slot(2)][:, :, :], rsh[k.slot(2)][:, :, :], 2,
                             m_mvh, m_veh, m_rsh, k)

            run_steps(pool, EC, SC, 4, 4, messages)
            pool.wait_ge(m_sc, 16 * EC)

            def messages2(s):
                k = s.back(3)
                if k.within(EC):
                    w = [(n_UB, k.value(1)), (n_idx, k.value(1))]
                    if k.past(1):
                        w.append((n_sc, k.value(0, 16)))
                    pass_on(pool, *w)
                    pool.indirect_dma_start(halves, bass.IndirectOffsetOnAxis(sidx[k.slot(4)][:, :], 0),
                                            UB[k.slot(4)][:, :], None, bounds_check=last_half,
                                            compute_op=ALU.add).then_inc(n_sc, 16)
                k = s.back(1)
                if k.within(EC):
                    inv_sqrt(mv[k.slot(2)][:, 0:1, 1:2], ve[k.slot(2)][:, 0:1, :], rs[k.slot(2)][:, 0:1, :], 1,
                             n_mv, n_ve, n_rs, k)
                k = s
                if k.within(EC):
                    w = [(n_ic, k.value(1))]
                    if k.past(2):
                        w += [(n_x1, k.value(-1)), (n_nr, k.value(-1)), (n_dif, k.value(-1))]
                    pass_on(pool, *w)
                    pool.indirect_dma_start(C0[k.slot(2)][:, :], None, halves,
                                            bass.IndirectOffsetOnAxis(ic[k.slot(2)][:, 0:1], 0),
                                            bounds_check=last_half, oob_is_err=True).then_inc(n_c0[k.slot(2)], 16)
                    pool.indirect_dma_start(tab_s[k.slot(2)][:, :], None, table,
                                            bass.IndirectOffsetOnAxis(ic[k.slot(2)][:, 1:2], 0),
                                            bounds_check=last_entry, oob_is_err=True).then_inc(n_tab[k.slot(2)], 16)

            run_steps(pool, EC, 3, 4, 4, messages2)
            pool.wait_ge(n_sc, 16 * EC)

            def nodes(s):
                k = s
                if k.within(NG):
                    inv_sqrt(b_mv[k.slot(2)][:, :, 1:2], b_ve[k.slot(2)][:, :, :], b_rs[k.slot(2)][:, :, :], G,
                             g_mv, g_ve, g_rs, k)

                def gathers(js):
                    for j in js:
                        pool.indirect_dma_start(CG[k.slot(3)][:, j, :], None, sums,
                                                bass.IndirectOffsetOnAxis(bi[k.slot(2)][:, j:j + 1], 0),
                                                bounds_check=last_row, oob_is_err=True
                                                ).then_inc(g_cg[k.slot(3)], 16)

                if k.within(NG):
                    w = [(g_bi, k.value(1))]
                    if k.past(3):
                        w.append((g_ag, k.value(-2)))
                    pass_on(pool, *w)
                    gathers(range(0, 2))
                k1 = s.back(1)
                if k1.within(NG):
                    inv_sqrt(b_mvh[k1.slot(2)][:, :, 1:2], b_veh[k1.slot(2)][:, :, :], b_rsh[k1.slot(2)][:, :, :], G,
                             g_mvh, g_veh, g_rsh, k1)
                if k.within(NG):
                    gathers(range(2, G))

            run_steps(pool, NG, 1, 6, 3, nodes)

        @block.vector
        def _(dve):
            c = [0]

            def link(ins):
                c[0] += 1
                ins.then_inc(s_dve, 1)
                dve.wait_ge(s_dve, c[0])

            dve.memset(e_rows[:, :, :], 0.0).then_inc(s_zero, 1)
            dve.memset(fill_row[:, :, :], 0.0).then_inc(s_zero, 1)
            link(dve.memset(half_pi[:, :], PI / 2))
            link(dve.memset(ones3[:, :], 1.0))
            dve.wait_ge(s_const, 10)
            link(dve.tensor_copy(iota_c[:, :], iota_i[:, :]))
            link(dve.tensor_copy(iota_p[:, :], iota_i[:, 0:P]))
            link(dve.tensor_copy(idle_f[:, :], idle_i[:, :]))
            link(dve.tensor_copy(dump_f[:, :], dump_i[:, :]))
            link(dve.tensor_scalar(dump2_f[:, :], dump_f[:, :], 1.0, None, ALU.add))
            link(dve.tensor_scalar(valid[:, :], edge_no[:, :], float(E), None, ALU.is_lt))
            link(dve.tensor_copy(pick3[:, :], identity[0:3, 0:3]))
            for i in range(2):
                link(dve.memset(aT[i][R:R + 1, :], 1.0))
            for i in range(4):
                link(dve.memset(attr[i][:, :], 0.0))
                link(dve.memset(row_d[i][:, :], 0))
                link(dve.memset(row_s[i][:, :], 0))

            dve.wait_ge(s_rows, 96)
            dve.tensor_copy(e_rowf[:, :, :], e_rows[:, 0:2, :].bitcast(I32)).then_inc(s_endsf, 1)
            dve.wait_ge(s_pre_pe, 1)
            for i, t in enumerate((src_f, dst_f, ew_f)):
                link(dve.tensor_copy(t[:, :], bank[:, 0, i * P:i * P + EC]))
            link(dve.tensor_copy(node_i[:, :, 0], dst_f[:, :]))
            link(dve.tensor_copy(node_i[:, :, 1], src_f[:, :]))
            link(dve.tensor_scalar(key_i[:, :, :], node_i[:, :, :], 2, P - 1, ALU.logical_shift_right,
                                   ALU.bitwise_and))
            link(dve.tensor_copy(pkey[:, :, :], key_i[:, :, :]))
            link(dve.tensor_scalar(key_i[:, :, :], node_i[:, :, :], 9, 2, ALU.logical_shift_right,
                                   ALU.logical_shift_left))
            link(dve.tensor_scalar(key_j[:, :, :], node_i[:, :, :], G - 1, None, ALU.bitwise_and))
            link(dve.tensor_tensor(ckey[:, :, :], key_i[:, :, :], key_j[:, :, :], ALU.add))
            link(dve.scalar_tensor_tensor(at_i[:, :, :], pkey[:, :, :], float(COLS), ckey[:, :, :], ALU.mult, ALU.add))
            link(dve.tensor_scalar(away[:, :], valid[:, :], -1000.0, 1000.0, ALU.mult, ALU.add))
            for i in range(2):
                link(dve.tensor_tensor(pkey[:, :, i], pkey[:, :, i], away[:, :], ALU.add))
            link(dve.tensor_copy(ew_low[0][:, :], ew_f[:, :]))
            link(dve.tensor_copy(ew_part[0][:, :], ew_low[0][:, :]))
            link(dve.tensor_tensor(ew_part[2][:, :], ew_f[:, :], ew_part[0][:, :], ALU.subtract))
            link(dve.tensor_copy(ew_low[1][:, :], ew_part[2][:, :]))
            link(dve.tensor_copy(ew_part[1][:, :], ew_low[1][:, :]))
            link(dve.tensor_tensor(ew_part[2][:, :], ew_part[2][:, :], ew_part[1][:, :], ALU.subtract))

            def col(t, k, i=None):
                if i is not None:
                    return t[:, bass.ds(k.value(0), 1), i]
                at0 = t[:, bass.ds(k.value(0), 1)]
                return at0 if len(t.shape) == 2 else at0.rearrange("p a b -> p (a b)")

            def hot(s):
                k = s
                if k.past(2):
                    dve.wait_ge(s_hotmm, k.value(-1))
                q = k.slot(2)

                for i in range(2):
                    dve.tensor_scalar(hot_p[q][:, i, :], iota_p[:, :], col(pkey, k, i), None, ALU.is_equal)
                    last = dve.tensor_scalar(hot_c[q][:, i, :], iota_c[:, :], col(ckey, k, i), None, ALU.is_equal)
                for i in range(3):
                    last = dve.tensor_scalar(hot_p[q][:, 2 + i, :], iota_p[:, :], col(pkey, k, 1), col(ew_part[i], k),
                                             ALU.is_equal, ALU.mult)
                last.then_inc(s_hot, 1)

            run_steps(dve, EC, 0, 2, 2, hot)

            dve.wait_ge(s_hotmm, EC)
            link(dve.tensor_scalar(touched[:, :], bank[:, 1, 0:COLS], 1.0, None, ALU.min))
            link(dve.tensor_scalar(deg1[:, :], bank[:, 2, 0:COLS], 1.0, None, ALU.add))
            link(dve.tensor_scalar(dinv2[:, :], deg1[:, :], 0.0, None, ALU.is_gt))
            dve.tensor_scalar(deg1[:, :], deg1[:, :], 1e-30, None, ALU.max).then_inc(s_deg, 1)
            dve.tensor_tensor_scan(running[:, :], ones[:, 0:1].broadcast_to([P, COLS]), touched[:, :], 0.0,
                                   ALU.mult, ALU.add).then_inc(s_scan, 1)
            dve.wait_ge(s_pre_pe, 2)
            link(dve.tensor_scalar(base[:, :], bank[:, 3, 0:1], -1.0, None, ALU.add))
            link(dve.scalar_tensor_tensor(running[:, :], running[:, :], base[:, :], idle_f[:, :], ALU.add,
                                          ALU.subtract))
            link(dve.tensor_tensor(running[:, :], running[:, :], touched[:, :], ALU.mult))
            link(dve.tensor_tensor(running[:, :], running[:, :], idle_f[:, :], ALU.add))
            link(dve.tensor_copy(slot_i[:, :], running[:, :]))
            link(dve.tensor_scalar(pair_f[:, :, 0], running[:, :], 2.0, None, ALU.mult))
            dve.wait_ge(s_rsq, 1)
            link(dve.tensor_tensor(pair_f[:, :, 1], deg1[:, :], dinv2[:, :], ALU.mult))
            dve.tensor_tensor(dinv2[:, :], pair_f[:, :, 1], pair_f[:, :, 1], ALU.mult).then_inc(s_tab_sb, 1)
            link(dve.tensor_scalar(away[:, :], ew_f[:, :], -1.0, None, ALU.mult))
            link(dve.tensor_tensor(away[:, :], away[:, :], ew_f[:, :], ALU.max))
            link(dve.tensor_scalar(cut[:, :], away[:, :], PI / CUTOFF, None, ALU.mult))
            dve.tensor_scalar(cut[:, :], cut[:, :], PI, None, ALU.min).then_inc(s_cos, 1)
            dve.wait_ge(s_cos, 2)
            link(dve.tensor_scalar(cut[:, :], cut[:, :], 0.5, 0.5, ALU.mult, ALU.add))
            link(dve.tensor_scalar(away[:, :], ew_f[:, :], CUTOFF, None, ALU.is_lt))
            link(dve.tensor_tensor(cut[:, :], cut[:, :], away[:, :], ALU.mult))
            link(dve.tensor_tensor(cut[:, :], cut[:, :], valid[:, :], ALU.mult))

            dve.wait_ge(s_ldw, 16 * 19)
            for i in range(3):
                dve.wait_ge(s_pre_pe, 3 + i)
                for k in range(KC):
                    link(dve.tensor_copy(wq_t[:, i, k, :], bank[:, 4 + i, k * D:(k + 1) * D]))
                    link(dve.tensor_scalar(qkv_w[:, k, i * D:(i + 1) * D], bank[:, 4 + i, k * D:(k + 1) * D],
                                           g_col[:, k:k + 1], None, ALU.mult))
            dve.wait_ge(s_pre_pe, 6)
            link(dve.tensor_copy(wo_t[:, :, :].rearrange("p k d -> p (k d)"), bank[:, 7, :]))
            dve.wait_ge(s_pre_pe, 7)
            link(dve.tensor_copy(w_t[:, :, :].rearrange("p k d -> p (k d)"), bank[:, 1, :]))
            dve.wait_ge(s_pre_pe, 8)
            dve.tensor_copy(wd_t[0:R, :], bank[0:R, 2, :]).then_inc(s_turned, 1)
            dve.wait_ge(s_pre_pe, 9)
            link(dve.tensor_copy(part3[:, D * 3:], rows3[:, D * 3:]))
            link(dve.tensor_tensor(part3[:, 0:2 * D], rows3[:, 0:2 * D], bank[0:3, 4, :], ALU.add))
            link(dve.tensor_tensor(part3[:, 2 * D:3 * D], rows3[:, 2 * D:3 * D], bank[0:3, 5, 0:D], ALU.add))
            link(dve.tensor_copy(piece[0][:, :], part3[:, :]))
            link(dve.tensor_tensor(rest3[:, :], part3[:, :], piece[0][:, :], ALU.subtract))
            link(dve.tensor_copy(piece[1][:, :], rest3[:, :]))
            link(dve.tensor_tensor(rest3[:, :], rest3[:, :], piece[1][:, :], ALU.subtract))
            link(dve.tensor_copy(piece[2][:, :], rest3[:, :]))
            link(dve.tensor_scalar(rest3[:, :], piece[0][:, :], pick3[:, 0:1], None, ALU.mult))
            for i in (1, 2):
                link(dve.scalar_tensor_tensor(rest3[:, :], piece[i][:, :], pick3[:, i:i + 1], rest3[:, :], ALU.mult,
                                              ALU.add))
            link(dve.tensor_copy(bias3[:, :], rest3[:, :]))
            dve.wait_ge(s_pre_pe, 10)
            link(dve.tensor_copy(w01[:, :, :].rearrange("p k d -> p (k d)"), bank[:, 6, :]))
            dve.tensor_tensor(b01_col[:, :], b1_col[:, :], bank[:, 3, 0:KC], ALU.add).then_inc(s_ready, 1)
            dve.wait_ge(s_table, 16)

            def messages(s):
                k = s
                if k.within(EC):
                    w = []
                    if k.past(2):
                        w = [(m_x[k.back(2).slot(4)], k.back(2).turns(4, 32)),
                             (m_tab[k.slot(2)], k.back(2).turns(2))]
                    pass_on(dve, *w)
                    dve.tensor_copy(ib[k.slot(2)][:, 0:2], col(node_i, k))
                    dve.tensor_copy(ib[k.slot(2)][:, 2:4], col(at_i, k)).then_inc(m_ib, 1)
                m, a, h, t = s.back(5), s.back(1), s.back(2), s.back(6)
                q = m.slot(2)
                if m.within(EC):
                    dve.wait_ge(m_qkv, m.value(1))
                    dve.wait_ge(m_ds, m.value(1))
                    dve.tensor_tensor(KD[q][:, :], bank[:, 2 + q, 0:D], DS[q][:, 0:D], ALU.mult).then_inc(m_kd, 1)
                if a.within(EC):
                    dve.wait_ge(m_x[a.slot(4)], a.turns(4, 32))
                    for i in range(2):
                        ins = dve.bn_stats(st[a.slot(2)][:, i, :], X2[a.slot(4)][:, i, :])
                    ins.then_inc(m_st, 1)
                if m.within(EC):
                    dve.wait_ge(m_kd, m.value(1))
                    dve.tensor_tensor_reduce(junk[:, :], bank[:, 4, 0:D], KD[q][:, :], 1.0, 0.0,
                                             ALU.mult, ALU.add, at[q][:, :]).then_inc(m_at, 1)
                if a.within(EC):
                    pass_on(dve, (m_st, a.value(1)))
                    for i in range(2):
                        ins = dve.bn_aggr(mv[a.slot(2)][:, i, :], st[a.slot(2)][:, i, :])
                    ins.then_inc(m_mv, 1)
                if m.within(EC):
                    pass_on(dve, (m_row[m.slot(4)], m.turns(4)))
                    dve.tensor_scalar(EQ[q][:, :], row_d[m.slot(4)][:, :], col(dst_f, m), None,
                                      ALU.is_equal).then_inc(m_eq, 1)
                if t.within(EC):
                    dve.wait_ge(m_S, t.value(1))
                    dve.tensor_copy(ST[t.slot(2)][:, :, :].rearrange("p k e -> p (k e)"),
                                    bank[:, 5, 0:KC * P]).then_inc(m_ST, 1)
                if m.within(EC):
                    dve.wait_ge(m_sa, m.value(1))
                    dve.tensor_scalar(aa[q][:, :], sa[q][:, :], col(cut, m), None, ALU.mult).then_inc(m_aa, 1)
                if a.within(EC):
                    dve.wait_ge(m_rs, a.value(1))
                    dve.scalar_tensor_tensor(nb[a.slot(2)][:, :, :], mv[a.slot(2)][:, :, 0:1], -1.0,
                                             rs[a.slot(2)][:, :, :], ALU.mult, ALU.mult).then_inc(m_nb, 1)
                if m.within(EC):
                    dve.wait_ge(m_eq, m.value(1))
                    dve.tensor_tensor_reduce(junk_e[:, :], EQ[q][:, :], lower[:, :], 1.0, 0.0, ALU.mult, ALU.add,
                                             cnt[q][:, :]).then_inc(m_cnt, 1)
                    dve.wait_ge(m_aa, m.value(1))
                    dve.scalar_tensor_tensor(MSG[q][:, :], bank[:, 2 + q, D:2 * D], aa[q][:, 0:1], DS[q][:, D:2 * D],
                                             ALU.mult, ALU.mult).then_inc(m_msg, 1)
                if h.within(EC):
                    dve.wait_ge(m_h, h.value(1))
                    for i in range(2):
                        ins = dve.bn_stats(sth[h.slot(2)][:, i, :], H2[h.slot(2)][:, i, :])
                    ins.then_inc(m_sth, 1)
                    dve.tensor_tensor(kept[:, bass.ds(h.value(0), 1), :].rearrange("p a d -> p (a d)"),
                                      X2[h.slot(4)][:, 0, :], H2[h.slot(2)][:, 0, :], ALU.add).then_inc(m_xh, 1)
                    pass_on(dve, (m_sth, h.value(1)))
                    for i in range(2):
                        ins = dve.bn_aggr(mvh[h.slot(2)][:, i, :], sth[h.slot(2)][:, i, :])
                    ins.then_inc(m_mvh, 1)
                if a.within(EC):
                    pass_on(dve, (m_tab[a.slot(2)], a.turns(2)))
                    dve.tensor_copy(col(ends_d, a), tab_d[a.slot(2)][:, :]).then_inc(m_keep, 1)
                if m.within(EC):
                    pass_on(dve, (m_cnt, m.value(1)), (m_keep, m.value(1)))
                    dve.tensor_scalar(fst[q][:, :], cnt[q][:, :], 0.5, col(valid, m), ALU.is_lt,
                                      ALU.mult)
                    dve.tensor_tensor(dif[q][:, :], col(ends_d, m, 0), dump_f[:, :], ALU.subtract).then_inc(m_fst, 1)
                w3 = s.back(3)
                if w3.within(EC):
                    dve.wait_ge(m_T, w3.value(1))
                    if w3.past(2):
                        dve.wait_ge(m_D, w3.value(-1))
                    dve.tensor_copy(aT[w3.slot(2)][0:R, :], bank[0:R, 7, 0:P]).then_inc(m_aT, 1)
                if m.within(EC):
                    w = [(m_fst, m.value(1))]
                    if m.past(4):
                        w.append((m_sc, m.value(-3, 16)))
                    for z, v in w:
                        dve.wait_ge(z, v)
                    dve.scalar_tensor_tensor(sidx[m.slot(4)][:, :], dif[q][:, :], fst[q][:, 0:1], dump_f[:, :],
                                             ALU.mult, ALU.add).then_inc(m_idx, 1)
                if h.within(EC):
                    dve.wait_ge(m_rsh, h.value(1))
                    dve.scalar_tensor_tensor(nbh[h.slot(2)][:, :, :], mvh[h.slot(2)][:, :, 0:1], -1.0,
                                             rsh[h.slot(2)][:, :, :], ALU.mult, ALU.mult).then_inc(m_nbh, 1)

            run_steps(dve, EC, 6, 4, 4, messages)

            dve.wait_ge(m_xh, EC)

            def messages2(s):
                k = s
                if k.within(EC):
                    w = []
                    if k.past(2):
                        w = [(n_c0[k.slot(2)], k.back(2).turns(2)), (n_tab[k.slot(2)], k.back(2).turns(2))]
                    pass_on(dve, *w)
                    dve.tensor_copy(ic[k.slot(2)][:, 0:1], col(ends_d, k, 0))
                    dve.tensor_copy(ic[k.slot(2)][:, 1:2], col(at_i, k, 1)).then_inc(n_ic, 1)
                a = s.back(1)
                q = a.slot(2)
                if a.within(EC):
                    w = [(n_c0[q], a.turns(2))]
                    if a.past(2):
                        w.append((n_h, a.value(-1)))
                    pass_on(dve, *w)
                    dve.tensor_tensor(X1e[q][:, :], kept[:, bass.ds(a.value(0), 1), :].rearrange("p a d -> p (a d)"),
                                      C0[q][:, :], ALU.add).then_inc(n_x1, 1)
                    pass_on(dve, (n_row[a.slot(4)], a.turns(4)))
                    dve.tensor_scalar(EQ[q][:, :], row_s[a.slot(4)][:, :], col(src_f, a), None,
                                      ALU.is_equal).then_inc(n_eq, 1)
                    dve.wait_ge(n_x1, a.value(1))
                    dve.bn_stats(st[q][:, 0, :], X1e[q][:, :]).then_inc(n_st, 1)
                    pass_on(dve, (n_tab[q], a.turns(2)))
                    dve.tensor_tensor(nr[q][:, :], tab_s[q][:, 1:2], col(ew_f, a), ALU.mult).then_inc(n_nr, 1)
                    pass_on(dve, (n_st, a.value(1)))
                    dve.bn_aggr(mv[q][:, 0, :], st[q][:, 0, :]).then_inc(n_mv, 1)
                    dve.wait_ge(n_eq, a.value(1))
                    dve.tensor_tensor_reduce(junk_e[:, :], EQ[q][:, :], lower[:, :], 1.0, 0.0, ALU.mult, ALU.add,
                                             cnt[q][:, :]).then_inc(n_cnt, 1)
                    pass_on(dve, (n_nr, a.value(1)))
                    dve.tensor_tensor(nr2[q][:, :], nr[q][:, :], col(ends_d, a, 1), ALU.mult).then_inc(n_nr2, 1)
                    dve.tensor_tensor(dif[q][:, :], tab_s[q][:, 0:1], dump_f[:, :], ALU.subtract).then_inc(n_dif, 1)
                    pass_on(dve, (n_cnt, a.value(1)))
                    dve.tensor_scalar(fst[q][:, :], cnt[q][:, :], 0.5, col(valid, a), ALU.is_lt,
                                      ALU.mult).then_inc(n_fst, 1)
                    dve.wait_ge(n_nr2, a.value(1))
                    if a.past(2):
                        dve.wait_ge(n_U, a.value(-1))
                    dve.tensor_scalar(EN[q][:, :], EQ[q][:, :], nr2[q][:, 0:1], None, ALU.mult).then_inc(n_en, 1)
                    dve.wait_ge(n_fst, a.value(1))
                    dve.wait_ge(n_dif, a.value(1))
                    if a.past(4):
                        dve.wait_ge(n_sc, a.value(-3, 16))
                    dve.scalar_tensor_tensor(sidx[a.slot(4)][:, :], dif[q][:, :], fst[q][:, 0:1], dump2_f[:, :],
                                             ALU.mult, ALU.add).then_inc(n_idx, 1)
                    dve.wait_ge(n_rs, a.value(1))
                    dve.scalar_tensor_tensor(nb[q][:, 0:1, :], mv[q][:, 0:1, 0:1], -1.0,
                                             rs[q][:, 0:1, :], ALU.mult, ALU.mult).then_inc(n_nb, 1)

            run_steps(dve, EC, 1, 4, 4, messages2)
            dve.wait_ge(n_x1, EC)
            dve.sem_inc(s_end2)

            FIN = 6

            def nodes(s):
                k = s.back(FIN)
                if k.within(NG):
                    if k.past(2):
                        dve.wait_ge(g_out[k.slot(2)], k.back(2).turns(2))
                    dve.wait_ge(g_m2, k.value(1))
                    dve.tensor_tensor(OUT[k.slot(2)], X1[k.slot(6)],
                                      bank[:, 4:6, :].rearrange("p a b -> p (a b)"), ALU.add).then_inc(g_fin, 1)
                k = s
                if k.within(NG):
                    dve.wait_ge(g_x[k.slot(3)], k.turns(3))
                    for j in range(G):
                        ins = dve.bn_stats(b_st[k.slot(2)][:, j, :], X[k.slot(3)][:, j * D:(j + 1) * D])
                    ins.then_inc(g_st, 1)
                    w = []
                    if k.past(2):
                        w = [(g_cg[k.back(2).slot(3)], k.back(2).turns(3, 16 * G))]
                    pass_on(dve, *w)
                    dve.tensor_copy(bi[k.slot(2)][:, :], slot_i[:, bass.ds(k.value(0, G), G)]).then_inc(g_bi, 1)
                    pass_on(dve, (g_st, k.value(1)))
                    for j in range(G):
                        ins = dve.bn_aggr(b_mv[k.slot(2)][:, j, :], b_st[k.slot(2)][:, j, :])
                    ins.then_inc(g_mv, 1)
                r = s.back(1)
                q = r.slot(2)
                if r.within(NG):
                    dve.wait_ge(g_h, r.value(1))
                    dve.tensor_tensor(X1[r.slot(6)], X[r.slot(3)], H[q], ALU.add).then_inc(g_xh, 1)
                if k.within(NG):
                    dve.wait_ge(g_rs, k.value(1))
                    dve.scalar_tensor_tensor(b_nb[k.slot(2)][:, :, :], b_mv[k.slot(2)][:, :, 0:1], -1.0,
                                             b_rs[k.slot(2)][:, :, :], ALU.mult, ALU.mult).then_inc(g_nb, 1)
                if r.within(NG):
                    dve.wait_ge(g_xh, r.value(1))
                    dve.wait_ge(g_cg[r.slot(3)], r.turns(3, 16 * G))
                    dve.tensor_tensor(X1[r.slot(6)].rearrange("p (j d) -> p j d", j=G),
                                      X1[r.slot(6)].rearrange("p (j d) -> p j d", j=G),
                                      CG[r.slot(3)][:, :, 0:D], ALU.add).then_inc(g_x1, 1)
                    dve.wait_ge(g_x1, r.value(1))
                    for j in range(G):
                        ins = dve.bn_stats(b_sth[q][:, j, :], X1[r.slot(6)][:, j * D:(j + 1) * D])
                    ins.then_inc(g_sth, 1)
                    pass_on(dve, (g_sth, r.value(1)))
                    for j in range(G):
                        ins = dve.bn_aggr(b_mvh[q][:, j, :], b_sth[q][:, j, :])
                    ins.then_inc(g_mvh, 1)
                k = s.back(2)
                if k.within(NG):
                    dve.wait_ge(g_h1, k.value(1))
                    if k.past(2):
                        dve.wait_ge(g_T, k.value(-1))
                    dve.tensor_tensor(AG[k.slot(2)].rearrange("p (j d) -> p j d", j=G),
                                      H1[k.slot(2)].rearrange("p (j d) -> p j d", j=G),
                                      CG[k.slot(3)][:, :, D:2 * D], ALU.add).then_inc(g_ag, 1)
                if r.within(NG):
                    pass_on(dve, (g_rsh, r.value(1)))
                    dve.tensor_tensor(b_rsd[q][:, :, 0], b_rsh[q][:, :, 0],
                                      dinv2[:, bass.ds(r.value(0, G), G)], ALU.mult).then_inc(g_rsd, 1)
                    dve.wait_ge(g_rsd, r.value(1))
                    dve.scalar_tensor_tensor(b_nbh[q][:, :, :], b_mvh[q][:, :, 0:1], -1.0,
                                             b_rsd[q][:, :, :], ALU.mult, ALU.mult).then_inc(g_nbh, 1)

            run_steps(dve, NG, FIN, 6, 6, nodes)

        @block.scalar
        def _(act):
            act.wait_ge(s_cos, 1)
            act.wait_ge(s_dve, 1)
            act.activation(cut[:, :], cut[:, :], ACT.Sin, bias=half_pi[:, 0:1], scale=-1.0).then_inc(s_cos, 1)

            def messages(s):
                k = s.back(3)
                if k.within(EC):
                    act.wait_ge(m_T, k.value(1))
                    if k.past(2):
                        act.wait_ge(m_qkv, k.value(-1))
                    act.activation(zT[k.slot(2)][:, :, :].rearrange("p a e -> p (a e)"), bank[:, 0, :],
                                   ACT.Copy).then_inc(m_zT, 1)
                k = s.back(7)
                if k.within(EC):
                    act.wait_ge(m_U, k.value(1))
                    if k.past(4):
                        act.wait_ge(m_sc, k.value(-3, 16))
                    act.activation(UB[k.slot(4)][:, :], bank[:, 6, 0:D], ACT.Copy).then_inc(m_UB, 1)
                k = s.back(5)
                if k.within(EC):
                    act.wait_ge(m_at, k.value(1))
                    if k.past(2):
                        act.wait_ge(m_aa, k.value(-1))
                    act.activation(sa[k.slot(2)][:, :], at[k.slot(2)][:, :], ACT.Silu).then_inc(m_sa, 1)
                k = s.back(4)
                if k.within(EC):
                    act.wait_ge(m_D, k.value(1))
                    if k.past(2):
                        act.wait_ge(m_msg, k.value(-1))
                    act.activation(DS[k.slot(2)][:, :], bank[:, 1, :], ACT.Silu).then_inc(m_ds, 1)
                k = s.back(1)
                if k.within(EC):
                    act.wait_ge(m_nb, k.value(1))
                    if k.past(2):
                        act.wait_ge(m_xh, k.value(-1))
                    for i in range(2):
                        ins = act.activation(H2[k.slot(2)][:, i, :], X2[k.slot(4)][:, i, :], ACT.Relu,
                                             bias=nb[k.slot(2)][:, i, :], scale=rs[k.slot(2)][:, i, :])
                    ins.then_inc(m_h, 1)
                k = s.back(2)
                if k.within(EC):
                    act.wait_ge(m_nbh, k.value(1))
                    if k.past(2):
                        act.wait_ge(m_T, k.value(-1))
                    for i in range(2):
                        ins = act.activation(Z2[k.slot(2)][:, i, :], H2[k.slot(2)][:, i, :], ACT.Identity,
                                             bias=nbh[k.slot(2)][:, i, :], scale=rsh[k.slot(2)][:, i, :])
                    ins.then_inc(m_z, 1)

            run_steps(act, EC, 7, 4, 4, messages)

            def messages2(s):
                k = s.back(2)
                if k.within(EC):
                    act.wait_ge(n_U, k.value(1))
                    if k.past(4):
                        act.wait_ge(n_sc, k.value(-3, 16))
                    act.activation(UB[k.slot(4)][:, :], bank[:, k.slot(2), 0:D], ACT.Copy).then_inc(n_UB, 1)
                k = s.back(1)
                if k.within(EC):
                    act.wait_ge(n_nb, k.value(1))
                    if k.past(2):
                        act.wait_ge(n_U, k.value(-1))
                    act.activation(H1e[k.slot(2)][:, :], X1e[k.slot(2)][:, :], ACT.Relu, bias=nb[k.slot(2)][:, 0, :],
                                   scale=rs[k.slot(2)][:, 0, :]).then_inc(n_h, 1)

            run_steps(act, EC, 2, 4, 4, messages2)

            def nodes(s):
                k = s.back(3)
                if k.within(NG):
                    act.wait_ge(g_T, k.value(1))
                    if k.past(2):
                        act.wait_ge(g_m1, k.value(-1))
                    for c in range(KC):
                        ins = act.activation(hT[k.slot(2)][:, c * GN:(c + 1) * GN], bank[:, c, :], ACT.Copy)
                    ins.then_inc(g_hT, 1)
                k = s
                if k.within(NG):
                    act.wait_ge(g_nb, k.value(1))
                    if k.past(2):
                        act.wait_ge(g_xh, k.value(-1))
                    for j in range(G):
                        ins = act.activation(H[k.slot(2)][:, j * D:(j + 1) * D], X[k.slot(3)][:, j * D:(j + 1) * D],
                                             ACT.Relu, bias=b_nb[k.slot(2)][:, j, :], scale=b_rs[k.slot(2)][:, j, :])
                    ins.then_inc(g_h, 1)
                k = s.back(4)
                if k.within(NG):
                    act.wait_ge(g_m1, k.value(1))
                    if k.past(2):
                        act.wait_ge(g_m2, k.value(-1))
                    for c in range(KC):
                        ins = act.activation(rT[k.slot(2)][:, c * GN:(c + 1) * GN], bank[:, 2 + c, :], ACT.Relu,
                                             bias=b01_col[:, c:c + 1])
                    ins.then_inc(g_rT, 1)
                k = s.back(1)
                if k.within(NG):
                    act.wait_ge(g_nbh, k.value(1))
                    if k.past(2):
                        act.wait_ge(g_ag, k.value(-1))
                    for j in range(G):
                        ins = act.activation(H1[k.slot(2)][:, j * D:(j + 1) * D], X1[k.slot(6)][:, j * D:(j + 1) * D],
                                             ACT.Relu, bias=b_nbh[k.slot(2)][:, j, :],
                                             scale=b_rsd[k.slot(2)][:, j, :])
                    ins.then_inc(g_h1, 1)

            run_steps(act, NG, 4, 6, 6, nodes)

        @block.tensor
        def _(pe):
            pe.wait_ge(s_const, 4)
            pe.wait_ge(s_rows, 96)
            pe.wait_ge(s_endsf, 1)
            for i in range(3):
                t = e_rows[:, 2, :] if i == 2 else e_rowf[:, i, :]
                ins = pe.transpose(bank[:, 0, i * P:i * P + EC], t, identity[0:EC, 0:EC])
            ins.then_inc(s_pre_pe, 1)

            def hot(s):
                k = s
                q = k.slot(2)
                pe.wait_ge(s_hot, k.value(1))
                first, last = k.reg is None and k.off == 0, k.reg is None and k.off == EC - 1
                for i in range(2):
                    pe.matmul(bank[:, 1, 0:COLS], hot_p[q][:, i, :], hot_c[q][:, i, :], start=first and i == 0,
                              stop=last and i == 1)
                for i in range(3):
                    ins = pe.matmul(bank[:, 2, 0:COLS], hot_p[q][:, 2 + i, :], hot_c[q][:, 1, :],
                                    start=first and i == 0, stop=last and i == 2)
                ins.then_inc(s_hotmm, 1)

            run_steps(pe, EC, 0, 2, 2, hot)
            pe.wait_ge(s_scan, 1)
            pe.matmul(bank[:, 3, 0:1], upper[:, :], running[:, COLS - 1:COLS], start=True,
                      stop=True).then_inc(s_pre_pe, 1)
            pe.wait_ge(s_ldw, 16 * 19)

            def turned(to, w):
                for k in range(KC):
                    for o in range(KC):
                        ins = pe.transpose(bank[:, to, k * D + o * P:k * D + (o + 1) * P],
                                           w[:, o, k * P:(k + 1) * P], identity[:, :])
                ins.then_inc(s_pre_pe, 1)

            for i in range(3):
                turned(4 + i, w_raw[:, i])
            turned(7, w_raw[:, 3])
            turned(1, w_raw[:, 4])
            for i in range(2):
                for o in range(KC):
                    ins = pe.transpose(bank[0:R, 2, i * D + o * P:i * D + (o + 1) * P], wd_raw[:, i, o, :],
                                       identity[:, :])
            ins.then_inc(s_pre_pe, 1)
            pe.wait_ge(s_turned, 1)
            for i in range(3):
                for k in range(KC):
                    ins = pe.matmul(bank[0:3, 4 + i // 2, (i % 2) * D:(i % 2 + 1) * D],
                                    b_col[:, k:k + 1].broadcast_to([P, 3]), wq_t[:, i, k, :],
                                    start=(k == 0), stop=(k == KC - 1))
            ins.then_inc(s_pre_pe, 1)
            for m in range(KC):
                for k in range(KC):
                    pe.matmul(bank[:, 6, m * D:(m + 1) * D], w_t[:, k, m * P:(m + 1) * P], w1_raw[:, k, :],
                              start=(k == 0), stop=(k == KC - 1))
            for m in range(KC):
                for k in range(KC):
                    ins = pe.matmul(bank[:, 3, m:m + 1], w1_raw[:, k, m * P:(m + 1) * P], b0_col[:, k:k + 1],
                                    start=(k == 0), stop=(k == KC - 1))
            ins.then_inc(s_pre_pe, 1)
            pe.wait_ge(s_ready, 1)

            def messages(s):
                k = s.back(3)
                if k.within(EC):
                    pe.wait_ge(m_z, k.value(1))
                    pe.wait_ge(m_attr[k.slot(4)], k.turns(4))
                    if k.past(1):
                        pe.wait_ge(m_zT, k.value(0))
                        pe.wait_ge(m_aT, k.value(0))
                    for i in range(2):
                        for c in range(KC):
                            pe.transpose(bank[:, 0, (i * KC + c) * P:(i * KC + c + 1) * P],
                                         Z2[k.slot(2)][:, i, c * P:(c + 1) * P], identity[:, :])
                    pe.transpose(bank[0:R, 7, 0:P], attr[k.slot(4)][:, :], identity[:, :]).then_inc(m_T, 1)
                k = s.back(4)
                if k.within(EC):
                    q = k.slot(2)
                    pe.wait_ge(m_aT, k.value(1))
                    if k.past(1):
                        pe.wait_ge(m_ds, k.value(0))
                    pe.matmul(bank[:, 1, :], aT[q][:, :], wd_t[:, :], start=True, stop=True).then_inc(m_D, 1)
                    pe.wait_ge(m_zT, k.value(1))
                    if k.past(2):
                        pe.wait_ge(m_msg, k.value(-1))
                    pe.matmul(bank[:, 2 + q, :], ones3[:, :], bias3[:, D:3 * D], start=True, stop=False)
                    for c in range(KC):
                        pe.matmul(bank[:, 2 + q, :], zT[q][:, KC + c, :], qkv_w[:, c, D:3 * D], start=False,
                                  stop=(c == KC - 1))
                    if k.past(1):
                        pe.wait_ge(m_at, k.value(0))
                    pe.matmul(bank[:, 4, 0:D], ones3[:, :], bias3[:, 0:D], start=True, stop=False)
                    for c in range(KC):
                        ins = pe.matmul(bank[:, 4, 0:D], zT[q][:, c, :], qkv_w[:, c, 0:D], start=False,
                                        stop=(c == KC - 1))
                    ins.then_inc(m_qkv, 1)
                k = s.back(5)
                if k.within(EC):
                    pe.wait_ge(m_msg, k.value(1))
                    pe.wait_ge(m_eq, k.value(1))
                    if k.past(1):
                        pe.wait_ge(m_ST, k.value(0))
                    for c in range(KC):
                        ins = pe.matmul(bank[:, 5, c * P:(c + 1) * P], MSG[k.slot(2)][:, c * P:(c + 1) * P],
                                        EQ[k.slot(2)][:, :], start=True, stop=True)
                    ins.then_inc(m_S, 1)
                k = s.back(6)
                if k.within(EC):
                    pe.wait_ge(m_ST, k.value(1))
                    if k.past(1):
                        pe.wait_ge(m_UB, k.value(0))
                    for c in range(KC):
                        ins = pe.matmul(bank[:, 6, 0:D], ST[k.slot(2)][:, c, :], wo_t[:, c, :], start=(c == 0),
                                        stop=(c == KC - 1))
                    ins.then_inc(m_U, 1)

            run_steps(pe, EC, 6, 4, 4, messages)

            def messages2(s):
                k = s.back(1)
                if k.within(EC):
                    q = k.slot(2)
                    pe.wait_ge(n_en, k.value(1))
                    pe.wait_ge(n_h, k.value(1))
                    if k.past(2):
                        pe.wait_ge(n_UB, k.value(-1))
                    pe.matmul(bank[:, q, 0:D], EN[q][:, :], H1e[q][:, :], start=True, stop=True).then_inc(n_U, 1)

            run_steps(pe, EC, 1, 4, 4, messages2)

            def nodes(s):
                k = s.back(3)
                if k.within(NG):
                    pe.wait_ge(g_ag, k.value(1))
                    if k.past(1):
                        pe.wait_ge(g_hT, k.value(0))
                    for c in range(KC):
                        for j in range(G):
                            ins = pe.transpose(bank[:, c, j * P:(j + 1) * P],
                                               AG[k.slot(2)][:, j * D + c * P:j * D + (c + 1) * P], identity[:, :])
                    ins.then_inc(g_T, 1)
                k = s.back(4)
                if k.within(NG):
                    pe.wait_ge(g_hT, k.value(1))
                    if k.past(1):
                        pe.wait_ge(g_rT, k.value(0))
                    for m in range(KC):
                        for c in range(KC):
                            ins = pe.matmul(bank[:, 2 + m, :], w01[:, c, m * P:(m + 1) * P],
                                            hT[k.slot(2)][:, c * GN:(c + 1) * GN], start=(c == 0),
                                            stop=(c == KC - 1))
                    ins.then_inc(g_m1, 1)
                k = s.back(5)
                if k.within(NG):
                    pe.wait_ge(g_rT, k.value(1))
                    if k.past(1):
                        pe.wait_ge(g_fin, k.value(0))
                    for j in range(G):
                        to = bank[:, 4 + j // 2, (j % 2) * D:(j % 2 + 1) * D]
                        pe.matmul(to, ones3[:, :], bias3[:, 3 * D:], start=True, stop=False)
                        for c in range(KC):
                            ins = pe.matmul(to, rT[k.slot(2)][:, c * GN + j * P:c * GN + (j + 1) * P], w2_sb[:, c, :],
                                            start=False, stop=(c == KC - 1))
                    ins.then_inc(g_m2, 1)

            run_steps(pe, NG, 5, 6, 6, nodes)


_INS = ['x', 'src', 'dst', 'edge_attr_64', 'edge_weight', 'L0_gnn_ln_g', 'L0_gnn_ln_b', 'L0_gnn_Wq', 'L0_gnn_bq',
        'L0_gnn_Wk', 'L0_gnn_bk', 'L0_gnn_Wv', 'L0_gnn_bv', 'L0_gnn_Wo', 'L0_gnn_bo', 'L0_gnn_Wdk', 'L0_gnn_bdk',
        'L0_gnn_Wdv', 'L0_gnn_bdv', 'L1_gnn_W', 'L1_gnn_b', 'L1_gnn_W1', 'L1_gnn_b1', 'L1_gnn_W2', 'L1_gnn_b2']


def kernel(**inputs):
    import numpy as np
    import concourse.bacc as bacc
    from concourse.bass_utils import run_bass_kernel_spmd

    nc = bacc.Bacc("TRN2", target_bir_lowering=False, num_devices=1)
    arrays, args = {}, []
    for name in _INS:
        a = np.ascontiguousarray(inputs[name])
        arrays[f"in_{name}_dram"] = a
        args.append(nc.dram_tensor(f"in_{name}_dram", a.shape, mybir.dt.from_np(a.dtype), kind="ExternalInput").ap())
    args.append(nc.dram_tensor("out_0_dram", (N, D), F32, kind="ExternalOutput").ap())
    build(nc, *args)
    r = run_bass_kernel_spmd(nc, [arrays], core_ids=[0])
    return r.results[0]["out_0_dram"]
```

```python
from contextlib import ExitStack

import concourse.bass as bass
from concourse import mybir

P = 128
D = 256
R = 64
N = 50000
E = 12500
KC = D // P
EC = -(-E // P)
ET = E - (EC - 1) * P
G = 4
GN = G * P
NG = -(-N // GN)
GT = (N - (NG - 1) * GN) // G
COLS = NG * G
SLOTS = -(-2 * E // P) * P
SPARE = 8
IDLE0 = SLOTS
DUMP0 = IDLE0 + SPARE * P
MESSAGE_STEPS = 11
PAIR_STEPS = 5
NODE_STEPS = 9
EP = EC // 2
FILL = 4
ROWS = -(-(DUMP0 + P) // (FILL * P)) * FILL * P
CUTOFF = 5.0
EPS = 1e-5
PI = 3.14159265358979

F32 = mybir.dt.float32
BF16 = mybir.dt.bfloat16
F16 = mybir.dt.float16
I32 = mybir.dt.int32
ALU = mybir.AluOpType
ACT = mybir.ActivationFunctionType


class Step:

    def __init__(self, off, reg=None, unroll=1):
        self.off, self.reg, self.unroll = off, reg, unroll

    def back(self, n):
        return Step(self.off - n, self.reg, self.unroll)

    def within(self, count):
        return self.reg is not None or 0 <= self.off < count

    def past(self, n):
        return self.reg is not None or self.off >= n

    def value(self, add=0, times=1):
        if self.reg is None:
            return (self.off + add) * times
        return self.reg * (self.unroll * times) + (self.off + add) * times

    def slot(self, ring):
        return self.off % ring

    def pair(self):
        return self.off // 2 % 2

    def turns(self, ring, times=16, add=1):
        if self.reg is None:
            return times * (self.off // ring + add)
        return self.reg * (times * (self.unroll // ring)) + times * (self.off // ring + add)


def run_steps(eng, count, depth, unroll, warm, body):
    first = -(-(depth + warm) // unroll)
    last = (count - 1) // unroll
    for s in range(first * unroll):
        body(Step(s))
    with eng.Fori(first, last) as reg:
        for u in range(unroll):
            body(Step(u, reg, unroll))
    for s in range(last * unroll, count + depth):
        body(Step(s))


def build(nc, x, src, dst, edge_attr, edge_weight, ln_g, ln_b, Wq, bq, Wk, bk, Wv, bv, Wo, bo,
          Wdk, bdk, Wdv, bdv, W, b, W1, b1, W2, b2, out):
    ctx = ExitStack()
    with ctx:
        def sb(name, shape, dt=F32):
            return ctx.enter_context(nc.sbuf_tensor(name, shape, dt))

        def ring(name, n, shape, dt=F32):
            return [sb(f"{name}{i}", shape, dt) for i in range(n)]

        def sem(name):
            return ctx.enter_context(nc.semaphore(name))

        def sems(name, n):
            return [sem(f"{name}_{i}") for i in range(n)]

        sums = nc.dram_tensor("sums_dram", (ROWS, 2 * D), F32).ap()
        halves = sums.rearrange("r (h d) -> (r h) d", h=2)
        table = nc.dram_tensor("table_dram", (P * COLS, 2), F32).ap()

        bank = ctx.enter_context(nc.psum_tensor("bank", [P, 8, 512], F32))

        identity = sb("identity", [P, P])
        before = sb("before", [P, 2 * P])
        lower = before[:, P:]
        upper = sb("upper", [P, P])
        ones = sb("ones", [P, P])
        ones3 = sb("ones3", [3, P], BF16)
        leave3 = sb("leave3", [3, 2])
        minus_half = sb("minus_half", [P, 2 * G])
        half_pi = sb("half_pi", [P, 1])

        kept = sb("kept", [P, EC, D])
        room = kept[:, :, :].rearrange("p c d -> p (c d)")
        early, late = [0], [0]

        def place(taken, shape, dt=F32):
            width = 1
            for n in shape[1:]:
                width *= n
            words = width // 2 if dt in (BF16, F16) else width
            at0 = taken[0]
            taken[0] += words
            assert taken[0] <= EC * D
            view = room[0:shape[0], at0:at0 + words]
            if dt != F32:
                view = view.bitcast(dt)
            names = "abc"[:len(shape) - 1]
            if len(names) > 1:
                view = view.rearrange(f"p ({' '.join(names)}) -> p {' '.join(names)}",
                                      **dict(zip(names, shape[1:])))
            return view

        def temp(shape, dt=F32):
            return place(early, shape, dt)

        w_raw = temp([P, 5, KC, D])
        wd_raw = temp([P, 2, KC, R])
        wq_t = temp([P, 3, KC, D])
        qkv_w = sb("qkv_w", [P, KC, 3 * D])
        wo_t = sb("wo_t", [P, KC, D])
        w_t = temp([P, KC, D])
        wd_t = sb("wd_t", [R + 1, 2 * D])
        w1_raw = temp([P, KC, D])
        w01 = sb("w01", [P, KC, D])
        w2_sb = sb("w2_sb", [P, KC, D])
        g_col = sb("g_col", [P, KC])
        b_col = sb("b_col", [P, KC])
        b0_col = sb("b0_col", [P, KC])
        b1_col = sb("b1_col", [P, KC])
        b01_col = sb("b01_col", [P, KC])
        rows3 = temp([3, 4 * D])
        part3 = temp([3, 4 * D])
        piece = temp([3, 4 * D], BF16)
        bias3 = sb("bias3", [3, 4 * D], BF16)

        e_rows = temp([EC, 3, P])
        e_rowf = temp([EC, 2, P])
        src_f = sb("src_f", [P, EC])
        dst_f = sb("dst_f", [P, EC])
        ew_f = sb("ew_f", [P, EC])
        look = sb("look", [P, EC, 4], I32)
        node_i, at_i = look[:, :, 0:2], look[:, :, 2:4]
        key_i = temp([P, EC, 2], I32)
        key_j = temp([P, EC, 2], I32)
        pkey = temp([P, EC, 2])
        ckey = temp([P, EC, 2])
        valid = sb("valid", [P, EC])
        edge_no = temp([P, EC], I32)
        away = temp([P, EC])
        cut = sb("cut", [P, EC])
        ew_part = temp([P, EC, 3])
        ew_low = [temp([P, EC], BF16) for _ in range(3)]
        ends_d = sb("ends_d", [P, EC, 2])
        dump_f = sb("dump_f", [P, 1])
        dump2_f = sb("dump2_f", [P, 1])
        dump_i = sb("dump_i", [P, 1], I32)

        iota_c = temp([P, COLS], F16)
        iota_p = temp([P, P], F16)
        iota_i = temp([P, COLS], I32)
        touched = temp([P, COLS])
        running = temp([P, COLS])
        idle_f = temp([P, COLS])
        idle_i = temp([P, COLS], I32)
        slot_i = sb("slot_i", [P, COLS], I32)
        pair_f = temp([P, COLS, 2])
        deg1 = temp([P, COLS])
        root = temp([P, COLS])
        turn = temp([P, COLS])
        dinv2 = sb("dinv2", [P, COLS])
        base = sb("base", [P, 1])
        hot_p = [temp([P, 5, P], BF16) for _ in range(2)]
        hot_c = [temp([P, 2, COLS], BF16) for _ in range(2)]
        ew_now = [temp([P, 3]) for _ in range(2)]


        s_ld, s_ldw, s_rows = sem("s_ld"), sem("s_ldw"), sem("s_rows")
        s_const, s_dve, s_pre_pe = sem("s_const"), sem("s_dve"), sem("s_pre_pe")
        s_fill, s_table = sem("s_fill"), sem("s_table")
        s_hot, s_hotw, s_hotmm, s_pass = sem("s_hot"), sem("s_hotw"), sem("s_hotmm"), sem("s_pass")
        s_fillrow, s_tab_sb, s_cos, s_zero = sem("s_fillrow"), sem("s_tab_sb"), sem("s_cos"), sem("s_zero")
        s_deg, s_rsq = sem("s_deg"), sem("s_rsq")
        s_endsf, s_scan, s_turned, s_ready = sem("s_endsf"), sem("s_scan"), sem("s_turned"), sem("s_ready")

        CG = ring("cg_", 3, [P, G, 2 * D])
        fill_row = CG[0]

        X2 = [CG[1][:, i, :].rearrange("p (a d) -> p a d", a=2) for i in range(4)]
        H2 = [CG[2][:, i, :].rearrange("p (a d) -> p a d", a=2) for i in range(4)]
        Z2 = ring("z2_", 2, [P, 2, D])
        ib = ring("ib_", 2, [P, 2, 4], I32)
        attr = ring("attr_", 4, [P, R])
        row_d = ring("row_d_", 4, [P, P], I32)
        st = ring("st_", 2, [P, 4, 6])
        mv = ring("mv_", 2, [P, 4, 2])
        ve = ring("ve_", 2, [P, 4, 1])
        rs = ring("rs_", 2, [P, 4, 1])
        nb = ring("nb_", 2, [P, 4, 1])
        zT = ring("zT_", 2, [P, 2 * KC, P])
        aT = ring("aT_", 2, [R + 1, P])
        DS = ring("ds_", 2, [P, 2 * D])
        KD = ring("kd_", 2, [P, D])
        junk = sb("junk", [P, D])
        junk_e = sb("junk_e", [P, P])
        at = ring("at_", 2, [P, 1])
        sa = ring("sa_", 2, [P, 1])
        aa = ring("aa_", 2, [P, 1])
        EQ = ring("eq_", 2, [P, P])
        MSG = ring("msg_", 2, [P, D])
        ST = ring("stt_", 2, [P, KC, P])
        UB4 = sb("ub4", [P, 4, D])
        UB = [UB4[:, i, :] for i in range(4)]
        tab_d = ring("tab_d_", 2, [P, 2, 2])
        cnt = ring("cnt_", 2, [P, 2])
        dif = ring("dif_", 2, [P, 2])
        fst = ring("fst_", 2, [P, 2])
        sidx = ring("sidx_", 2, [P, 2], I32)
        m_ib, m_row, m_attr = sem("m_ib"), sems("m_row", 4), sems("m_attr", 4)
        m_x, m_tab = sems("m_x", 4), sems("m_tab", 2)
        (m_st, m_mv, m_ve, m_rs, m_nb, m_h, m_z, m_xh, m_T, m_zT, m_aT, m_D, m_qkv, m_ds, m_kd, m_at, m_sa, m_aa,
         m_eq, m_cnt, m_dif, m_fst, m_idx, m_msg, m_S, m_ST, m_U, m_UB, m_keep) = [
            sem("m_" + n) for n in ("st mv ve rs nb h z xh T zT aT D qkv ds kd at sa aa eq cnt dif fst idx msg S ST U "
                                    "UB keep").split()]
        m_sc = sem("m_sc")

        def halved(t, i):
            return t[:, 2 * i:2 * i + 2, :].rearrange("p a d -> p (a d)").rearrange("p (a d) -> p a d", a=4)

        C0 = [halved(CG[1], i)[:, 0:2, :] for i in range(2)]
        X1e = [halved(CG[1], i)[:, 2:4, :] for i in range(2)]
        H1e = [halved(CG[2], i)[:, 0:2, :] for i in range(2)]
        EQ2 = [halved(CG[2], i)[:, 2:4, :] for i in range(2)]
        EN = ring("en_", 2, [P, 2, 2 * P])
        sidx2 = ring("sidx2_", 4, [P, 2], I32)
        ic = ring("ic_", 2, [P, 2, 2], I32)
        row_s = ring("row_s_", 2, [P, 2 * P], I32)
        tab_s = ring("tab_s_", 2, [P, 2, 2])
        nr = ring("nr_", 2, [P, 2])
        nr2 = ring("nr2_", 2, [P, 2])
        cnt2 = ring("cnt2_", 2, [P, 2])
        dif2 = ring("dif2_", 2, [P, 2])
        fst2 = ring("fst2_", 4, [P, 2])
        n_ic, n_row, n_c0, n_tab, n_sc = sem("n_ic"), sems("n_row", 2), sems("n_c0", 2), sems("n_tab", 2), sem("n_sc")
        (n_x1, n_st, n_mv, n_ve, n_rs, n_nb, n_h, n_eq, n_cnt, n_nr, n_nr2, n_en, n_fst, n_dif, n_idx, n_U, n_UB) = [
            sem("n_" + n) for n in "x1 st mv ve rs nb h eq cnt nr nr2 en fst dif idx U UB".split()]

        def part(width):
            return place(late, [P, width])

        X = [part(G * D) for _ in range(4)]
        X1 = [part(G * D) for _ in range(8)]
        H = [part(G * D) for _ in range(2)]
        H1 = [part(G * D) for _ in range(2)]
        AG = [part(G * D) for _ in range(2)]
        hT = [part(KC * GN) for _ in range(2)]
        rT = [part(KC * GN) for _ in range(2)]
        CG = CG + [part(2 * G * D).rearrange("p (j d) -> p j d", j=G)]
        bi = ring("bi_", 2, [P, 2 * G], I32)
        b_st = ring("b_st_", 2, [P, 2 * G, 6])
        b_mv = ring("b_mv_", 2, [P, 2 * G, 2])
        b_ve, b_rs, b_nb = (ring(f"b_{n}_", 2, [P, 2 * G, 1]) for n in ("ve", "rs", "nb"))
        g_x, g_cg, g_out = sems("g_x", 4), sems("g_cg", 4), sems("g_out", 8)
        (g_bi, g_st, g_mv, g_ve, g_rs, g_rsd, g_nb, g_h, g_xh, g_x1, g_h1, g_ag, g_T, g_hT, g_m1, g_rT, g_m2, g_fin) = [
            sem("g_" + n) for n in "bi st mv ve rs rsd nb h xh x1 h1 ag T hT m1 rT m2 fin".split()]
        s_end2 = sem("s_end2")

        def pass_on(eng, *waits):
            for s, v in waits:
                eng.wait_ge(s, v)
            if not all(isinstance(v, int) for _, v in waits):
                eng.sem_inc(s_pass)

        block = ctx.enter_context(nc.Block())

        @block.sync
        def _(sp):
            sp.wait_ge(s_zero, 1)
            full = (EC - 1) * P
            for i, t in enumerate((src, dst, edge_weight)):
                to = e_rows[:, i, :] if t.dtype == F32 else e_rows[:, i, :].bitcast(I32)
                sp.dma_start(to[0:EC - 1, :], t[0:full].rearrange("(c p) -> c p", p=P)).then_inc(s_rows, 16)
                sp.dma_start(to[EC - 1:EC, 0:ET], t[full:E].rearrange("(c p) -> c p", c=1)).then_inc(s_rows, 16)
            for i, w in enumerate((Wq, Wk, Wv, Wo, W)):
                sp.dma_start(w_raw[:, i, :, :], w.rearrange("(c p) k -> p c k", p=P)).then_inc(s_ldw, 16)
            for i, w in enumerate((Wdk, Wdv)):
                sp.dma_start(wd_raw[:, i, :, :], w.rearrange("(c p) k -> p c k", p=P)).then_inc(s_ldw, 16)
            sp.dma_start(w1_raw[:, :, :], W1.rearrange("(c p) k -> p c k", p=P)).then_inc(s_ldw, 16)
            sp.dma_start(w2_sb[:, :, :], W2.rearrange("(c p) k -> p c k", p=P)).then_inc(s_ldw, 16)
            with nc.allow_non_contiguous_dma(reason="256 numbers, one a partition"):
                for t, v in ((g_col, ln_g), (b_col, ln_b), (b0_col, b), (b1_col, b1)):
                    sp.dma_start(t[:, :], v.rearrange("(c p) -> p c", p=P)).then_inc(s_ldw, 16)
            for i, v in enumerate((bq, bk, bv, b2)):
                sp.dma_start(rows3[:, i * D:(i + 1) * D],
                             v.rearrange("(a d) -> a d", a=1).broadcast_to([3, D])).then_inc(s_ldw, 16)
            for i, v in enumerate((bdk, bdv)):
                sp.dma_start(wd_t[R:R + 1, i * D:(i + 1) * D], v.rearrange("(a d) -> a d", a=1)).then_inc(s_ldw, 16)
            sp.wait_ge(s_zero, 2)
            for r in range(FILL):
                sp.dma_start(fill_row[:, r, 0:D],
                             bo.rearrange("(a d) -> a d", a=1).broadcast_to([P, D])).then_inc(s_fillrow, 16)
            sp.wait_ge(s_fillrow, 16 * FILL)
            to = sums.rearrange("(p k r) d -> p k (r d)", p=P, r=FILL)
            for k in range(ROWS // (FILL * P)):
                sp.dma_start(to[:, k, :], fill_row[:, :, :].rearrange("p r d -> p (r d)")).then_inc(s_fill, 16)

            sp.wait_ge(s_tab_sb, 1)
            sp.dma_start(table.rearrange("(p c) k -> p (c k)", p=P),
                         pair_f[:, :, :].rearrange("p c k -> p (c k)")).then_inc(s_table, 16)

            def load_edges(s):
                k = s
                if k.within(EC):
                    n = k.off if k.reg is None else None
                    rows = ET if n == EC - 1 else P
                    if k.past(4):
                        pass_on(sp, (m_T, k.value(-3)))
                    sp.dma_start(attr[k.slot(4)][0:rows, :],
                                 edge_attr[bass.ds(k.value(0, P), rows), :]).then_inc(m_attr[k.slot(4)], 16)
                    if k.past(4):
                        pass_on(sp, (m_eq, k.value(-3)))
                    sp.dma_start(row_d[k.slot(4)][:, 0:rows],
                                 dst[bass.ds(k.value(0, P), rows)].rearrange("(a e) -> a e", a=1)
                                 .broadcast_to([P, rows])).then_inc(m_row[k.slot(4)], 16)

            run_steps(sp, EC, 0, 4, 4, load_edges)

            def load_src(s):
                k = s
                if k.within(EP):
                    rows = E - (EP - 1) * 2 * P if k.reg is None and k.off == EP - 1 else 2 * P
                    if k.past(2):
                        pass_on(sp, (n_eq, k.value(-1)))
                    sp.dma_start(row_s[k.slot(2)][:, 0:rows],
                                 src[bass.ds(k.value(0, 2 * P), rows)].rearrange("(a e) -> a e", a=1)
                                 .broadcast_to([P, rows])).then_inc(n_row[k.slot(2)], 16)

            run_steps(sp, EP, 0, 4, 4, load_src)

            sp.wait_ge(s_end2, 1)
            STORE = NODE_STEPS + 1

            def nodes(s):
                k = s
                if k.within(NG):
                    parts = GT if k.reg is None and k.off == NG - 1 else P
                    if k.past(4):
                        pass_on(sp, (g_xh, k.value(-3)))
                    sp.dma_start(X[k.slot(4)][0:parts, :],
                                 x[bass.ds(k.value(0, GN), parts * G), :].rearrange("(p j) d -> p (j d)", j=G)
                                 ).then_inc(g_x[k.slot(4)], 16)
                k = s.back(STORE)
                if k.within(NG):
                    parts = GT if k.reg is None and k.off == NG - 1 else P
                    pass_on(sp, (g_fin, k.value(1)))
                    sp.dma_start(out[bass.ds(k.value(0, GN), parts * G), :].rearrange("(p j) d -> p (j d)", j=G),
                                 X1[k.slot(8)][0:parts, :]).then_inc(g_out[k.slot(8)], 16)

            run_steps(sp, NG, STORE + 1, 8, 4, nodes)
            for q in range(8):
                sp.wait_ge(g_out[q], 16 * ((NG - q + 7) // 8))

        @block.gpsimd
        def _(pool):
            c = [0]

            def link(ins):
                c[0] += 1
                ins.then_inc(s_const, 1)
                pool.wait_ge(s_const, c[0])

            link(pool.memset(ones[:, :], 1.0))
            link(pool.memset(before[:, 0:P], 1.0))
            link(pool.affine_select(out=identity[:, :], in_=ones[:, :], compare_op=ALU.is_equal, fill=0.0,
                                    base=0, pattern=[[-1, P]], channel_multiplier=1))
            link(pool.affine_select(out=lower, in_=ones[:, :], compare_op=ALU.is_gt, fill=0.0,
                                    base=0, pattern=[[-1, P]], channel_multiplier=1))
            link(pool.affine_select(out=upper[:, :], in_=ones[:, :], compare_op=ALU.is_gt, fill=0.0,
                                    base=0, pattern=[[1, P]], channel_multiplier=-1))
            link(pool.iota(edge_no[:, :], [[P, EC]], base=0, channel_multiplier=1))
            link(pool.iota(iota_i[:, :], [[1, COLS]], base=0, channel_multiplier=0))
            link(pool.iota(idle_i[:, :], [[0, COLS // SPARE], [1, SPARE]], base=IDLE0, channel_multiplier=SPARE))
            link(pool.iota(dump_i[:, :], [[0, 1]], base=2 * DUMP0, channel_multiplier=2))
            link(pool.memset(minus_half[:, :], -0.5))
            last_node = pool.to_reg(N - 1)
            last_half = pool.to_reg(2 * ROWS - 1)
            last_row = pool.to_reg(ROWS - 1)
            last_entry = pool.to_reg(P * COLS - 1)

            def inv_sqrt(var, to, ready, done, k):
                width = var.shape[1]
                pool.wait_ge(ready, k.value(1))
                pool.tensor_tensor(to, var, minus_half[:, 0:width].rearrange("p (a b) -> p a b", b=1),
                                   ALU.pow).then_inc(done, 1)

            def scatter_add(idx, rows, done):
                pool.indirect_dma_start(halves, bass.IndirectOffsetOnAxis(idx, 0), rows, None,
                                        bounds_check=last_half, compute_op=ALU.add).then_inc(done, 16)

            def gather(to, table, idx, bound, done):
                pool.indirect_dma_start(to, None, table, bass.IndirectOffsetOnAxis(idx, 0), bounds_check=bound,
                                        oob_is_err=True).then_inc(done, 16)

            def messages(s):
                k = s
                pair, half = k.pair(), k.slot(2)
                if k.within(EC):
                    w = []
                    if half == 0:
                        w.append((m_ib, k.turns(2, 1)))
                        if k.past(4):
                            w.append((m_keep, k.turns(2, 1, -1)))
                    if k.past(4):
                        w.append((m_xh, k.value(-3)))
                    pass_on(pool, *w)
                    for i in range(2):
                        gather(X2[k.slot(4)][:, i, :], x, ib[pair][:, half, i:i + 1], last_node, m_x[k.slot(4)])
                u = s.back(1)
                if u.within(EC + 2):
                    inv_sqrt(ve[u.slot(2)][:, :, :], rs[u.slot(2)][:, :, :], m_ve, m_rs, u)
                if k.within(EC):
                    if not k.past(1):
                        pool.wait_ge(s_table, 16)
                    gather(tab_d[pair][:, half, :], table, ib[pair][:, half, 2:3], last_entry, m_tab[pair])
                k = s.back(11)
                if k.within(EC):
                    w = [(m_UB, k.value(1)), (m_idx, k.turns(2, 1))]
                    if k.past(1):
                        w.append((m_sc, k.value(0, 16)))
                    else:
                        w.append((s_fill, 16 * (ROWS // (FILL * P))))
                    pass_on(pool, *w)
                    scatter_add(sidx[k.pair()][:, k.slot(2):k.slot(2) + 1], UB[k.slot(4)], m_sc)

            run_steps(pool, EC, MESSAGE_STEPS, 4, 4, messages)
            pool.wait_ge(m_sc, 16 * EC)

            def messages2(s):
                k = s
                q = k.slot(2)
                if k.within(EP):
                    w = [(n_ic, k.value(1))]
                    if k.past(2):
                        w += [(n_x1, k.value(-1)), (n_nr, k.value(-1)), (n_dif, k.value(-1))]
                    pass_on(pool, *w)
                    for i in range(2):
                        gather(C0[q][:, i, :], halves, ic[q][:, i, 0:1], last_half, n_c0[q])
                    for i in range(2):
                        gather(tab_s[q][:, i, :], table, ic[q][:, i, 1:2], last_entry, n_tab[q])
                k = s.back(1)
                if k.within(EP):
                    inv_sqrt(ve[k.slot(2)][:, 0:2, :], rs[k.slot(2)][:, 0:2, :], n_ve, n_rs, k)
                k = s.back(5)
                if k.within(EP):
                    w = [(n_UB, k.value(1)), (n_idx, k.value(1))]
                    if k.past(1):
                        w.append((n_sc, k.value(0, 32)))
                    pass_on(pool, *w)
                    for i in range(2):
                        scatter_add(sidx2[k.slot(4)][:, i:i + 1], UB[2 * k.slot(2) + i], n_sc)

            run_steps(pool, EP, PAIR_STEPS, 4, 4, messages2)
            pool.wait_ge(n_sc, 32 * EP)

            def nodes(s):
                k = s.back(1)
                if k.within(NG):
                    w = []
                    if k.slot(2) == 0:
                        w.append((g_bi, k.turns(2, 1)))
                    if k.past(4):
                        w.append((g_ag, k.value(-3)))
                    pass_on(pool, *w)
                    for j in range(G):
                        at0 = k.slot(2) * G + j
                        gather(CG[k.slot(4)][:, j, :], sums, bi[k.pair()][:, at0:at0 + 1], last_row,
                               g_cg[k.slot(4)])
                k = s
                if k.within(NG + 2):
                    inv_sqrt(b_ve[k.slot(2)][:, :, :], b_rs[k.slot(2)][:, :, :], g_ve, g_rs, k)

            run_steps(pool, NG, NODE_STEPS, 8, 4, nodes)

        @block.vector
        def _(dve):
            c = [0]

            def link(ins):
                c[0] += 1
                ins.then_inc(s_dve, 1)
                dve.wait_ge(s_dve, c[0])

            dve.memset(e_rows[:, :, :], 0.0).then_inc(s_zero, 1)
            dve.memset(fill_row[:, :, :], 0.0).then_inc(s_zero, 1)
            link(dve.memset(half_pi[:, :], PI / 2))
            link(dve.memset(ones3[:, :], 1.0))
            dve.wait_ge(s_const, 10)
            link(dve.tensor_copy(iota_c[:, :], iota_i[:, :]))
            link(dve.tensor_copy(iota_p[:, :], iota_i[:, 0:P]))
            link(dve.tensor_copy(idle_f[:, :], idle_i[:, :]))
            link(dve.tensor_copy(dump_f[:, :], dump_i[:, :]))
            link(dve.tensor_scalar(dump2_f[:, :], dump_f[:, :], 1.0, None, ALU.add))
            link(dve.tensor_scalar(valid[:, :], edge_no[:, :], float(E), None, ALU.is_lt))
            link(dve.tensor_scalar(leave3[:, :], before[0:3, P:P + 2], -1.0, None, ALU.mult))
            for i in range(2):
                link(dve.memset(aT[i][R:R + 1, :], 1.0))
            for i in range(4):
                link(dve.memset(attr[i][:, :], 0.0))
                link(dve.memset(row_d[i][:, :], 0))

            for i in range(2):
                link(dve.memset(row_s[i][:, :], 0))

            dve.wait_ge(s_rows, 96)
            dve.tensor_copy(e_rowf[:, :, :], e_rows[:, 0:2, :].bitcast(I32)).then_inc(s_endsf, 1)
            dve.wait_ge(s_pre_pe, 1)
            for i, t in enumerate((src_f, dst_f, ew_f)):
                link(dve.tensor_copy(t[:, :], bank[:, 0, i * P:i * P + EC]))
            link(dve.tensor_copy(node_i[:, :, 0], dst_f[:, :]))
            link(dve.tensor_copy(node_i[:, :, 1], src_f[:, :]))
            link(dve.tensor_scalar(key_i[:, :, :], node_i[:, :, :], 2, P - 1, ALU.logical_shift_right,
                                   ALU.bitwise_and))
            link(dve.tensor_copy(pkey[:, :, :], key_i[:, :, :]))
            link(dve.tensor_scalar(key_i[:, :, :], node_i[:, :, :], 9, 2, ALU.logical_shift_right,
                                   ALU.logical_shift_left))
            link(dve.tensor_scalar(key_j[:, :, :], node_i[:, :, :], G - 1, None, ALU.bitwise_and))
            link(dve.tensor_tensor(ckey[:, :, :], key_i[:, :, :], key_j[:, :, :], ALU.add))
            link(dve.scalar_tensor_tensor(at_i[:, :, :], pkey[:, :, :], float(COLS), ckey[:, :, :], ALU.mult, ALU.add))
            link(dve.tensor_scalar(away[:, :], valid[:, :], -1000.0, 1000.0, ALU.mult, ALU.add))
            for i in range(2):
                link(dve.tensor_tensor(pkey[:, :, i], pkey[:, :, i], away[:, :], ALU.add))
            dve.tensor_copy(ib[0][:, :, :], look[:, 0:2, :]).then_inc(m_ib, 1)
            link(dve.tensor_copy(ew_low[0][:, :], ew_f[:, :]))
            link(dve.tensor_copy(ew_part[:, :, 0], ew_low[0][:, :]))
            link(dve.tensor_tensor(ew_part[:, :, 2], ew_f[:, :], ew_part[:, :, 0], ALU.subtract))
            link(dve.tensor_copy(ew_low[1][:, :], ew_part[:, :, 2]))
            link(dve.tensor_copy(ew_part[:, :, 1], ew_low[1][:, :]))
            link(dve.tensor_tensor(ew_part[:, :, 2], ew_part[:, :, 2], ew_part[:, :, 1], ALU.subtract))

            link(dve.tensor_scalar(away[:, :], ew_f[:, :], -1.0, None, ALU.mult))
            link(dve.tensor_tensor(away[:, :], away[:, :], ew_f[:, :], ALU.max))
            link(dve.tensor_scalar(cut[:, :], away[:, :], PI / CUTOFF, None, ALU.mult))
            dve.tensor_scalar(cut[:, :], cut[:, :], PI, None, ALU.min).then_inc(s_cos, 1)
            dve.wait_ge(s_cos, 2)
            link(dve.tensor_scalar(cut[:, :], cut[:, :], 0.5, 0.5, ALU.mult, ALU.add))
            link(dve.tensor_scalar(away[:, :], ew_f[:, :], CUTOFF, None, ALU.is_lt))
            link(dve.tensor_tensor(cut[:, :], cut[:, :], away[:, :], ALU.mult))
            link(dve.tensor_tensor(cut[:, :], cut[:, :], valid[:, :], ALU.mult))

            def col(t, k, i=None):
                if i is not None:
                    return t[:, bass.ds(k.value(0), 1), i]
                at0 = t[:, bass.ds(k.value(0), 1)]
                return at0 if len(t.shape) == 2 else at0.rearrange("p a b -> p (a b)")

            def hot(s):
                k = s
                q = k.slot(2)
                if k.past(2):
                    dve.wait_ge(s_hotmm, k.value(-1))
                for i in (1, 0):
                    dve.tensor_scalar(hot_p[q][:, i, :], iota_p[:, :], col(pkey, k, i), None, ALU.is_equal)
                    if i == 1:
                        dve.tensor_copy(ew_now[q][:, :], ew_part[:, bass.ds(k.value(0), 1), :]
                                        .rearrange("p a b -> p (a b)")).then_inc(s_hot, 1)
                    ins = dve.tensor_scalar(hot_c[q][:, i, :], iota_c[:, :], col(ckey, k, i), None, ALU.is_equal)
                ins.then_inc(s_hot, 1)

            run_steps(dve, EC, 0, 2, 2, hot)

            dve.wait_ge(s_hotmm, EC)
            link(dve.tensor_scalar(touched[:, :], bank[:, 1, 0:COLS], 1.0, None, ALU.min))
            link(dve.tensor_scalar(deg1[:, :], bank[:, 2, 0:COLS], 1.0, None, ALU.add))
            link(dve.tensor_scalar(dinv2[:, :], deg1[:, :], 0.0, None, ALU.is_gt))
            dve.tensor_scalar(deg1[:, :], deg1[:, :], 1e-30, None, ALU.max).then_inc(s_deg, 1)
            dve.tensor_tensor_scan(running[:, :], ones[:, 0:1].broadcast_to([P, COLS]), touched[:, :], 0.0,
                                   ALU.mult, ALU.add).then_inc(s_scan, 1)
            dve.wait_ge(s_pre_pe, 8)
            link(dve.tensor_scalar(base[:, :], bank[:, 3, 0:1], -1.0, None, ALU.add))
            link(dve.scalar_tensor_tensor(running[:, :], running[:, :], base[:, :], idle_f[:, :], ALU.add,
                                          ALU.subtract))
            link(dve.tensor_tensor(running[:, :], running[:, :], touched[:, :], ALU.mult))
            link(dve.tensor_tensor(running[:, :], running[:, :], idle_f[:, :], ALU.add))
            link(dve.tensor_copy(slot_i[:, :], running[:, :]))
            link(dve.tensor_scalar(pair_f[:, :, 0], running[:, :], 2.0, None, ALU.mult))
            dve.wait_ge(s_rsq, 1)
            link(dve.reciprocal(root[:, :], root[:, :]))
            link(dve.tensor_tensor(turn[:, :], root[:, :], root[:, :], ALU.mult))
            link(dve.tensor_tensor(turn[:, :], turn[:, :], deg1[:, :], ALU.mult))
            link(dve.tensor_scalar(turn[:, :], turn[:, :], -0.5, 1.5, ALU.mult, ALU.add))
            link(dve.tensor_tensor(root[:, :], root[:, :], turn[:, :], ALU.mult))
            link(dve.tensor_tensor(pair_f[:, :, 1], root[:, :], dinv2[:, :], ALU.mult))
            dve.tensor_tensor(dinv2[:, :], pair_f[:, :, 1], pair_f[:, :, 1], ALU.mult).then_inc(s_tab_sb, 1)
            dve.wait_ge(s_pre_pe, 9)
            link(dve.tensor_copy(part3[:, D * 3:], rows3[:, D * 3:]))
            link(dve.tensor_tensor(part3[:, 0:2 * D], rows3[:, 0:2 * D], bank[0:3, 4, :], ALU.add))
            link(dve.tensor_tensor(part3[:, 2 * D:3 * D], rows3[:, 2 * D:3 * D], bank[0:3, 5, 0:D], ALU.add))
            for i in range(2):
                link(dve.tensor_copy(piece[:, :], part3[:, :]))
                link(dve.scalar_tensor_tensor(part3[:, :], piece[:, :], leave3[:, i:i + 1], part3[:, :], ALU.mult,
                                              ALU.add))
            link(dve.tensor_copy(bias3[:, :], part3[:, :]))
            dve.wait_ge(s_pre_pe, 10)
            link(dve.tensor_copy(w01[:, :, :].rearrange("p k d -> p (k d)"), bank[:, 6, :]))
            dve.tensor_tensor(b01_col[:, :], b1_col[:, :], bank[:, 7, 0:KC], ALU.add).then_inc(s_ready, 1)
            dve.wait_ge(s_table, 16)

            for i in range(2):
                link(dve.memset(mv[i][:, 2:4, :], 0.0))

            def pair_of(t, k, *i):
                return t[(slice(None), bass.ds(k.value(0), 2), *i)]

            def indices(k):
                dve.tensor_copy(ib[k.pair()][:, :, :], pair_of(look, k, slice(None))).then_inc(m_ib, 1)

            def messages(s):
                a, h, t, m, f = s.back(1), s.back(3), s.back(5), s.back(7), s.back(9)
                u, q, v = s.back(1), m.slot(2), s.back(2)
                if v.within(EC + 2):
                    dve.wait_ge(m_rs, v.value(1))
                    dve.scalar_tensor_tensor(nb[v.slot(2)][:, :, :], mv[v.slot(2)][:, :, 0:1], -1.0,
                                             rs[v.slot(2)][:, :, :], ALU.mult, ALU.mult).then_inc(m_nb, 1)
                if m.within(EC):
                    dve.wait_ge(m_qkv, m.value(1))
                    dve.wait_ge(m_ds, m.value(1))
                    dve.tensor_tensor(KD[q][:, :], bank[:, 2 + q, 0:D], DS[q][:, 0:D], ALU.mult).then_inc(m_kd, 1)
                if a.within(EC):
                    dve.wait_ge(m_x[a.slot(4)], a.turns(4, 32))
                    for i in range(2):
                        ins = dve.bn_stats(st[u.slot(2)][:, i, :], X2[a.slot(4)][:, i, :])
                if m.within(EC):
                    dve.wait_ge(m_kd, m.value(1))
                    dve.tensor_tensor_reduce(junk[:, :], bank[:, 4, 0:D], KD[q][:, :], 1.0, 0.0,
                                             ALU.mult, ALU.add, at[q][:, :]).then_inc(m_at, 1)
                if h.within(EC):
                    dve.wait_ge(m_h, h.value(1))
                    for i in range(2):
                        ins = dve.bn_stats(st[u.slot(2)][:, 2 + i, :], H2[h.slot(4)][:, i, :])
                if u.within(EC + 2):
                    ins.then_inc(m_st, 1)
                if m.within(EC):
                    dve.wait_ge(m_row[m.slot(4)], m.turns(4))
                    if m.past(2):
                        dve.wait_ge(m_S, m.value(-1))
                    dve.tensor_scalar(EQ[q][:, :], row_d[m.slot(4)][:, :], col(dst_f, m), None,
                                      ALU.is_equal).then_inc(m_eq, 1)
                if u.within(EC + 2):
                    pass_on(dve, (m_st, u.value(1)))
                    for i in [0, 1] * a.within(EC) + [2, 3] * h.within(EC):
                        ins = dve.bn_aggr(mv[u.slot(2)][:, i, :], st[u.slot(2)][:, i, :])
                    ins.then_inc(m_mv, 1)
                if f.within(EC):
                    dve.wait_ge(m_S, f.value(1))
                    dve.tensor_copy(ST[f.slot(2)][:, :, :].rearrange("p k e -> p (k e)"),
                                    bank[:, 5, 0:KC * P]).then_inc(m_ST, 1)
                if u.within(EC + 2):
                    dve.wait_ge(m_mv, u.value(1))
                    dve.tensor_scalar(ve[u.slot(2)][:, :, :], mv[u.slot(2)][:, :, 1:2], EPS, None,
                                      ALU.add).then_inc(m_ve, 1)
                if m.within(EC):
                    dve.wait_ge(m_sa, m.value(1))
                    dve.tensor_scalar(aa[q][:, :], sa[q][:, :], col(cut, m), None, ALU.mult).then_inc(m_aa, 1)
                    dve.wait_ge(m_eq, m.value(1))
                    dve.tensor_tensor_reduce(junk_e[:, :], EQ[q][:, :], lower, 1.0, 0.0, ALU.mult, ALU.add,
                                             cnt[m.pair()][:, q:q + 1]).then_inc(m_cnt, 1)
                    dve.wait_ge(m_aa, m.value(1))
                    dve.scalar_tensor_tensor(MSG[q][:, :], bank[:, 2 + q, D:2 * D], aa[q][:, 0:1], DS[q][:, D:2 * D],
                                             ALU.mult, ALU.mult).then_inc(m_msg, 1)
                last = f.within(EC) and f.slot(2) == 1
                z, first = f.pair(), f.back(1)
                if last:
                    dve.tensor_scalar(dif[z][:, :], pair_of(ends_d, first, 0), dump_f[:, 0:1], None,
                                      ALU.subtract).then_inc(m_dif, 1)
                if h.within(EC):
                    dve.tensor_tensor(kept[:, bass.ds(h.value(0), 1), :].rearrange("p a d -> p (a d)"),
                                      X2[h.slot(4)][:, 0, :], H2[h.slot(4)][:, 0, :], ALU.add).then_inc(m_xh, 1)
                if last:
                    dve.wait_ge(m_dif, f.turns(2, 1))
                    dve.scalar_tensor_tensor(fst[z][:, :], cnt[z][:, :], 0.5, dif[z][:, :], ALU.is_lt,
                                             ALU.mult).then_inc(m_fst, 1)
                    if f.reg is None and f.off == EC - 1:
                        dve.wait_ge(m_fst, f.turns(2, 1))
                        link(dve.tensor_tensor(fst[z][:, :], fst[z][:, :], pair_of(valid, first), ALU.mult))
                if t.within(EC):
                    dve.wait_ge(m_T, t.value(1))
                    dve.tensor_copy(aT[t.slot(2)][0:R, :], bank[0:R, 7, 0:P]).then_inc(m_aT, 1)
                if last:
                    dve.wait_ge(m_fst, f.turns(2, 1))
                    if f.past(4):
                        dve.wait_ge(m_sc, f.value(-3, 16))
                    dve.tensor_scalar(sidx[z][:, :], fst[z][:, :], dump_f[:, 0:1], None, ALU.add).then_inc(m_idx, 1)
                if a.within(EC) and a.slot(2) == 1:
                    pass_on(dve, (m_tab[a.pair()], a.turns(4, 32)))
                    dve.tensor_copy(pair_of(ends_d, a.back(1), slice(None)), tab_d[a.pair()][:, :, :]
                                    ).then_inc(m_keep, 1)
                n = s.back(-1)
                if n.within(EC) and n.slot(2) == 0:
                    indices(n)

            run_steps(dve, EC, MESSAGE_STEPS, 4, 4, messages)

            dve.wait_ge(m_xh, EC)

            def cols(t, k, *i):
                return t[(slice(None), bass.ds(k.value(0, 2), 2), *i)]

            def ends(k):
                dve.tensor_copy(ic[k.slot(2)][:, :, 0], cols(ends_d, k, 0))
                dve.tensor_copy(ic[k.slot(2)][:, :, 1], cols(look, k, 3)).then_inc(n_ic, 1)

            ends(Step(0))

            def messages2(s):
                v = s.back(2)
                z = v.slot(2)
                if v.within(EP):
                    dve.wait_ge(n_rs, v.value(1))
                    dve.scalar_tensor_tensor(nb[z][:, 0:2, :], mv[z][:, 0:2, 0:1], -1.0,
                                             rs[z][:, 0:2, :], ALU.mult, ALU.mult).then_inc(n_nb, 1)
                a = s.back(1)
                q = a.slot(2)
                if a.within(EP):
                    w = [(n_c0[q], a.turns(2, 32))]
                    if a.past(2):
                        w.append((n_h, a.value(-1)))
                    pass_on(dve, *w)
                    dve.tensor_tensor(X1e[q], cols(kept, a, slice(None)), C0[q], ALU.add).then_inc(n_x1, 1)
                    dve.wait_ge(n_row[q], a.turns(2))
                    for i in range(2):
                        ins = dve.tensor_scalar(EQ2[q][:, i, :], row_s[q][:, :],
                                                src_f[:, bass.ds(a.value(0, 2) + i, 1)], None, ALU.is_equal)
                    ins.then_inc(n_eq, 1)
                    dve.wait_ge(n_x1, a.value(1))
                    for i in range(2):
                        ins = dve.bn_stats(st[q][:, i, :], X1e[q][:, i, :])
                    ins.then_inc(n_st, 1)
                    dve.wait_ge(n_tab[q], a.turns(2, 32))
                    dve.tensor_tensor(nr[q][:, :], tab_s[q][:, :, 1], cols(ew_f, a), ALU.mult).then_inc(n_nr, 1)
                    pass_on(dve, (n_st, a.value(1)))
                    for i in range(2):
                        ins = dve.bn_aggr(mv[q][:, i, :], st[q][:, i, :])
                    ins.then_inc(n_mv, 1)
                    dve.wait_ge(n_nr, a.value(1))
                    dve.tensor_tensor(nr2[q][:, :], nr[q][:, :], cols(ends_d, a, 1), ALU.mult).then_inc(n_nr2, 1)
                    dve.wait_ge(n_mv, a.value(1))
                    dve.tensor_scalar(ve[q][:, 0:2, :], mv[q][:, 0:2, 1:2], EPS, None, ALU.add).then_inc(n_ve, 1)
                    dve.wait_ge(n_eq, a.value(1))
                    dve.tensor_tensor_reduce(junk_e[:, :], EQ2[q][:, 0, 0:P], lower, 1.0, 0.0, ALU.mult, ALU.add,
                                             cnt2[q][:, 0:1])
                    dve.tensor_tensor_reduce(junk[:, :], EQ2[q][:, 1, :], before[:, :], 1.0, 0.0, ALU.mult,
                                             ALU.add, cnt2[q][:, 1:2]).then_inc(n_cnt, 1)
                    dve.tensor_scalar(dif2[q][:, :], tab_s[q][:, :, 0], dump_f[:, 0:1], None,
                                      ALU.subtract).then_inc(n_dif, 1)
                    dve.wait_ge(n_nr2, a.value(1))
                    if a.past(2):
                        dve.wait_ge(n_U, a.value(-1))
                    for i in range(2):
                        ins = dve.tensor_scalar(EN[q][:, i, :], EQ2[q][:, i, :], nr2[q][:, i:i + 1], None, ALU.mult)
                        if i == 0:
                            dve.wait_ge(n_cnt, a.value(1))
                            dve.wait_ge(n_dif, a.value(1))
                            dve.scalar_tensor_tensor(fst2[a.slot(4)][:, :], cnt2[q][:, :], 0.5, dif2[q][:, :], ALU.is_lt,
                                                     ALU.mult).then_inc(n_fst, 1)
                    ins.then_inc(n_en, 1)
                    if a.reg is None and a.off == EP - 1:
                        dve.wait_ge(n_fst, a.value(1))
                        link(dve.tensor_tensor(fst2[a.slot(4)][:, :], fst2[a.slot(4)][:, :], cols(valid, a), ALU.mult))
                k = s.back(3)
                if k.within(EP):
                    dve.wait_ge(n_fst, k.value(1))
                    if k.past(4):
                        dve.wait_ge(n_sc, k.value(-3, 32))
                    dve.tensor_scalar(sidx2[k.slot(4)][:, :], fst2[k.slot(4)][:, :], dump2_f[:, 0:1], None,
                                      ALU.add).then_inc(n_idx, 1)
                k = s.back(-1)
                if k.within(EP):
                    if k.past(2):
                        dve.wait_ge(n_c0[k.slot(2)], k.back(2).turns(2, 32))
                    ends(k)

            run_steps(dve, EP, PAIR_STEPS, 4, 4, messages2)
            dve.wait_ge(n_x1, EP)
            dve.sem_inc(s_end2)

            for i in range(2):
                link(dve.memset(b_mv[i][:, :, :], 0.0))

            def rows4(t):
                return t.rearrange("p (j d) -> p j d", j=G)

            def nodes(s):
                a, v, h = s, s.back(1), s.back(2)
                z = v.slot(2)
                if v.within(NG + 2):
                    r = s.back(3)
                    dve.wait_ge(g_rs, v.value(1))
                    if r.within(NG):
                        dve.tensor_tensor(b_rs[z][:, G:2 * G, 0], b_rs[z][:, G:2 * G, 0],
                                          dinv2[:, bass.ds(r.value(0, G), G)], ALU.mult).then_inc(g_rsd, 1)
                        dve.wait_ge(g_rsd, r.value(1))
                    dve.scalar_tensor_tensor(b_nb[z][:, :, :], b_mv[z][:, :, 0:1], -1.0, b_rs[z][:, :, :],
                                             ALU.mult, ALU.mult).then_inc(g_nb, 1)
                if h.within(NG):
                    dve.wait_ge(g_h, h.value(1))
                    if h.past(8):
                        dve.wait_ge(g_out[h.slot(8)], h.back(8).turns(8))
                    dve.tensor_tensor(X1[h.slot(8)], X[h.slot(4)], H[h.slot(2)], ALU.add).then_inc(g_xh, 1)
                if a.within(NG):
                    dve.wait_ge(g_x[a.slot(4)], a.turns(4))
                    for j in range(G):
                        ins = dve.bn_stats(b_st[a.slot(2)][:, j, :], X[a.slot(4)][:, j * D:(j + 1) * D])
                if h.within(NG):
                    dve.wait_ge(g_xh, h.value(1))
                    dve.wait_ge(g_cg[h.slot(4)], h.turns(4, 16 * G))
                    dve.tensor_tensor(rows4(X1[h.slot(8)]), rows4(X1[h.slot(8)]), CG[h.slot(4)][:, :, 0:D],
                                      ALU.add).then_inc(g_x1, 1)
                    dve.wait_ge(g_x1, h.value(1))
                    for j in range(G):
                        ins = dve.bn_stats(b_st[a.slot(2)][:, G + j, :], X1[h.slot(8)][:, j * D:(j + 1) * D])
                if a.within(NG + 2):
                    ins.then_inc(g_st, 1)
                    pass_on(dve, (g_st, a.value(1)))
                    for j in list(range(G)) * a.within(NG) + list(range(G, 2 * G)) * h.within(NG):
                        ins = dve.bn_aggr(b_mv[a.slot(2)][:, j, :], b_st[a.slot(2)][:, j, :])
                    ins.then_inc(g_mv, 1)
                    dve.wait_ge(g_mv, a.value(1))
                    dve.tensor_scalar(b_ve[a.slot(2)][:, :, :], b_mv[a.slot(2)][:, :, 1:2], EPS, None,
                                      ALU.add).then_inc(g_ve, 1)
                k = s.back(4)
                if k.within(NG):
                    dve.wait_ge(g_h1, k.value(1))
                    if k.past(2):
                        dve.wait_ge(g_T, k.value(-1))
                    dve.tensor_tensor(rows4(AG[k.slot(2)]), rows4(H1[k.slot(2)]), CG[k.slot(4)][:, :, D:2 * D],
                                      ALU.add).then_inc(g_ag, 1)
                k = s.back(8)
                if k.within(NG):
                    dve.wait_ge(g_m2, k.value(1))
                    to = 4 + 2 * k.slot(2)
                    dve.tensor_tensor(X1[k.slot(8)], X1[k.slot(8)],
                                      bank[:, to:to + 2, :].rearrange("p a b -> p (a b)"), ALU.add).then_inc(g_fin, 1)
                if a.within(NG) and a.slot(2) == 0:
                    dve.tensor_copy(bi[a.pair()][:, :], slot_i[:, bass.ds(a.value(0, G), 2 * G)]).then_inc(g_bi, 1)

            run_steps(dve, NG, NODE_STEPS, 8, 4, nodes)

        @block.scalar
        def _(act):
            act.wait_ge(s_cos, 1)
            act.wait_ge(s_dve, 1)
            act.activation(cut[:, :], cut[:, :], ACT.Sin, bias=half_pi[:, 0:1], scale=-1.0).then_inc(s_cos, 1)

            for i in range(3):
                act.wait_ge(s_pre_pe, 2 + i)
                act.activation(wq_t[:, i, :, :].rearrange("p k d -> p (k d)"), bank[:, 4 + i, :], ACT.Copy)
                for k in range(KC):
                    act.activation(qkv_w[:, k, i * D:(i + 1) * D], bank[:, 4 + i, k * D:(k + 1) * D], ACT.Copy,
                                   scale=g_col[:, k:k + 1])
            act.wait_ge(s_pre_pe, 5)
            act.activation(wo_t[:, :, :].rearrange("p k d -> p (k d)"), bank[:, 7, :], ACT.Copy)
            act.wait_ge(s_pre_pe, 6)
            act.activation(w_t[:, :, :].rearrange("p k d -> p (k d)"), bank[:, 3, :], ACT.Copy)
            act.wait_ge(s_pre_pe, 7)
            act.activation(wd_t[0:R, :], bank[0:R, 0, :], ACT.Copy).then_inc(s_turned, 1)

            def hot(s):
                q = s.slot(2)
                act.wait_ge(s_hot, s.value(0, 2) + 1)
                if s.past(2):
                    act.wait_ge(s_hotmm, s.value(-1))
                for i in range(3):
                    ins = act.activation(hot_p[q][:, 2 + i, :], hot_p[q][:, 1, :], ACT.Copy,
                                         scale=ew_now[q][:, i:i + 1])
                ins.then_inc(s_hotw, 1)

            run_steps(act, EC, 0, 2, 2, hot)
            act.wait_ge(s_deg, 1)
            act.activation(root[:, :], deg1[:, :], ACT.Sqrt).then_inc(s_rsq, 1)

            def messages(s):
                k = s.back(10)
                if k.within(EC):
                    act.wait_ge(m_U, k.value(1))
                    if k.past(4):
                        act.wait_ge(m_sc, k.value(-3, 16))
                    act.activation(UB[k.slot(4)], bank[:, 6, 0:D], ACT.Copy).then_inc(m_UB, 1)
                k = s.back(5)
                if k.within(EC):
                    act.wait_ge(m_T, k.value(1))
                    if k.past(2):
                        act.wait_ge(m_qkv, k.value(-1))
                    act.activation(zT[k.slot(2)][:, :, :].rearrange("p a e -> p (a e)"), bank[:, 0, :],
                                   ACT.Copy).then_inc(m_zT, 1)
                k = s.back(4)
                if k.within(EC):
                    act.wait_ge(m_nb, k.value(3))
                    if k.past(2):
                        act.wait_ge(m_T, k.value(-1))
                    for i in range(2):
                        ins = act.activation(Z2[k.slot(2)][:, i, :], H2[k.slot(4)][:, i, :], ACT.Identity,
                                             bias=nb[k.slot(2)][:, 2 + i, :], scale=rs[k.slot(2)][:, 2 + i, :])
                    ins.then_inc(m_z, 1)
                k = s.back(2)
                if k.within(EC):
                    act.wait_ge(m_nb, k.value(1))
                    if k.past(4):
                        act.wait_ge(m_xh, k.value(-3))
                    for i in range(2):
                        ins = act.activation(H2[k.slot(4)][:, i, :], X2[k.slot(4)][:, i, :], ACT.Relu,
                                             bias=nb[k.slot(2)][:, i, :], scale=rs[k.slot(2)][:, i, :])
                    ins.then_inc(m_h, 1)
                k = s.back(7)
                if k.within(EC):
                    act.wait_ge(m_at, k.value(1))
                    if k.past(2):
                        act.wait_ge(m_aa, k.value(-1))
                    act.activation(sa[k.slot(2)][:, :], at[k.slot(2)][:, :], ACT.Silu).then_inc(m_sa, 1)
                k = s.back(6)
                if k.within(EC):
                    act.wait_ge(m_D, k.value(1))
                    if k.past(2):
                        act.wait_ge(m_msg, k.value(-1))
                    act.activation(DS[k.slot(2)][:, :], bank[:, 1, :], ACT.Silu).then_inc(m_ds, 1)

            run_steps(act, EC, MESSAGE_STEPS, 4, 4, messages)

            def messages2(s):
                k = s.back(4)
                q = k.slot(2)
                if k.within(EP):
                    act.wait_ge(n_U, k.value(1))
                    if k.past(2):
                        act.wait_ge(n_sc, k.value(-1, 32))
                    act.activation(UB4[:, 2 * q:2 * q + 2, :].rearrange("p a d -> p (a d)"), bank[:, q, :],
                                   ACT.Copy).then_inc(n_UB, 1)
                k = s.back(2)
                q = k.slot(2)
                if k.within(EP):
                    act.wait_ge(n_nb, k.value(1))
                    if k.past(2):
                        act.wait_ge(n_U, k.value(-1))
                    for i in range(2):
                        ins = act.activation(H1e[q][:, i, :], X1e[q][:, i, :], ACT.Relu, bias=nb[q][:, i, :],
                                             scale=rs[q][:, i, :])
                    ins.then_inc(n_h, 1)

            run_steps(act, EP, PAIR_STEPS, 4, 4, messages2)

            def nodes(s):
                k = s.back(5)
                if k.within(NG):
                    act.wait_ge(g_T, k.value(1))
                    if k.past(2):
                        act.wait_ge(g_m1, k.value(-1))
                    for c in range(KC):
                        ins = act.activation(hT[k.slot(2)][:, c * GN:(c + 1) * GN], bank[:, c, :], ACT.Copy)
                    ins.then_inc(g_hT, 1)
                k = s.back(3)
                if k.within(NG):
                    act.wait_ge(g_nb, k.value(3))
                    if k.past(2):
                        act.wait_ge(g_ag, k.value(-1))
                    for j in range(G):
                        ins = act.activation(H1[k.slot(2)][:, j * D:(j + 1) * D], X1[k.slot(8)][:, j * D:(j + 1) * D],
                                             ACT.Relu, bias=b_nb[k.slot(2)][:, G + j, :],
                                             scale=b_rs[k.slot(2)][:, G + j, :])
                    ins.then_inc(g_h1, 1)
                k = s.back(1)
                if k.within(NG):
                    act.wait_ge(g_nb, k.value(1))
                    if k.past(2):
                        act.wait_ge(g_xh, k.value(-1))
                    for j in range(G):
                        ins = act.activation(H[k.slot(2)][:, j * D:(j + 1) * D], X[k.slot(4)][:, j * D:(j + 1) * D],
                                             ACT.Relu, bias=b_nb[k.slot(2)][:, j, :], scale=b_rs[k.slot(2)][:, j, :])
                    ins.then_inc(g_h, 1)
                k = s.back(6)
                if k.within(NG):
                    act.wait_ge(g_m1, k.value(1))
                    if k.past(2):
                        act.wait_ge(g_m2, k.value(-1))
                    for c in range(KC):
                        ins = act.activation(rT[k.slot(2)][:, c * GN:(c + 1) * GN], bank[:, 2 + c, :], ACT.Relu,
                                             bias=b01_col[:, c:c + 1])
                    ins.then_inc(g_rT, 1)

            run_steps(act, NG, NODE_STEPS, 8, 4, nodes)

        @block.tensor
        def _(pe):
            pe.wait_ge(s_const, 5)
            pe.wait_ge(s_rows, 96)
            pe.wait_ge(s_endsf, 1)
            for i in range(3):
                t = e_rows[:, 2, :] if i == 2 else e_rowf[:, i, :]
                ins = pe.transpose(bank[:, 0, i * P:i * P + EC], t, identity[0:EC, 0:EC])
            ins.then_inc(s_pre_pe, 1)

            pe.wait_ge(s_ldw, 16 * 19)

            def turned(to, w):
                for k in range(KC):
                    for o in range(KC):
                        ins = pe.transpose(bank[:, to, k * D + o * P:k * D + (o + 1) * P],
                                           w[:, o, k * P:(k + 1) * P], identity[:, :])
                ins.then_inc(s_pre_pe, 1)

            for i in range(4):
                turned(4 + i, w_raw[:, i])
            turned(3, w_raw[:, 4])
            pe.wait_ge(s_cos, 1)
            for i in range(2):
                for o in range(KC):
                    ins = pe.transpose(bank[0:R, 0, i * D + o * P:i * D + (o + 1) * P], wd_raw[:, i, o, :],
                                       identity[:, :])
            ins.then_inc(s_pre_pe, 1)

            def hot(s):
                k = s
                q = k.slot(2)
                pe.wait_ge(s_hot, k.value(1, 2))
                first, last = k.reg is None and k.off == 0, k.reg is None and k.off == EC - 1
                for i in range(2):
                    pe.matmul(bank[:, 1, 0:COLS], hot_p[q][:, i, :], hot_c[q][:, i, :], start=first and i == 0,
                              stop=last and i == 1)
                pe.wait_ge(s_hotw, k.value(1))
                for i in range(3):
                    ins = pe.matmul(bank[:, 2, 0:COLS], hot_p[q][:, 2 + i, :], hot_c[q][:, 1, :],
                                    start=first and i == 0, stop=last and i == 2)
                ins.then_inc(s_hotmm, 1)

            run_steps(pe, EC, 0, 2, 2, hot)
            pe.wait_ge(s_turned, 1)
            pe.wait_ge(s_scan, 1)
            pe.matmul(bank[:, 3, 0:1], upper[:, :], running[:, COLS - 1:COLS], start=True,
                      stop=True).then_inc(s_pre_pe, 1)
            for i in range(3):
                for k in range(KC):
                    ins = pe.matmul(bank[0:3, 4 + i // 2, (i % 2) * D:(i % 2 + 1) * D],
                                    b_col[:, k:k + 1].broadcast_to([P, 3]), wq_t[:, i, k, :],
                                    start=(k == 0), stop=(k == KC - 1))
            ins.then_inc(s_pre_pe, 1)
            for m in range(KC):
                for k in range(KC):
                    pe.matmul(bank[:, 6, m * D:(m + 1) * D], w_t[:, k, m * P:(m + 1) * P], w1_raw[:, k, :],
                              start=(k == 0), stop=(k == KC - 1))
            for m in range(KC):
                for k in range(KC):
                    ins = pe.matmul(bank[:, 7, m:m + 1], w1_raw[:, k, m * P:(m + 1) * P], b0_col[:, k:k + 1],
                                    start=(k == 0), stop=(k == KC - 1))
            ins.then_inc(s_pre_pe, 1)
            pe.wait_ge(s_ready, 1)

            def messages(s):
                k = s.back(5)
                if k.within(EC):
                    pe.wait_ge(m_z, k.value(1))
                    pe.wait_ge(m_attr[k.slot(4)], k.turns(4))
                    if k.past(1):
                        pe.wait_ge(m_zT, k.value(0))
                        pe.wait_ge(m_aT, k.value(0))
                    for i in range(2):
                        for c in range(KC):
                            pe.transpose(bank[:, 0, (i * KC + c) * P:(i * KC + c + 1) * P],
                                         Z2[k.slot(2)][:, i, c * P:(c + 1) * P], identity[:, :])
                    pe.transpose(bank[0:R, 7, 0:P], attr[k.slot(4)][:, :], identity[:, :]).then_inc(m_T, 1)
                k = s.back(6)
                if k.within(EC):
                    q = k.slot(2)
                    pe.wait_ge(m_aT, k.value(1))
                    if k.past(1):
                        pe.wait_ge(m_ds, k.value(0))
                    pe.matmul(bank[:, 1, :], aT[q][:, :], wd_t[:, :], start=True, stop=True).then_inc(m_D, 1)
                    pe.wait_ge(m_zT, k.value(1))
                    if k.past(2):
                        pe.wait_ge(m_msg, k.value(-1))
                    pe.matmul(bank[:, 2 + q, :], ones3[:, :], bias3[:, D:3 * D], start=True, stop=False)
                    for c in range(KC):
                        pe.matmul(bank[:, 2 + q, :], zT[q][:, KC + c, :], qkv_w[:, c, D:3 * D], start=False,
                                  stop=(c == KC - 1))
                    if k.past(1):
                        pe.wait_ge(m_at, k.value(0))
                    pe.matmul(bank[:, 4, 0:D], ones3[:, :], bias3[:, 0:D], start=True, stop=False)
                    for c in range(KC):
                        ins = pe.matmul(bank[:, 4, 0:D], zT[q][:, c, :], qkv_w[:, c, 0:D], start=False,
                                        stop=(c == KC - 1))
                    ins.then_inc(m_qkv, 1)
                k = s.back(8)
                if k.within(EC):
                    pe.wait_ge(m_msg, k.value(1))
                    pe.wait_ge(m_eq, k.value(1))
                    if k.past(1):
                        pe.wait_ge(m_ST, k.value(0))
                    for c in range(KC):
                        ins = pe.matmul(bank[:, 5, c * P:(c + 1) * P], MSG[k.slot(2)][:, c * P:(c + 1) * P],
                                        EQ[k.slot(2)][:, :], start=True, stop=True)
                    ins.then_inc(m_S, 1)
                k = s.back(9)
                if k.within(EC):
                    pe.wait_ge(m_ST, k.value(1))
                    if k.past(1):
                        pe.wait_ge(m_UB, k.value(0))
                    for c in range(KC):
                        ins = pe.matmul(bank[:, 6, 0:D], ST[k.slot(2)][:, c, :], wo_t[:, c, :], start=(c == 0),
                                        stop=(c == KC - 1))
                    ins.then_inc(m_U, 1)

            run_steps(pe, EC, MESSAGE_STEPS, 4, 4, messages)

            def messages2(s):
                k = s.back(3)
                q = k.slot(2)
                if k.within(EP):
                    pe.wait_ge(n_en, k.value(1))
                    pe.wait_ge(n_h, k.value(1))
                    if k.past(2):
                        pe.wait_ge(n_UB, k.value(-1))
                    for to in range(2):
                        for i in range(2):
                            ins = pe.matmul(bank[:, q, to * D:(to + 1) * D], EN[q][:, i, to * P:(to + 1) * P],
                                            H1e[q][:, i, :], start=(i == 0), stop=(i == 1))
                    ins.then_inc(n_U, 1)

            run_steps(pe, EP, PAIR_STEPS, 4, 4, messages2)

            def nodes(s):
                k = s.back(5)
                if k.within(NG):
                    pe.wait_ge(g_ag, k.value(1))
                    if k.past(1):
                        pe.wait_ge(g_hT, k.value(0))
                    for c in range(KC):
                        for j in range(G):
                            ins = pe.transpose(bank[:, c, j * P:(j + 1) * P],
                                               AG[k.slot(2)][:, j * D + c * P:j * D + (c + 1) * P], identity[:, :])
                    ins.then_inc(g_T, 1)
                k = s.back(6)
                if k.within(NG):
                    pe.wait_ge(g_hT, k.value(1))
                    if k.past(1):
                        pe.wait_ge(g_rT, k.value(0))
                    for m in range(KC):
                        for c in range(KC):
                            ins = pe.matmul(bank[:, 2 + m, :], w01[:, c, m * P:(m + 1) * P],
                                            hT[k.slot(2)][:, c * GN:(c + 1) * GN], start=(c == 0),
                                            stop=(c == KC - 1))
                    ins.then_inc(g_m1, 1)
                k = s.back(7)
                if k.within(NG):
                    pe.wait_ge(g_rT, k.value(1))
                    if k.past(2):
                        pe.wait_ge(g_fin, k.value(-1))
                    for j in range(G):
                        to = bank[:, 4 + 2 * k.slot(2) + j // 2, (j % 2) * D:(j % 2 + 1) * D]
                        pe.matmul(to, ones3[:, :], bias3[:, 3 * D:], start=True, stop=False)
                        for c in range(KC):
                            ins = pe.matmul(to, rT[k.slot(2)][:, c * GN + j * P:c * GN + (j + 1) * P], w2_sb[:, c, :],
                                            start=False, stop=(c == KC - 1))
                    ins.then_inc(g_m2, 1)

            run_steps(pe, NG, NODE_STEPS, 8, 4, nodes)


_INS = ['x', 'src', 'dst', 'edge_attr_64', 'edge_weight', 'L0_gnn_ln_g', 'L0_gnn_ln_b', 'L0_gnn_Wq', 'L0_gnn_bq',
        'L0_gnn_Wk', 'L0_gnn_bk', 'L0_gnn_Wv', 'L0_gnn_bv', 'L0_gnn_Wo', 'L0_gnn_bo', 'L0_gnn_Wdk', 'L0_gnn_bdk',
        'L0_gnn_Wdv', 'L0_gnn_bdv', 'L1_gnn_W', 'L1_gnn_b', 'L1_gnn_W1', 'L1_gnn_b1', 'L1_gnn_W2', 'L1_gnn_b2']


def kernel(**inputs):
    import numpy as np
    import concourse.bacc as bacc
    from concourse.bass_utils import run_bass_kernel_spmd

    nc = bacc.Bacc("TRN2", target_bir_lowering=False, num_devices=1)
    arrays, args = {}, []
    for name in _INS:
        a = np.ascontiguousarray(inputs[name])
        arrays[f"in_{name}_dram"] = a
        args.append(nc.dram_tensor(f"in_{name}_dram", a.shape, mybir.dt.from_np(a.dtype), kind="ExternalInput").ap())
    args.append(nc.dram_tensor("out_0_dram", (N, D), F32, kind="ExternalOutput").ap())
    build(nc, *args)
    r = run_bass_kernel_spmd(nc, [arrays], core_ids=[0])
    return r.results[0]["out_0_dram"]
```

```python
from contextlib import ExitStack

import concourse.bass as bass
from concourse import mybir

P = 128
D = 256
R = 64
N = 50000
E = 12500
KC = D // P
EC = -(-E // P)
ET = E - (EC - 1) * P
G = 4
GN = G * P
NG = -(-N // GN)
GT = (N - (NG - 1) * GN) // G
COLS = NG * G
ROWS = NG * GN
assert ROWS - N >= P
MESSAGE_STEPS = 11
PAIR_STEPS = 5
NODE_STEPS = 10
EP = EC // 2
AHEAD = 5
FILLS_FIRST = 64
FILLS_STEP = 4
CUTOFF = 5.0
EPS = 1e-5
PI = 3.14159265358979

F32 = mybir.dt.float32
BF16 = mybir.dt.bfloat16
F16 = mybir.dt.float16
I32 = mybir.dt.int32
ALU = mybir.AluOpType
ACT = mybir.ActivationFunctionType


class Step:

    def __init__(self, off, reg=None, unroll=1):
        self.off, self.reg, self.unroll = off, reg, unroll

    def back(self, n):
        return Step(self.off - n, self.reg, self.unroll)

    def within(self, count):
        return self.reg is not None or 0 <= self.off < count

    def past(self, n):
        return self.reg is not None or self.off >= n

    def value(self, add=0, times=1):
        if self.reg is None:
            return (self.off + add) * times
        return self.reg * (self.unroll * times) + (self.off + add) * times

    def slot(self, ring):
        return self.off % ring

    def pair(self):
        return self.off // 2 % 2

    def turns(self, ring, times=16, add=1):
        if self.reg is None:
            return times * (self.off // ring + add)
        return self.reg * (times * (self.unroll // ring)) + times * (self.off // ring + add)


def run_steps(eng, count, depth, unroll, warm, body, start=0):
    first = -(-(depth + warm) // unroll)
    last = (count - 1) // unroll
    for s in range(start, first * unroll):
        body(Step(s))
    with eng.Fori(first, last) as reg:
        for u in range(unroll):
            body(Step(u, reg, unroll))
    for s in range(last * unroll, count + depth):
        body(Step(s))


def build(nc, x, src, dst, edge_attr, edge_weight, ln_g, ln_b, Wq, bq, Wk, bk, Wv, bv, Wo, bo,
          Wdk, bdk, Wdv, bdv, W, b, W1, b1, W2, b2, out):
    ctx = ExitStack()
    with ctx:
        def sb(name, shape, dt=F32):
            return ctx.enter_context(nc.sbuf_tensor(name, shape, dt))

        def ring(name, n, shape, dt=F32):
            return [sb(f"{name}{i}", shape, dt) for i in range(n)]

        def sem(name):
            return ctx.enter_context(nc.semaphore(name))

        def sems(name, n):
            return [sem(f"{name}_{i}") for i in range(n)]

        sums0 = nc.dram_tensor("sums0_dram", (ROWS, D), F32).ap()
        sums1 = nc.dram_tensor("sums1_dram", (ROWS, D), F32).ap()
        table = nc.dram_tensor("table_dram", (P * COLS, 1), F32).ap()

        bank = ctx.enter_context(nc.psum_tensor("bank", [P, 8, 512], F32))

        identity = sb("identity", [P, P])
        before = sb("before", [P, 2 * P])
        lower = before[:, P:]
        ones = sb("ones", [P, P])
        ones3 = sb("ones3", [3, P], BF16)
        leave3 = sb("leave3", [3, 2])
        minus_half = sb("minus_half", [P, 2 * G])
        half_pi = sb("half_pi", [P, 1])

        kept = sb("kept", [P, EC, D])
        room = kept[:, :, :].rearrange("p c d -> p (c d)")
        early, late = [0], [0]

        def place(taken, shape, dt=F32):
            width = 1
            for n in shape[1:]:
                width *= n
            words = width // 2 if dt in (BF16, F16) else width
            at0 = taken[0]
            taken[0] += words
            assert taken[0] <= EC * D
            view = room[0:shape[0], at0:at0 + words]
            if dt != F32:
                view = view.bitcast(dt)
            names = "abc"[:len(shape) - 1]
            if len(names) > 1:
                view = view.rearrange(f"p ({' '.join(names)}) -> p {' '.join(names)}",
                                      **dict(zip(names, shape[1:])))
            return view

        def temp(shape, dt=F32):
            return place(early, shape, dt)

        w_raw = temp([P, 5, KC, D])
        wd_raw = temp([P, 2, KC, R])
        wq_t = temp([P, 3, KC, D])
        qkv_w = sb("qkv_w", [P, KC, 3 * D])
        wo_t = sb("wo_t", [P, KC, D])
        w_t = temp([P, KC, D])
        wd_t = sb("wd_t", [R + 1, 2 * D])
        w1_raw = temp([P, KC, D])
        w01 = sb("w01", [P, KC, D])
        w2_sb = sb("w2_sb", [P, KC, D])
        g_col = sb("g_col", [P, KC])
        b_col = sb("b_col", [P, KC])
        b0_col = sb("b0_col", [P, KC])
        b1_col = sb("b1_col", [P, KC])
        b01_col = sb("b01_col", [P, KC])
        rows3 = temp([3, 4 * D])
        part3 = temp([3, 4 * D])
        piece = temp([3, 4 * D], BF16)
        bias3 = sb("bias3", [3, 4 * D], BF16)

        e_rows = temp([EC, 3, P])
        e_rowf = temp([EC, 2, P])
        src_f = sb("src_f", [P, EC])
        dst_f = sb("dst_f", [P, EC])
        ew_f = sb("ew_f", [P, EC])
        look = sb("look", [P, EC, 3], I32)
        node_i = look[:, :, 0:2]
        key_i = temp([P, EC, 2], I32)
        key_j = temp([P, EC, 2], I32)
        pkey = temp([P, EC, 2])
        ckey = temp([P, EC, 2])
        valid = sb("valid", [P, EC])
        edge_no = temp([P, EC], I32)
        away = temp([P, EC])
        turns_i = temp([P, EC], I32)
        cut = sb("cut", [P, EC])
        ew_part = temp([P, EC, 3])
        ew_low = [temp([P, EC], BF16) for _ in range(2)]
        off_d = sb("off_d", [P, EC])
        off_s = sb("off_s", [P, EC])
        norm = sb("norm", [P, EC])
        dump_f = sb("dump_f", [P, 1])
        dump_i = sb("dump_i", [P, 1], I32)

        iota_c = temp([P, COLS], F16)
        iota_p = temp([P, P], F16)
        iota_i = temp([P, COLS], I32)
        deg1 = temp([P, COLS])
        root = temp([P, COLS])
        turn = temp([P, COLS])
        some = temp([P, COLS])
        dinv = sb("dinv", [P, COLS])
        dinv2 = sb("dinv2", [P, COLS])
        hot_p = [temp([P, 4, P], BF16) for _ in range(4)]
        hot_c = [temp([P, COLS], BF16) for _ in range(4)]
        ew_now = [temp([P, 3]) for _ in range(4)]

        s_ldw, s_rows = sem("s_ldw"), sem("s_rows")
        s_const, s_dve, s_pre_pe = sem("s_const"), sem("s_dve"), sem("s_pre_pe")
        s_fill, s_fill1, s_table = sem("s_fill"), sem("s_fill1"), sem("s_table")
        s_hot, s_hotw, s_hotmm, s_pass = sem("s_hot"), sem("s_hotw"), sem("s_hotmm"), sem("s_pass")
        s_fillrow, s_tab_sb, s_cos, s_zero = sem("s_fillrow"), sem("s_tab_sb"), sem("s_cos"), sem("s_zero")
        s_deg, s_rsq = sem("s_deg"), sem("s_rsq")
        s_endsf, s_turned, s_ready = sem("s_endsf"), sem("s_turned"), sem("s_ready")

        CG = ring("cg_", 3, [P, G, 2 * D])
        fill_b, fill_0 = CG[0][:, 0:2, :], CG[0][:, 2:4, :]

        rows_b = fill_b.rearrange("p a d -> p (a d)")
        rows_0 = fill_0.rearrange("p a d -> p (a d)")

        X2 = [CG[1][:, i, :].rearrange("p (a d) -> p a d", a=2) for i in range(4)]
        H2 = [CG[2][:, i, :].rearrange("p (a d) -> p a d", a=2) for i in range(4)]
        Z2 = ring("z2_", 2, [P, 2, D])
        ib = ring("ib_", 2, [P, 2, 3], I32)
        attr = ring("attr_", 4, [P, R])
        row_d = ring("row_d_", 4, [P, P], I32)
        st = ring("st_", 2, [P, 4, 6])
        mv = ring("mv_", 2, [P, 4, 2])
        ve = ring("ve_", 2, [P, 4, 1])
        rs = ring("rs_", 2, [P, 4, 1])
        nb = ring("nb_", 2, [P, 4, 1])
        zT = ring("zT_", 2, [P, 2 * KC, P])
        aT = ring("aT_", 2, [R + 1, P])
        DS = ring("ds_", 2, [P, 2 * D])
        KD = ring("kd_", 2, [P, D])
        junk = sb("junk", [P, D])
        junk_e = sb("junk_e", [P, P])
        at = ring("at_", 2, [P, 1])
        sa = ring("sa_", 2, [P, 1])
        aa = ring("aa_", 2, [P, 1])
        EQ = ring("eq_", 2, [P, P])
        MSG = ring("msg_", 2, [P, D])
        ST = ring("stt_", 2, [P, KC, P])
        UB4 = sb("ub4", [P, 4, D])
        UB = [UB4[:, i, :] for i in range(4)]
        tab_d = ring("tab_d_", 2, [P, 2, 1])
        cnt = ring("cnt_", 2, [P, 2])
        fst = ring("fst_", 2, [P, 2])
        sidx = ring("sidx_", 2, [P, 2], I32)
        m_ib, m_row, m_attr = sem("m_ib"), sems("m_row", 4), sems("m_attr", 4)
        m_x, m_tab = sems("m_x", 4), sems("m_tab", 2)
        (m_st, m_mv, m_ve, m_rs, m_nb, m_h, m_z, m_xh, m_T, m_zT, m_aT, m_D, m_qkv, m_ds, m_kd, m_at, m_sa, m_aa,
         m_eq, m_cnt, m_fst, m_idx, m_msg, m_S, m_ST, m_U, m_UB, m_keep) = [
            sem("m_" + n) for n in ("st mv ve rs nb h z xh T zT aT D qkv ds kd at sa aa eq cnt fst idx msg S ST U "
                                    "UB keep").split()]
        m_sc = sem("m_sc")

        def halved(t, i):
            return t[:, 2 * i:2 * i + 2, :].rearrange("p a d -> p (a d)").rearrange("p (a d) -> p a d", a=4)

        C0 = [halved(CG[1], i)[:, 0:2, :] for i in range(2)]
        X1e = [halved(CG[1], i)[:, 2:4, :] for i in range(2)]
        H1e = [halved(CG[2], i)[:, 0:2, :] for i in range(2)]
        EQ2 = [halved(CG[2], i)[:, 2:4, :] for i in range(2)]
        EN = ring("en_", 2, [P, 2, 2 * P])
        sidx2 = ring("sidx2_", 4, [P, 2], I32)
        ic = ring("ic_", 2, [P, 2], I32)
        row_s = ring("row_s_", 2, [P, 2 * P], I32)
        cnt2 = ring("cnt2_", 2, [P, 2])
        fst2 = ring("fst2_", 4, [P, 2])
        n_ic, n_row, n_c0, n_sc = sem("n_ic"), sems("n_row", 2), sems("n_c0", 2), sem("n_sc")
        (n_x1, n_st, n_mv, n_ve, n_rs, n_nb, n_h, n_eq, n_cnt, n_en, n_fst, n_idx, n_U, n_UB) = [
            sem("n_" + n) for n in "x1 st mv ve rs nb h eq cnt en fst idx U UB".split()]

        def part(width):
            return place(late, [P, width])

        X = [part(G * D) for _ in range(4)]
        X1 = [part(G * D) for _ in range(8)]
        H = [part(G * D) for _ in range(2)]
        H1 = [part(G * D) for _ in range(2)]
        AG = [part(G * D) for _ in range(2)]
        hT = [part(KC * GN) for _ in range(2)]
        rT = [part(KC * GN) for _ in range(2)]
        rooms = [t[:, 2 * i:2 * i + 2, :].rearrange("p a d -> p (a d)") for t in CG for i in range(2)]
        OUT = rooms[0:2]
        S1 = rooms[2:6]
        b_st = ring("b_st_", 2, [P, 2 * G, 6])
        b_mv = ring("b_mv_", 2, [P, 2 * G, 2])
        b_ve, b_rs, b_nb = (ring(f"b_{n}_", 2, [P, 2 * G, 1]) for n in ("ve", "rs", "nb"))
        g_x, g_s0, g_s1, g_out = sems("g_x", 4), sems("g_s0", 4), sems("g_s1", 4), sems("g_out", 2)
        (g_st, g_mv, g_ve, g_rs, g_rsd, g_nb, g_h, g_xh, g_h1, g_ag, g_T, g_hT, g_m1, g_rT, g_m2, g_fin) = [
            sem("g_" + n) for n in "st mv ve rs rsd nb h xh h1 ag T hT m1 rT m2 fin".split()]
        s_end2 = sem("s_end2")

        def pass_on(eng, *waits):
            for s, v in waits:
                eng.wait_ge(s, v)
            if not all(isinstance(v, int) for _, v in waits):
                eng.sem_inc(s_pass)

        def group(t, k, parts=P):
            return t[bass.ds(k.value(0, GN), parts * G), :].rearrange("(p j) d -> p (j d)", j=G)

        def parts_of(k):
            return GT if k.reg is None and k.off == NG - 1 else P

        def last_pairs(messages2, nodes):
            for i in range(AHEAD):
                nodes(Step(i))
                if EP + 1 + i < EP + PAIR_STEPS:
                    messages2(Step(EP + 1 + i))

        block = ctx.enter_context(nc.Block())

        @block.sync
        def _(sp):
            sp.wait_ge(s_zero, 1)
            full = (EC - 1) * P
            for i, t in enumerate((src, dst, edge_weight)):
                to = e_rows[:, i, :] if t.dtype == F32 else e_rows[:, i, :].bitcast(I32)
                sp.dma_start(to[0:EC - 1, :], t[0:full].rearrange("(c p) -> c p", p=P)).then_inc(s_rows, 16)
                sp.dma_start(to[EC - 1:EC, 0:ET], t[full:E].rearrange("(c p) -> c p", c=1)).then_inc(s_rows, 16)
            sp.wait_ge(s_zero, 2)
            for r in range(G):
                sp.dma_start(rows_b[:, r * D:(r + 1) * D],
                             bo.rearrange("(a d) -> a d", a=1).broadcast_to([P, D])).then_inc(s_fillrow, 16)

            for i, w in enumerate((Wq, Wk, Wv, Wo, W)):
                sp.dma_start(w_raw[:, i, :, :], w.rearrange("(c p) k -> p c k", p=P)).then_inc(s_ldw, 16)
            for i, w in enumerate((Wdk, Wdv)):
                sp.dma_start(wd_raw[:, i, :, :], w.rearrange("(c p) k -> p c k", p=P)).then_inc(s_ldw, 16)
            sp.dma_start(w1_raw[:, :, :], W1.rearrange("(c p) k -> p c k", p=P)).then_inc(s_ldw, 16)
            sp.dma_start(w2_sb[:, :, :], W2.rearrange("(c p) k -> p c k", p=P)).then_inc(s_ldw, 16)
            with nc.allow_non_contiguous_dma(reason="256 numbers, one a partition"):
                for t, v in ((g_col, ln_g), (b_col, ln_b), (b0_col, b), (b1_col, b1)):
                    sp.dma_start(t[:, :], v.rearrange("(c p) -> p c", p=P)).then_inc(s_ldw, 16)
            for i, v in enumerate((bq, bk, bv, b2)):
                sp.dma_start(rows3[:, i * D:(i + 1) * D],
                             v.rearrange("(a d) -> a d", a=1).broadcast_to([3, D])).then_inc(s_ldw, 16)
            for i, v in enumerate((bdk, bdv)):
                sp.dma_start(wd_t[R:R + 1, i * D:(i + 1) * D], v.rearrange("(a d) -> a d", a=1)).then_inc(s_ldw, 16)
            sp.wait_ge(s_fillrow, 16 * G)
            for i in range(FILLS_FIRST):
                sp.dma_start(group(sums0, Step(i)), rows_b).then_inc(s_fill, 16)

            sp.wait_ge(s_tab_sb, 1)
            sp.dma_start(table.rearrange("(p c) k -> p (c k)", p=P), dinv[:, :]).then_inc(s_table, 16)

            LATER = 8

            def load_edges(s):
                k = s
                if k.within(EC):
                    n = k.off if k.reg is None else None
                    rows = ET if n == EC - 1 else P
                    if k.past(4):
                        pass_on(sp, (m_T, k.value(-3)))
                    sp.dma_start(attr[k.slot(4)][0:rows, :],
                                 edge_attr[bass.ds(k.value(0, P), rows), :]).then_inc(m_attr[k.slot(4)], 16)
                    if k.past(4):
                        pass_on(sp, (m_eq, k.value(-3)))
                    sp.dma_start(row_d[k.slot(4)][:, 0:rows],
                                 dst[bass.ds(k.value(0, P), rows)].rearrange("(a e) -> a e", a=1)
                                 .broadcast_to([P, rows])).then_inc(m_row[k.slot(4)], 16)

                k = s.back(LATER)
                if k.within(EC):
                    sp.dma_start(group(sums1, k), rows_0).then_inc(s_fill1, 16)

            assert NG == EC
            run_steps(sp, EC, LATER, 4, 4, load_edges)

            def load_src(s):
                k = s
                if k.within(EP):
                    rows = E - (EP - 1) * 2 * P if k.reg is None and k.off == EP - 1 else 2 * P
                    if k.past(2):
                        pass_on(sp, (n_eq, k.value(-1)))
                    sp.dma_start(row_s[k.slot(2)][:, 0:rows],
                                 src[bass.ds(k.value(0, 2 * P), rows)].rearrange("(a e) -> a e", a=1)
                                 .broadcast_to([P, rows])).then_inc(n_row[k.slot(2)], 16)

            run_steps(sp, EP, 0, 4, 4, load_src)

            sp.wait_ge(s_end2, 1)
            STORE = NODE_STEPS + 1

            def nodes(s):
                k = s
                if k.within(NG):
                    if k.past(4):
                        pass_on(sp, (g_xh, k.value(-3)))
                    sp.dma_start(X[k.slot(4)][0:parts_of(k), :], group(x, k, parts_of(k))
                                 ).then_inc(g_x[k.slot(4)], 16)
                k = s.back(4)
                if k.within(NG):
                    if not k.past(1):
                        sp.wait_ge(n_sc, 32 * EP)
                    if k.past(4):
                        pass_on(sp, (g_ag, k.value(-3)))
                    sp.dma_start(S1[k.slot(4)][0:parts_of(k), :], group(sums1, k, parts_of(k))
                                 ).then_inc(g_s1[k.slot(4)], 16)
                k = s.back(STORE)
                if k.within(NG):
                    pass_on(sp, (g_fin, k.value(1)))
                    sp.dma_start(group(out, k, parts_of(k)), OUT[k.slot(2)][0:parts_of(k), :]
                                 ).then_inc(g_out[k.slot(2)], 16)

            run_steps(sp, NG, STORE + 1, 8, 4, nodes)
            for q in range(2):
                sp.wait_ge(g_out[q], 16 * ((NG - q + 1) // 2))

        @block.gpsimd
        def _(pool):
            c = [0]

            def link(ins):
                c[0] += 1
                ins.then_inc(s_const, 1)
                pool.wait_ge(s_const, c[0])

            link(pool.memset(ones[:, :], 1.0))
            link(pool.memset(before[:, 0:P], 1.0))
            link(pool.affine_select(out=identity[:, :], in_=ones[:, :], compare_op=ALU.is_equal, fill=0.0,
                                    base=0, pattern=[[-1, P]], channel_multiplier=1))
            link(pool.affine_select(out=lower, in_=ones[:, :], compare_op=ALU.is_gt, fill=0.0,
                                    base=0, pattern=[[-1, P]], channel_multiplier=1))
            link(pool.iota(edge_no[:, :], [[P, EC]], base=0, channel_multiplier=1))
            link(pool.iota(iota_i[:, :], [[1, COLS]], base=0, channel_multiplier=0))
            link(pool.iota(dump_i[:, :], [[0, 1]], base=N, channel_multiplier=1))
            link(pool.memset(minus_half[:, :], -0.5))
            last_node = pool.to_reg(N - 1)
            last_row = pool.to_reg(ROWS - 1)
            last_entry = pool.to_reg(P * COLS - 1)

            def inv_sqrt(var, to, ready, done, k):
                width = var.shape[1]
                pool.wait_ge(ready, k.value(1))
                pool.tensor_tensor(to, var, minus_half[:, 0:width].rearrange("p (a b) -> p a b", b=1),
                                   ALU.pow).then_inc(done, 1)

            def scatter_add(sums, idx, rows, done):
                pool.indirect_dma_start(sums, bass.IndirectOffsetOnAxis(idx, 0), rows, None,
                                        bounds_check=last_row, compute_op=ALU.add).then_inc(done, 16)

            def gather(to, table, idx, bound, done):
                pool.indirect_dma_start(to, None, table, bass.IndirectOffsetOnAxis(idx, 0), bounds_check=bound,
                                        oob_is_err=True).then_inc(done, 16)

            def gather_x(k):
                for i in range(2):
                    gather(X2[k.slot(4)][:, i, :], x, ib[k.pair()][:, k.slot(2), i:i + 1], last_node, m_x[k.slot(4)])

            pool.wait_ge(m_ib, 2)
            for i in range(4):
                gather_x(Step(i))

            def messages(s):
                k = s
                if k.within(EC) and k.past(4):
                    w = [(m_xh, k.value(-3))]
                    if k.slot(2) == 0:
                        w.append((m_ib, k.turns(2, 1)))
                    pass_on(pool, *w)
                    gather_x(k)
                k = s.back(1)
                if k.within(EC + 2):
                    inv_sqrt(ve[k.slot(2)][:, :, :], rs[k.slot(2)][:, :, :], m_ve, m_rs, k)
                if k.within(EC):
                    if not k.past(1):
                        pool.wait_ge(s_table, 16)
                    if k.slot(2) == 0 and k.past(4):
                        pass_on(pool, (m_keep, k.turns(2, 1, -1)))
                    gather(tab_d[k.pair()][:, k.slot(2), :], table, ib[k.pair()][:, k.slot(2), 2:3], last_entry,
                           m_tab[k.pair()])
                k = s.back(11)
                if k.within(EC):
                    w = [(m_UB, k.value(1)), (m_idx, k.turns(2, 1))]
                    if k.past(1):
                        w.append((m_sc, k.value(0, 16)))
                    else:
                        w.append((s_fill, 16 * NG))
                    pass_on(pool, *w)
                    scatter_add(sums0, sidx[k.pair()][:, k.slot(2):k.slot(2) + 1], UB[k.slot(4)], m_sc)

            run_steps(pool, EC, MESSAGE_STEPS, 4, 4, messages)
            pool.wait_ge(m_sc, 16 * EC)

            def messages2(s):
                k = s
                q = k.slot(2)
                if k.within(EP):
                    w = [(n_ic, k.value(1))]
                    if k.past(2):
                        w.append((n_x1, k.value(-1)))
                    pass_on(pool, *w)
                    for i in range(2):
                        gather(C0[q][:, i, :], sums0, ic[q][:, i:i + 1], last_row, n_c0[q])
                k = s.back(1)
                if k.within(EP):
                    inv_sqrt(ve[k.slot(2)][:, 0:2, :], rs[k.slot(2)][:, 0:2, :], n_ve, n_rs, k)
                k = s.back(5)
                if k.within(EP):
                    w = [(n_UB, k.value(1)), (n_idx, k.value(1))]
                    if k.past(1):
                        w.append((n_sc, k.value(0, 32)))
                    else:
                        w.append((s_fill1, 16 * NG))
                    pass_on(pool, *w)
                    for i in range(2):
                        scatter_add(sums1, sidx2[k.slot(4)][:, i:i + 1], UB[2 * k.slot(2) + i], n_sc)

            run_steps(pool, EP, 1, 4, PAIR_STEPS + 3, messages2)

            def nodes(s):
                k = s.back(2)
                if k.within(NG):
                    pass_on(pool, (g_xh, k.value(1)))
                    pool.dma_start(X1[k.slot(8)][0:parts_of(k), :], group(sums0, k, parts_of(k)),
                                   accum_op=ALU.add).then_inc(g_s0[k.slot(4)], 16)
                k = s
                if k.within(NG + 3):
                    if k.reg is None and k.off > NG + 1:
                        pool.wait_ge(g_h1, k.value(-4))
                    inv_sqrt(b_ve[k.slot(2)][:, :, :], b_rs[k.slot(2)][:, :, :], g_ve, g_rs, k)

            last_pairs(messages2, nodes)
            run_steps(pool, NG, NODE_STEPS, 8, 4, nodes, start=AHEAD)

        @block.vector
        def _(dve):
            c = [0]

            def link(ins):
                c[0] += 1
                ins.then_inc(s_dve, 1)
                dve.wait_ge(s_dve, c[0])

            dve.memset(e_rows[:, :, :], 0.0).then_inc(s_zero, 1)
            dve.memset(fill_0, 0.0).then_inc(s_zero, 1)
            link(dve.memset(half_pi[:, :], PI / 2))
            link(dve.memset(ones3[:, :], 1.0))
            dve.wait_ge(s_const, 8)
            link(dve.tensor_copy(iota_c[:, :], iota_i[:, :]))
            link(dve.tensor_copy(iota_p[:, :], iota_i[:, 0:P]))
            link(dve.tensor_copy(dump_f[:, :], dump_i[:, :]))
            link(dve.tensor_scalar(valid[:, :], edge_no[:, :], float(E), None, ALU.is_lt))
            link(dve.tensor_scalar(leave3[:, :], before[0:3, P:P + 2], -1.0, None, ALU.mult))
            for i in range(2):
                link(dve.memset(aT[i][R:R + 1, :], 1.0))
            for i in range(4):
                link(dve.memset(attr[i][:, :], 0.0))
                link(dve.memset(row_d[i][:, :], 0))

            for i in range(2):
                link(dve.memset(row_s[i][:, :], 0))

            dve.wait_ge(s_rows, 96)
            dve.tensor_copy(e_rowf[:, :, :], e_rows[:, 0:2, :].bitcast(I32)).then_inc(s_endsf, 1)
            dve.wait_ge(s_pre_pe, 1)
            for i, t in enumerate((src_f, dst_f, ew_f)):
                link(dve.tensor_copy(t[:, :], bank[:, 0, i * P:i * P + EC]))
            link(dve.tensor_copy(node_i[:, :, 0], dst_f[:, :]))
            link(dve.tensor_copy(node_i[:, :, 1], src_f[:, :]))
            link(dve.tensor_scalar(key_i[:, :, :], node_i[:, :, :], 2, P - 1, ALU.logical_shift_right,
                                   ALU.bitwise_and))
            link(dve.tensor_copy(pkey[:, :, :], key_i[:, :, :]))
            link(dve.tensor_scalar(key_i[:, :, :], node_i[:, :, :], 9, 2, ALU.logical_shift_right,
                                   ALU.logical_shift_left))
            link(dve.tensor_scalar(key_j[:, :, :], node_i[:, :, :], G - 1, None, ALU.bitwise_and))
            link(dve.tensor_tensor(ckey[:, :, :], key_i[:, :, :], key_j[:, :, :], ALU.add))
            link(dve.scalar_tensor_tensor(look[:, :, 2], pkey[:, :, 0], float(COLS), ckey[:, :, 0], ALU.mult, ALU.add))
            for t, ends in ((off_d, dst_f), (off_s, src_f)):
                link(dve.tensor_scalar(t[:, :], ends[:, :], dump_f[:, 0:1], None, ALU.subtract))
                link(dve.tensor_tensor(t[:, :], t[:, :], valid[:, :], ALU.mult))
            link(dve.tensor_scalar(away[:, :], valid[:, :], -1000.0, 1000.0, ALU.mult, ALU.add))
            link(dve.tensor_tensor(pkey[:, :, 1], pkey[:, :, 1], away[:, :], ALU.add))
            for i in range(2):
                dve.tensor_copy(ib[i][:, :, :], look[:, 2 * i:2 * i + 2, :]).then_inc(m_ib, 1)
            link(dve.tensor_copy(ew_low[0][:, :], ew_f[:, :]))
            link(dve.tensor_copy(ew_part[:, :, 0], ew_low[0][:, :]))
            link(dve.tensor_tensor(ew_part[:, :, 2], ew_f[:, :], ew_part[:, :, 0], ALU.subtract))
            link(dve.tensor_copy(ew_low[1][:, :], ew_part[:, :, 2]))
            link(dve.tensor_copy(ew_part[:, :, 1], ew_low[1][:, :]))
            link(dve.tensor_tensor(ew_part[:, :, 2], ew_part[:, :, 2], ew_part[:, :, 1], ALU.subtract))

            link(dve.tensor_scalar(away[:, :], ew_f[:, :], -1.0, None, ALU.mult))
            link(dve.tensor_tensor(away[:, :], away[:, :], ew_f[:, :], ALU.max))
            link(dve.tensor_scalar(cut[:, :], away[:, :], PI / CUTOFF, None, ALU.mult))
            link(dve.tensor_scalar(turns_i[:, :], cut[:, :], 0.5 / PI, None, ALU.mult))
            link(dve.tensor_copy(away[:, :], turns_i[:, :]))
            link(dve.scalar_tensor_tensor(cut[:, :], away[:, :], -2 * PI, cut[:, :], ALU.mult, ALU.add))
            link(dve.tensor_scalar(away[:, :], cut[:, :], -1.0, None, ALU.mult))
            link(dve.tensor_tensor(cut[:, :], cut[:, :], away[:, :], ALU.max))
            link(dve.tensor_scalar(away[:, :], cut[:, :], -1.0, 2 * PI, ALU.mult, ALU.add))
            link(dve.tensor_tensor(cut[:, :], cut[:, :], away[:, :], ALU.min))
            dve.tensor_scalar(cut[:, :], cut[:, :], 0.0, PI, ALU.max, ALU.min).then_inc(s_cos, 1)
            dve.wait_ge(s_cos, 2)
            link(dve.tensor_scalar(cut[:, :], cut[:, :], 0.5, 0.5, ALU.mult, ALU.add))
            link(dve.tensor_scalar(away[:, :], ew_f[:, :], CUTOFF, None, ALU.is_lt))
            link(dve.tensor_tensor(cut[:, :], cut[:, :], away[:, :], ALU.mult))
            link(dve.tensor_tensor(cut[:, :], cut[:, :], valid[:, :], ALU.mult))

            def col(t, k, i=None):
                if i is not None:
                    return t[:, bass.ds(k.value(0), 1), i]
                at0 = t[:, bass.ds(k.value(0), 1)]
                return at0 if len(t.shape) == 2 else at0.rearrange("p a b -> p (a b)")

            def hot(s):
                k = s
                q = k.slot(4)
                if k.past(4):
                    dve.wait_ge(s_hotmm, k.value(-3))
                dve.tensor_scalar(hot_p[q][:, 0, :], iota_p[:, :], col(pkey, k, 1), None, ALU.is_equal)
                dve.tensor_copy(ew_now[q][:, :], ew_part[:, bass.ds(k.value(0), 1), :]
                                .rearrange("p a b -> p (a b)")).then_inc(s_hot, 1)
                dve.tensor_scalar(hot_c[q][:, :], iota_c[:, :], col(ckey, k, 1), None, ALU.is_equal)
                dve.tensor_scalar(hot_p[q][:, 1, :], iota_p[:, :], col(pkey, k, 1), col(ew_part, k, 0),
                                  ALU.is_equal, ALU.mult).then_inc(s_hot, 1)

            run_steps(dve, EC, 0, 4, 4, hot)

            dve.wait_ge(s_hotmm, EC)
            link(dve.tensor_scalar(deg1[:, :], bank[:, 2, 0:COLS], 1.0, None, ALU.add))
            link(dve.tensor_scalar(some[:, :], deg1[:, :], 0.0, None, ALU.is_gt))
            dve.tensor_scalar(deg1[:, :], deg1[:, :], 1e-30, None, ALU.max).then_inc(s_deg, 1)
            dve.wait_ge(s_rsq, 1)
            link(dve.reciprocal(root[:, :], root[:, :]))
            link(dve.tensor_tensor(turn[:, :], root[:, :], root[:, :], ALU.mult))
            link(dve.tensor_tensor(turn[:, :], turn[:, :], deg1[:, :], ALU.mult))
            link(dve.tensor_scalar(turn[:, :], turn[:, :], -0.5, 1.5, ALU.mult, ALU.add))
            link(dve.tensor_tensor(root[:, :], root[:, :], turn[:, :], ALU.mult))
            dve.tensor_tensor(dinv[:, :], root[:, :], some[:, :], ALU.mult).then_inc(s_tab_sb, 1)
            dve.wait_ge(s_tab_sb, 1)
            link(dve.tensor_tensor(dinv2[:, :], dinv[:, :], dinv[:, :], ALU.mult))
            dve.wait_ge(s_pre_pe, 9)
            link(dve.tensor_copy(w01[:, :, :].rearrange("p k d -> p (k d)"), bank[:, 6, :]))
            dve.tensor_tensor(b01_col[:, :], b1_col[:, :], bank[:, 7, 0:KC], ALU.add).then_inc(s_ready, 1)

            for i in range(2):
                link(dve.memset(mv[i][:, 2:4, :], 0.0))

            def pair_of(t, k, *i):
                return t[(slice(None), bass.ds(k.value(0), 2), *i)]

            def indices(k):
                dve.tensor_copy(ib[k.pair()][:, :, :], pair_of(look, k, slice(None))).then_inc(m_ib, 1)

            def biases():
                dve.wait_ge(s_pre_pe, 8)
                link(dve.tensor_copy(part3[:, D * 3:], rows3[:, D * 3:]))
                link(dve.tensor_tensor(part3[:, 0:2 * D], rows3[:, 0:2 * D], bank[0:3, 4, :], ALU.add))
                link(dve.tensor_tensor(part3[:, 2 * D:3 * D], rows3[:, 2 * D:3 * D], bank[0:3, 5, 0:D], ALU.add))
                for i in range(2):
                    link(dve.tensor_copy(piece[:, :], part3[:, :]))
                    link(dve.scalar_tensor_tensor(part3[:, :], piece[:, :], leave3[:, i:i + 1], part3[:, :], ALU.mult,
                                                  ALU.add))
                dve.tensor_copy(bias3[:, :], part3[:, :]).then_inc(s_ready, 1)

            def messages(s):
                if s.reg is None and s.off == 2:
                    biases()
                a, h, t, m, f = s.back(1), s.back(3), s.back(5), s.back(7), s.back(9)
                u, q, v = s.back(1), m.slot(2), s.back(2)
                if v.within(EC + 2):
                    dve.wait_ge(m_rs, v.value(1))
                    dve.scalar_tensor_tensor(nb[v.slot(2)][:, :, :], mv[v.slot(2)][:, :, 0:1], -1.0,
                                             rs[v.slot(2)][:, :, :], ALU.mult, ALU.mult).then_inc(m_nb, 1)
                if m.within(EC):
                    dve.wait_ge(m_qkv, m.value(1))
                    dve.wait_ge(m_ds, m.value(1))
                    dve.tensor_tensor(KD[q][:, :], bank[:, 2 + q, 0:D], DS[q][:, 0:D], ALU.mult).then_inc(m_kd, 1)
                if a.within(EC):
                    dve.wait_ge(m_x[a.slot(4)], a.turns(4, 32))
                    for i in range(2):
                        ins = dve.bn_stats(st[u.slot(2)][:, i, :], X2[a.slot(4)][:, i, :])
                if m.within(EC):
                    dve.wait_ge(m_kd, m.value(1))
                    dve.tensor_tensor_reduce(junk[:, :], bank[:, 4, 0:D], KD[q][:, :], 1.0, 0.0,
                                             ALU.mult, ALU.add, at[q][:, :]).then_inc(m_at, 1)
                if h.within(EC):
                    dve.wait_ge(m_h, h.value(1))
                    for i in range(2):
                        ins = dve.bn_stats(st[u.slot(2)][:, 2 + i, :], H2[h.slot(4)][:, i, :])
                if u.within(EC + 2):
                    ins.then_inc(m_st, 1)
                if m.within(EC):
                    dve.wait_ge(m_row[m.slot(4)], m.turns(4))
                    if m.past(2):
                        dve.wait_ge(m_S, m.value(-1))
                    dve.tensor_scalar(EQ[q][:, :], row_d[m.slot(4)][:, :], col(dst_f, m), None,
                                      ALU.is_equal).then_inc(m_eq, 1)
                if u.within(EC + 2):
                    pass_on(dve, (m_st, u.value(1)))
                    for i in [0, 1] * a.within(EC) + [2, 3] * h.within(EC):
                        ins = dve.bn_aggr(mv[u.slot(2)][:, i, :], st[u.slot(2)][:, i, :])
                    ins.then_inc(m_mv, 1)
                if f.within(EC):
                    dve.wait_ge(m_S, f.value(1))
                    dve.tensor_copy(ST[f.slot(2)][:, :, :].rearrange("p k e -> p (k e)"),
                                    bank[:, 5, 0:KC * P]).then_inc(m_ST, 1)
                if u.within(EC + 2):
                    dve.wait_ge(m_mv, u.value(1))
                    dve.tensor_scalar(ve[u.slot(2)][:, :, :], mv[u.slot(2)][:, :, 1:2], EPS, None,
                                      ALU.add).then_inc(m_ve, 1)
                if m.within(EC):
                    dve.wait_ge(m_sa, m.value(1))
                    dve.tensor_scalar(aa[q][:, :], sa[q][:, :], col(cut, m), None, ALU.mult).then_inc(m_aa, 1)
                    dve.wait_ge(m_eq, m.value(1))
                    dve.tensor_tensor_reduce(junk_e[:, :], EQ[q][:, :], lower, 1.0, 0.0, ALU.mult, ALU.add,
                                             cnt[m.pair()][:, q:q + 1]).then_inc(m_cnt, 1)
                    dve.wait_ge(m_aa, m.value(1))
                    dve.scalar_tensor_tensor(MSG[q][:, :], bank[:, 2 + q, D:2 * D], aa[q][:, 0:1], DS[q][:, D:2 * D],
                                             ALU.mult, ALU.mult).then_inc(m_msg, 1)
                last = f.within(EC) and f.slot(2) == 1
                z, first = f.pair(), f.back(1)
                if h.within(EC):
                    dve.tensor_tensor(kept[:, bass.ds(h.value(0), 1), :].rearrange("p a d -> p (a d)"),
                                      X2[h.slot(4)][:, 0, :], H2[h.slot(4)][:, 0, :], ALU.add).then_inc(m_xh, 1)
                if last:
                    dve.scalar_tensor_tensor(fst[z][:, :], cnt[z][:, :], 0.5, pair_of(off_d, first), ALU.is_lt,
                                             ALU.mult).then_inc(m_fst, 1)
                if t.within(EC):
                    dve.wait_ge(m_T, t.value(1))
                    dve.tensor_copy(aT[t.slot(2)][0:R, :], bank[0:R, 7, 0:P]).then_inc(m_aT, 1)
                if last:
                    dve.wait_ge(m_fst, f.turns(2, 1))
                    if f.past(4):
                        dve.wait_ge(m_sc, f.value(-3, 16))
                    dve.tensor_scalar(sidx[z][:, :], fst[z][:, :], dump_f[:, 0:1], None, ALU.add).then_inc(m_idx, 1)
                if v.within(EC) and v.slot(2) == 1:
                    dve.wait_ge(m_tab[v.pair()], v.turns(4, 32))
                    dve.tensor_tensor(pair_of(norm, v.back(1)), tab_d[v.pair()][:, :, 0],
                                      pair_of(ew_f, v.back(1)), ALU.mult).then_inc(m_keep, 1)
                n = s.back(-1)
                if n.within(EC) and n.slot(2) == 0 and n.past(4):
                    indices(n)

            run_steps(dve, EC, MESSAGE_STEPS, 4, 4, messages)

            dve.wait_ge(m_xh, EC)

            def cols(t, k, *i):
                return t[(slice(None), bass.ds(k.value(0, 2), 2), *i)]

            def ends(k):
                dve.tensor_copy(ic[k.slot(2)][:, :], cols(look, k, 0)).then_inc(n_ic, 1)

            ends(Step(0))

            def messages2(s):
                v = s.back(2)
                z = v.slot(2)
                if v.within(EP):
                    dve.wait_ge(n_rs, v.value(1))
                    dve.scalar_tensor_tensor(nb[z][:, 0:2, :], mv[z][:, 0:2, 0:1], -1.0,
                                             rs[z][:, 0:2, :], ALU.mult, ALU.mult).then_inc(n_nb, 1)
                a = s.back(1)
                q = a.slot(2)
                if a.within(EP):
                    dve.wait_ge(n_c0[q], a.turns(2, 32))
                    if a.past(2):
                        dve.wait_ge(n_h, a.value(-1))
                    dve.tensor_tensor(X1e[q], cols(kept, a, slice(None)), C0[q], ALU.add).then_inc(n_x1, 1)
                    dve.wait_ge(n_row[q], a.turns(2))
                    for i in range(2):
                        ins = dve.tensor_scalar(EQ2[q][:, i, :], row_s[q][:, :],
                                                src_f[:, bass.ds(a.value(0, 2) + i, 1)], None, ALU.is_equal)
                    ins.then_inc(n_eq, 1)
                    dve.wait_ge(n_x1, a.value(1))
                    for i in range(2):
                        ins = dve.bn_stats(st[q][:, i, :], X1e[q][:, i, :])
                    ins.then_inc(n_st, 1)
                    dve.wait_ge(n_eq, a.value(1))
                    dve.tensor_tensor_reduce(junk_e[:, :], EQ2[q][:, 0, 0:P], lower, 1.0, 0.0, ALU.mult, ALU.add,
                                             cnt2[q][:, 0:1])
                    pass_on(dve, (n_st, a.value(1)))
                    for i in range(2):
                        ins = dve.bn_aggr(mv[q][:, i, :], st[q][:, i, :])
                    ins.then_inc(n_mv, 1)
                    dve.tensor_tensor_reduce(junk[:, :], EQ2[q][:, 1, :], before[:, :], 1.0, 0.0, ALU.mult,
                                             ALU.add, cnt2[q][:, 1:2]).then_inc(n_cnt, 1)
                    dve.wait_ge(n_mv, a.value(1))
                    dve.tensor_scalar(ve[q][:, 0:2, :], mv[q][:, 0:2, 1:2], EPS, None, ALU.add).then_inc(n_ve, 1)
                    if a.past(2):
                        dve.wait_ge(n_U, a.value(-1))
                    for i in range(2):
                        ins = dve.tensor_scalar(EN[q][:, i, :], EQ2[q][:, i, :],
                                                norm[:, bass.ds(a.value(0, 2) + i, 1)], None, ALU.mult)
                    ins.then_inc(n_en, 1)
                    dve.wait_ge(n_cnt, a.value(1))
                    dve.scalar_tensor_tensor(fst2[a.slot(4)][:, :], cnt2[q][:, :], 0.5, cols(off_s, a), ALU.is_lt,
                                             ALU.mult).then_inc(n_fst, 1)
                k = s.back(3)
                if k.within(EP):
                    dve.wait_ge(n_fst, k.value(1))
                    if k.past(4):
                        dve.wait_ge(n_sc, k.value(-3, 32))
                    dve.tensor_scalar(sidx2[k.slot(4)][:, :], fst2[k.slot(4)][:, :], dump_f[:, 0:1], None,
                                      ALU.add).then_inc(n_idx, 1)
                k = s.back(-1)
                if k.within(EP):
                    if k.past(2):
                        pass_on(dve, (n_c0[k.slot(2)], k.back(2).turns(2, 32)))
                    ends(k)

            run_steps(dve, EP, 1, 4, PAIR_STEPS + 3, messages2)
            dve.wait_ge(n_x1, EP)
            dve.sem_inc(s_end2)

            for i in range(2):
                link(dve.memset(b_mv[i][:, :, :], 0.0))

            def nodes(s):
                a, v, h, r, t = s, s.back(1), s.back(2), s.back(4), s.back(3)
                z = v.slot(2)
                if v.within(NG + 3):
                    dve.wait_ge(g_rs, v.value(1))
                    if r.within(NG):
                        dve.tensor_tensor(b_rs[z][:, G:2 * G, 0], b_rs[z][:, G:2 * G, 0],
                                          dinv2[:, bass.ds(r.value(0, G), G)], ALU.mult).then_inc(g_rsd, 1)
                        dve.wait_ge(g_rsd, r.value(1))
                    dve.scalar_tensor_tensor(b_nb[z][:, :, :], b_mv[z][:, :, 0:1], -1.0, b_rs[z][:, :, :],
                                             ALU.mult, ALU.mult).then_inc(g_nb, 1)
                if h.within(NG):
                    dve.wait_ge(g_h, h.value(1))
                    dve.tensor_tensor(X1[h.slot(8)], X[h.slot(4)], H[h.slot(2)], ALU.add).then_inc(g_xh, 1)
                if a.within(NG):
                    dve.wait_ge(g_x[a.slot(4)], a.turns(4))
                    for j in range(G):
                        ins = dve.bn_stats(b_st[a.slot(2)][:, j, :], X[a.slot(4)][:, j * D:(j + 1) * D])
                k = s.back(9)
                if k.within(NG):
                    dve.wait_ge(g_m2, k.value(1))
                    if k.past(2):
                        dve.wait_ge(g_out[k.slot(2)], k.back(2).turns(2))
                    to = 4 + 2 * k.slot(2)
                    dve.tensor_tensor(OUT[k.slot(2)], X1[k.slot(8)],
                                      bank[:, to:to + 2, :].rearrange("p a b -> p (a b)"), ALU.add).then_inc(g_fin, 1)
                if t.within(NG):
                    dve.wait_ge(g_s0[t.slot(4)], t.turns(4))
                    for j in range(G):
                        ins = dve.bn_stats(b_st[a.slot(2)][:, G + j, :], X1[t.slot(8)][:, j * D:(j + 1) * D])
                if a.within(NG + 3):
                    ins.then_inc(g_st, 1)
                    pass_on(dve, (g_st, a.value(1)))
                    for j in list(range(G)) * a.within(NG) + list(range(G, 2 * G)) * t.within(NG):
                        ins = dve.bn_aggr(b_mv[a.slot(2)][:, j, :], b_st[a.slot(2)][:, j, :])
                    ins.then_inc(g_mv, 1)
                    dve.wait_ge(g_mv, a.value(1))
                    dve.tensor_scalar(b_ve[a.slot(2)][:, :, :], b_mv[a.slot(2)][:, :, 1:2], EPS, None,
                                      ALU.add).then_inc(g_ve, 1)
                k = s.back(5)
                if k.within(NG):
                    dve.wait_ge(g_h1, k.value(1))
                    if k.past(2):
                        dve.wait_ge(g_T, k.value(-1))
                    dve.wait_ge(g_s1[k.slot(4)], k.turns(4))
                    for j in range(G):
                        at0 = slice(j * D, (j + 1) * D)
                        ins = dve.scalar_tensor_tensor(AG[k.slot(2)][:, at0], S1[k.slot(4)][:, at0],
                                                       dinv[:, bass.ds(k.value(0, G) + j, 1)],
                                                       H1[k.slot(2)][:, at0], ALU.mult, ALU.add)
                    ins.then_inc(g_ag, 1)

            last_pairs(messages2, nodes)
            run_steps(dve, NG, NODE_STEPS, 8, 4, nodes, start=AHEAD)

        @block.scalar
        def _(act):
            act.wait_ge(s_cos, 1)
            act.wait_ge(s_dve, 1)
            act.activation(cut[:, :], cut[:, :], ACT.Sin, bias=half_pi[:, 0:1], scale=-1.0).then_inc(s_cos, 1)

            for i in range(3):
                act.wait_ge(s_pre_pe, 2 + i)
                act.activation(wq_t[:, i, :, :].rearrange("p k d -> p (k d)"), bank[:, 4 + i, :], ACT.Copy)
                for k in range(KC):
                    act.activation(qkv_w[:, k, i * D:(i + 1) * D], bank[:, 4 + i, k * D:(k + 1) * D], ACT.Copy,
                                   scale=g_col[:, k:k + 1])
            act.wait_ge(s_pre_pe, 5)
            act.activation(wo_t[:, :, :].rearrange("p k d -> p (k d)"), bank[:, 7, :], ACT.Copy)
            act.wait_ge(s_pre_pe, 6)
            act.activation(w_t[:, :, :].rearrange("p k d -> p (k d)"), bank[:, 3, :], ACT.Copy)
            act.wait_ge(s_pre_pe, 7)
            act.activation(wd_t[0:R, :], bank[0:R, 0, :], ACT.Copy).then_inc(s_turned, 1)

            def hot(s):
                q = s.slot(4)
                act.wait_ge(s_hot, s.value(0, 2) + 1)
                if s.past(4):
                    act.wait_ge(s_hotmm, s.value(-3))
                for i in (1, 2):
                    ins = act.activation(hot_p[q][:, 1 + i, :], hot_p[q][:, 0, :], ACT.Copy,
                                         scale=ew_now[q][:, i:i + 1])
                ins.then_inc(s_hotw, 1)

            run_steps(act, EC, 0, 4, 4, hot)
            act.wait_ge(s_deg, 1)
            act.activation(root[:, :], deg1[:, :], ACT.Sqrt).then_inc(s_rsq, 1)

            def messages(s):
                if s.reg is None and s.off >= 2:
                    at0 = FILLS_FIRST + FILLS_STEP * (s.off - 2)
                    for i in range(at0, min(at0 + FILLS_STEP, NG)):
                        act.wait_ge(m_nb, s.off - 1)
                        act.dma_start(group(sums0, Step(i)), rows_b).then_inc(s_fill, 16)
                k = s.back(10)
                if k.within(EC):
                    act.wait_ge(m_U, k.value(1))
                    if k.past(4):
                        act.wait_ge(m_sc, k.value(-3, 16))
                    act.activation(UB[k.slot(4)], bank[:, 6, 0:D], ACT.Copy).then_inc(m_UB, 1)
                k = s.back(5)
                if k.within(EC):
                    act.wait_ge(m_T, k.value(1))
                    if k.past(2):
                        act.wait_ge(m_qkv, k.value(-1))
                    act.activation(zT[k.slot(2)][:, :, :].rearrange("p a e -> p (a e)"), bank[:, 0, :],
                                   ACT.Copy).then_inc(m_zT, 1)
                k = s.back(4)
                if k.within(EC):
                    act.wait_ge(m_nb, k.value(3))
                    if k.past(2):
                        act.wait_ge(m_T, k.value(-1))
                    for i in range(2):
                        ins = act.activation(Z2[k.slot(2)][:, i, :], H2[k.slot(4)][:, i, :], ACT.Identity,
                                             bias=nb[k.slot(2)][:, 2 + i, :], scale=rs[k.slot(2)][:, 2 + i, :])
                    ins.then_inc(m_z, 1)
                k = s.back(2)
                if k.within(EC):
                    act.wait_ge(m_nb, k.value(1))
                    if k.past(4):
                        act.wait_ge(m_xh, k.value(-3))
                    for i in range(2):
                        ins = act.activation(H2[k.slot(4)][:, i, :], X2[k.slot(4)][:, i, :], ACT.Relu,
                                             bias=nb[k.slot(2)][:, i, :], scale=rs[k.slot(2)][:, i, :])
                    ins.then_inc(m_h, 1)
                k = s.back(7)
                if k.within(EC):
                    act.wait_ge(m_at, k.value(1))
                    if k.past(2):
                        act.wait_ge(m_aa, k.value(-1))
                    act.activation(sa[k.slot(2)][:, :], at[k.slot(2)][:, :], ACT.Silu).then_inc(m_sa, 1)
                k = s.back(6)
                if k.within(EC):
                    act.wait_ge(m_D, k.value(1))
                    if k.past(2):
                        act.wait_ge(m_msg, k.value(-1))
                    act.activation(DS[k.slot(2)][:, :], bank[:, 1, :], ACT.Silu).then_inc(m_ds, 1)

            run_steps(act, EC, MESSAGE_STEPS, 4, 4, messages)

            def messages2(s):
                k = s.back(4)
                q = k.slot(2)
                if k.within(EP):
                    act.wait_ge(n_U, k.value(1))
                    if k.past(2):
                        act.wait_ge(n_sc, k.value(-1, 32))
                    act.activation(UB4[:, 2 * q:2 * q + 2, :].rearrange("p a d -> p (a d)"), bank[:, q, :],
                                   ACT.Copy).then_inc(n_UB, 1)
                k = s.back(2)
                q = k.slot(2)
                if k.within(EP):
                    act.wait_ge(n_nb, k.value(1))
                    if k.past(2):
                        act.wait_ge(n_U, k.value(-1))
                    for i in range(2):
                        ins = act.activation(H1e[q][:, i, :], X1e[q][:, i, :], ACT.Relu, bias=nb[q][:, i, :],
                                             scale=rs[q][:, i, :])
                    ins.then_inc(n_h, 1)

            run_steps(act, EP, 1, 4, PAIR_STEPS + 3, messages2)

            def nodes(s):
                k = s.back(6)
                if k.within(NG):
                    act.wait_ge(g_T, k.value(1))
                    if k.past(2):
                        act.wait_ge(g_m1, k.value(-1))
                    for c in range(KC):
                        ins = act.activation(hT[k.slot(2)][:, c * GN:(c + 1) * GN], bank[:, c, :], ACT.Copy)
                    ins.then_inc(g_hT, 1)
                k = s.back(4)
                if k.within(NG):
                    act.wait_ge(g_nb, k.value(4))
                    if k.past(2):
                        act.wait_ge(g_ag, k.value(-1))
                    for j in range(G):
                        ins = act.activation(H1[k.slot(2)][:, j * D:(j + 1) * D], X1[k.slot(8)][:, j * D:(j + 1) * D],
                                             ACT.Relu, bias=b_nb[k.back(-3).slot(2)][:, G + j, :],
                                             scale=b_rs[k.back(-3).slot(2)][:, G + j, :])
                    ins.then_inc(g_h1, 1)
                k = s.back(1)
                if k.within(NG):
                    act.wait_ge(g_nb, k.value(1))
                    if k.past(2):
                        act.wait_ge(g_xh, k.value(-1))
                    for j in range(G):
                        ins = act.activation(H[k.slot(2)][:, j * D:(j + 1) * D], X[k.slot(4)][:, j * D:(j + 1) * D],
                                             ACT.Relu, bias=b_nb[k.slot(2)][:, j, :], scale=b_rs[k.slot(2)][:, j, :])
                    ins.then_inc(g_h, 1)
                k = s.back(7)
                if k.within(NG):
                    act.wait_ge(g_m1, k.value(1))
                    if k.past(2):
                        act.wait_ge(g_m2, k.value(-1))
                    for c in range(KC):
                        ins = act.activation(rT[k.slot(2)][:, c * GN:(c + 1) * GN], bank[:, 2 + c, :], ACT.Relu,
                                             bias=b01_col[:, c:c + 1])
                    ins.then_inc(g_rT, 1)

            last_pairs(messages2, nodes)
            run_steps(act, NG, NODE_STEPS, 8, 4, nodes, start=AHEAD)

        @block.tensor
        def _(pe):
            pe.wait_ge(s_const, 4)
            pe.wait_ge(s_rows, 96)
            pe.wait_ge(s_endsf, 1)
            for i in range(3):
                t = e_rows[:, 2, :] if i == 2 else e_rowf[:, i, :]
                ins = pe.transpose(bank[:, 0, i * P:i * P + EC], t, identity[0:EC, 0:EC])
            ins.then_inc(s_pre_pe, 1)

            pe.wait_ge(s_ldw, 16 * 19)

            def turned(to, w):
                for k in range(KC):
                    for o in range(KC):
                        ins = pe.transpose(bank[:, to, k * D + o * P:k * D + (o + 1) * P],
                                           w[:, o, k * P:(k + 1) * P], identity[:, :])
                ins.then_inc(s_pre_pe, 1)

            for i in range(4):
                turned(4 + i, w_raw[:, i])
            turned(3, w_raw[:, 4])
            pe.wait_ge(s_cos, 1)
            for i in range(2):
                for o in range(KC):
                    ins = pe.transpose(bank[0:R, 0, i * D + o * P:i * D + (o + 1) * P], wd_raw[:, i, o, :],
                                       identity[:, :])
            ins.then_inc(s_pre_pe, 1)

            def hot(s):
                k = s
                q = k.slot(4)
                first, last = k.reg is None and k.off == 0, k.reg is None and k.off == EC - 1
                for i in range(3):
                    pe.wait_ge(*((s_hot, k.value(1, 2)) if i == 0 else (s_hotw, k.value(1))))
                    ins = pe.matmul(bank[:, 2, 0:COLS], hot_p[q][:, 1 + i, :], hot_c[q][:, :],
                                    start=first and i == 0, stop=last and i == 2)
                ins.then_inc(s_hotmm, 1)

            run_steps(pe, EC, 0, 4, 4, hot)
            pe.wait_ge(s_turned, 1)
            for i in range(3):
                for k in range(KC):
                    ins = pe.matmul(bank[0:3, 4 + i // 2, (i % 2) * D:(i % 2 + 1) * D],
                                    b_col[:, k:k + 1].broadcast_to([P, 3]), wq_t[:, i, k, :],
                                    start=(k == 0), stop=(k == KC - 1))
            ins.then_inc(s_pre_pe, 1)
            for m in range(KC):
                for k in range(KC):
                    pe.matmul(bank[:, 6, m * D:(m + 1) * D], w_t[:, k, m * P:(m + 1) * P], w1_raw[:, k, :],
                              start=(k == 0), stop=(k == KC - 1))
            for m in range(KC):
                for k in range(KC):
                    ins = pe.matmul(bank[:, 7, m:m + 1], w1_raw[:, k, m * P:(m + 1) * P], b0_col[:, k:k + 1],
                                    start=(k == 0), stop=(k == KC - 1))
            ins.then_inc(s_pre_pe, 1)
            pe.wait_ge(s_ready, 1)

            def messages(s):
                k = s.back(5)
                if k.within(EC):
                    pe.wait_ge(m_z, k.value(1))
                    pe.wait_ge(m_attr[k.slot(4)], k.turns(4))
                    if k.past(1):
                        pe.wait_ge(m_zT, k.value(0))
                        pe.wait_ge(m_aT, k.value(0))
                    for i in range(2):
                        for c in range(KC):
                            pe.transpose(bank[:, 0, (i * KC + c) * P:(i * KC + c + 1) * P],
                                         Z2[k.slot(2)][:, i, c * P:(c + 1) * P], identity[:, :])
                    pe.transpose(bank[0:R, 7, 0:P], attr[k.slot(4)][:, :], identity[:, :]).then_inc(m_T, 1)
                k = s.back(6)
                if k.within(EC):
                    q = k.slot(2)
                    if not k.past(1):
                        pe.wait_ge(s_ready, 2)
                    pe.wait_ge(m_aT, k.value(1))
                    if k.past(1):
                        pe.wait_ge(m_ds, k.value(0))
                    pe.matmul(bank[:, 1, :], aT[q][:, :], wd_t[:, :], start=True, stop=True).then_inc(m_D, 1)
                    pe.wait_ge(m_zT, k.value(1))
                    if k.past(2):
                        pe.wait_ge(m_msg, k.value(-1))
                    pe.matmul(bank[:, 2 + q, :], ones3[:, :], bias3[:, D:3 * D], start=True, stop=False)
                    for c in range(KC):
                        pe.matmul(bank[:, 2 + q, :], zT[q][:, KC + c, :], qkv_w[:, c, D:3 * D], start=False,
                                  stop=(c == KC - 1))
                    if k.past(1):
                        pe.wait_ge(m_at, k.value(0))
                    pe.matmul(bank[:, 4, 0:D], ones3[:, :], bias3[:, 0:D], start=True, stop=False)
                    for c in range(KC):
                        ins = pe.matmul(bank[:, 4, 0:D], zT[q][:, c, :], qkv_w[:, c, 0:D], start=False,
                                        stop=(c == KC - 1))
                    ins.then_inc(m_qkv, 1)
                k = s.back(8)
                if k.within(EC):
                    pe.wait_ge(m_msg, k.value(1))
                    pe.wait_ge(m_eq, k.value(1))
                    if k.past(1):
                        pe.wait_ge(m_ST, k.value(0))
                    for c in range(KC):
                        ins = pe.matmul(bank[:, 5, c * P:(c + 1) * P], MSG[k.slot(2)][:, c * P:(c + 1) * P],
                                        EQ[k.slot(2)][:, :], start=True, stop=True)
                    ins.then_inc(m_S, 1)
                k = s.back(9)
                if k.within(EC):
                    pe.wait_ge(m_ST, k.value(1))
                    if k.past(1):
                        pe.wait_ge(m_UB, k.value(0))
                    for c in range(KC):
                        ins = pe.matmul(bank[:, 6, 0:D], ST[k.slot(2)][:, c, :], wo_t[:, c, :], start=(c == 0),
                                        stop=(c == KC - 1))
                    ins.then_inc(m_U, 1)

            run_steps(pe, EC, MESSAGE_STEPS, 4, 4, messages)

            def messages2(s):
                k = s.back(3)
                q = k.slot(2)
                if k.within(EP):
                    pe.wait_ge(n_en, k.value(1))
                    pe.wait_ge(n_h, k.value(1))
                    if k.past(2):
                        pe.wait_ge(n_UB, k.value(-1))
                    for to in range(2):
                        for i in range(2):
                            ins = pe.matmul(bank[:, q, to * D:(to + 1) * D], EN[q][:, i, to * P:(to + 1) * P],
                                            H1e[q][:, i, :], start=(i == 0), stop=(i == 1))
                    ins.then_inc(n_U, 1)

            run_steps(pe, EP, 1, 4, PAIR_STEPS + 3, messages2)

            def nodes(s):
                k = s.back(6)
                if k.within(NG):
                    pe.wait_ge(g_ag, k.value(1))
                    if k.past(1):
                        pe.wait_ge(g_hT, k.value(0))
                    for c in range(KC):
                        for j in range(G):
                            ins = pe.transpose(bank[:, c, j * P:(j + 1) * P],
                                               AG[k.slot(2)][:, j * D + c * P:j * D + (c + 1) * P], identity[:, :])
                    ins.then_inc(g_T, 1)
                k = s.back(7)
                if k.within(NG):
                    pe.wait_ge(g_hT, k.value(1))
                    if k.past(1):
                        pe.wait_ge(g_rT, k.value(0))
                    for m in range(KC):
                        for c in range(KC):
                            ins = pe.matmul(bank[:, 2 + m, :], w01[:, c, m * P:(m + 1) * P],
                                            hT[k.slot(2)][:, c * GN:(c + 1) * GN], start=(c == 0),
                                            stop=(c == KC - 1))
                    ins.then_inc(g_m1, 1)
                k = s.back(8)
                if k.within(NG):
                    pe.wait_ge(g_rT, k.value(1))
                    if k.past(2):
                        pe.wait_ge(g_fin, k.value(-1))
                    for j in range(G):
                        to = bank[:, 4 + 2 * k.slot(2) + j // 2, (j % 2) * D:(j % 2 + 1) * D]
                        pe.matmul(to, ones3[:, :], bias3[:, 3 * D:], start=True, stop=False)
                        for c in range(KC):
                            ins = pe.matmul(to, rT[k.slot(2)][:, c * GN + j * P:c * GN + (j + 1) * P], w2_sb[:, c, :],
                                            start=False, stop=(c == KC - 1))
                    ins.then_inc(g_m2, 1)

            last_pairs(messages2, nodes)
            run_steps(pe, NG, NODE_STEPS, 8, 4, nodes, start=AHEAD)


_INS = ['x', 'src', 'dst', 'edge_attr_64', 'edge_weight', 'L0_gnn_ln_g', 'L0_gnn_ln_b', 'L0_gnn_Wq', 'L0_gnn_bq',
        'L0_gnn_Wk', 'L0_gnn_bk', 'L0_gnn_Wv', 'L0_gnn_bv', 'L0_gnn_Wo', 'L0_gnn_bo', 'L0_gnn_Wdk', 'L0_gnn_bdk',
        'L0_gnn_Wdv', 'L0_gnn_bdv', 'L1_gnn_W', 'L1_gnn_b', 'L1_gnn_W1', 'L1_gnn_b1', 'L1_gnn_W2', 'L1_gnn_b2']


def kernel(**inputs):
    import numpy as np
    import concourse.bacc as bacc
    from concourse.bass_utils import run_bass_kernel_spmd

    nc = bacc.Bacc("TRN2", target_bir_lowering=False, num_devices=1)
    arrays, args = {}, []
    for name in _INS:
        a = np.ascontiguousarray(inputs[name])
        arrays[f"in_{name}_dram"] = a
        args.append(nc.dram_tensor(f"in_{name}_dram", a.shape, mybir.dt.from_np(a.dtype), kind="ExternalInput").ap())
    args.append(nc.dram_tensor("out_0_dram", (N, D), F32, kind="ExternalOutput").ap())
    build(nc, *args)
    r = run_bass_kernel_spmd(nc, [arrays], core_ids=[0])
    return r.results[0]["out_0_dram"]
```
